# Optimizing a Trainium2 kernel written in Bass

```python
import numpy as np
import jax
import jax.numpy as jnp

def _softmax(x, axis=-1):
    return jax.nn.softmax(x, axis=axis)

def _gelu(x):
    return jax.nn.gelu(x, approximate=True)

def _silu(x):
    return jax.nn.silu(x)

def _sigmoid(x):
    return jax.nn.sigmoid(x)

def _layernorm(x, axis=-1, eps=1e-05):
    m = jnp.mean(x, axis=axis, keepdims=True)
    v = jnp.var(x, axis=axis, keepdims=True)
    return (x - m) / jnp.sqrt(v + eps)

def _scatter_add(tgt, idx, src, axis=0):
    return tgt.at[idx].add(src)

def _segment_sum(src, seg, n):
    return jax.ops.segment_sum(src, seg, n)
kernel_name = 'mk_vit_tower_d4_tok_img256_r4_af22b4'

def setup_inputs(seed: int=0):
    np.random.seed(seed)
    _w = jnp.asarray

    def _rec_inputs():
        import jax
        import jax.numpy as jnp
        _rk = jax.random.key(seed)
        x = -7.10856e-05 + 0.999911 * jax.random.normal(jax.random.fold_in(_rk, 1), (64, 1, 224, 224), jnp.float32)
        return x
    x = _rec_inputs()

    def _L0_tok_setup():
        import jax, jax.numpy as jnp
        import numpy as np
        INV_SQRT2 = 0.7071067811865476

        def haar_dwt2(x):
            lo = (x[..., ::2] + x[..., 1::2]) * INV_SQRT2
            hi = (x[..., ::2] - x[..., 1::2]) * INV_SQRT2
            cA = (lo[..., ::2, :] + lo[..., 1::2, :]) * INV_SQRT2
            cH = (lo[..., ::2, :] - lo[..., 1::2, :]) * INV_SQRT2
            cV = (hi[..., ::2, :] + hi[..., 1::2, :]) * INV_SQRT2
            cD = (hi[..., ::2, :] - hi[..., 1::2, :]) * INV_SQRT2
            return (cA, (cH, cV, cD))

        def wavedec2_maps(x, levels):
            a = x
            details = []
            for _ in range(levels):
                a, d = haar_dwt2(a)
                details.append(d)
            maps = [a]
            for d in reversed(details):
                maps.extend(d)
            return maps
        key = jax.random.key(seed)
        k1, k2 = jax.random.split(key)
        B, H, W_img = (64, 256, 256)
        x = jax.random.normal(k1, (B, 1, H, W_img), dtype=jnp.float32)
        n_maps = 1 + 3 * 2
        W = jax.random.normal(k2, (n_maps, 64), dtype=jnp.float32) * (1.0 / np.sqrt(n_maps))
        b = jnp.zeros((64,), dtype=jnp.float32)
        return {'x': x, 'W': W, 'b': b}
    _L0_tok_all = _L0_tok_setup()
    _L0_tok_in = {k: v for k, v in _L0_tok_all.items() if k in ('W', 'b')}
    del _L0_tok_all

    def _L0_attn_setup():
        import jax, jax.numpy as jnp
        import numpy as np
        L, B, E = (128, 4, 64)
        SCALE = 0.05
        key = jax.random.key(seed)
        ks = jax.random.split(key, 6)
        return {'emb': jax.random.normal(ks[0], (L, B, E), dtype=jnp.float32), 'w1': jax.random.normal(ks[1], (E, E), dtype=jnp.float32) * SCALE, 'w2': jax.random.normal(ks[2], (E, E), dtype=jnp.float32) * SCALE, 'w3': jax.random.normal(ks[3], (E, E), dtype=jnp.float32) * SCALE, 'b3': jax.random.normal(ks[4], (E,), dtype=jnp.float32) * SCALE, 'w0': jax.random.normal(ks[5], (E,), dtype=jnp.float32) * SCALE}
    _L0_attn_all = _L0_attn_setup()
    _L0_attn_in = {k: v for k, v in _L0_attn_all.items() if k in ('w1', 'w2', 'w3', 'b3', 'w0')}
    del _L0_attn_all

    def _L0_ffn_setup():
        import math
        import jax, jax.numpy as jnp
        import numpy as np
        CAPACITY_FACTOR = 1.25
        TOP_K = 2
        LN_EPS = 1e-05

        def _layer_norm(x, gamma, beta):
            mu = jnp.mean(x, axis=-1, keepdims=True)
            var = jnp.var(x, axis=-1, keepdims=True)
            return (x - mu) * jax.lax.rsqrt(var + LN_EPS) * gamma + beta
        key = jax.random.key(seed)
        ks = jax.random.split(key, 4)
        B, S, D, F, E = (8, 1024, 64, 128, 8)
        x = jax.random.normal(ks[0], (B, S, D), dtype=jnp.float32)
        Wr = jax.random.normal(ks[1], (D, E), dtype=jnp.float32) / np.sqrt(D)
        br = jnp.zeros((E,), jnp.float32)
        W1 = jax.random.normal(ks[2], (E, D, F), dtype=jnp.float32) / np.sqrt(D)
        b1 = jnp.zeros((E, F), jnp.float32)
        W2 = jax.random.normal(ks[3], (E, F, D), dtype=jnp.float32) / np.sqrt(F)
        b2 = jnp.zeros((E, D), jnp.float32)
        gamma = jnp.ones((D,), jnp.float32)
        beta = jnp.zeros((D,), jnp.float32)
        return {'x': x, 'Wr': Wr, 'br': br, 'W1': W1, 'b1': b1, 'W2': W2, 'b2': b2, 'gamma': gamma, 'beta': beta}
    _L0_ffn_all = _L0_ffn_setup()
    _L0_ffn_in = {k: v for k, v in _L0_ffn_all.items() if k in ('Wr', 'br', 'W1', 'b1', 'W2', 'b2', 'gamma', 'beta')}
    del _L0_ffn_all

    def _L1_attn_setup():
        import jax, jax.numpy as jnp
        import numpy as np
        B, S, D = (4, 1024, 64)
        key = jax.random.key(seed)
        k1, k2, k3, k4 = jax.random.split(key, 4)
        inputs = jax.random.normal(k1, (B, S, D), dtype=jnp.float32)
        Wq = jax.random.normal(k2, (D, D), dtype=jnp.float32) * 0.05
        Wk = jax.random.normal(k3, (D, D), dtype=jnp.float32) * 0.05
        Wv = jax.random.normal(k4, (D, D), dtype=jnp.float32) * 0.05
        return {'inputs': inputs, 'Wq': Wq, 'Wk': Wk, 'Wv': Wv}
    _L1_attn_all = _L1_attn_setup()
    _L1_attn_in = {k: v for k, v in _L1_attn_all.items() if k in ('Wq', 'Wk', 'Wv')}
    del _L1_attn_all

    def _L1_ffn_setup():
        import jax, jax.numpy as jnp
        import numpy as np
        NUM_EXPERTS = 8
        TOP_K = 2
        B, S, D = (8, 2048, 64)

        def _moe(tokens, router_w, w1, b1, w2, b2):
            N = tokens.shape[0]
            E = router_w.shape[0]
            logits = tokens.astype(jnp.float32) @ router_w.astype(jnp.float32).T
            probs = jax.nn.softmax(logits, axis=-1)
            rw, re = jax.lax.top_k(probs, TOP_K)
            if TOP_K > 1:
                rw = rw / jnp.maximum(rw.sum(-1, keepdims=True), 1e-12)
            rw = rw.astype(tokens.dtype)
            combine = jnp.zeros((N, E), tokens.dtype).at[jnp.arange(N)[:, None], re].set(rw)
            out = tokens
            for e in range(E):
                h = jax.nn.gelu(tokens @ w1[e] + b1[e], approximate=False)
                y = h @ w2[e] + b2[e]
                out = out + combine[:, e:e + 1] * y
            return out
        key = jax.random.key(seed)
        ks = jax.random.split(key, 4)
        scale = 1.0 / np.sqrt(D).astype(np.float32)
        return {'input_embeddings': jax.random.normal(ks[0], (B, S, D), jnp.float32), 'router_w': jax.random.normal(ks[1], (NUM_EXPERTS, D), jnp.float32) * scale, 'w1': jax.random.normal(ks[2], (NUM_EXPERTS, D, D), jnp.float32) * scale, 'b1': jnp.zeros((NUM_EXPERTS, D), jnp.float32), 'w2': jax.random.normal(ks[3], (NUM_EXPERTS, D, D), jnp.float32) * scale, 'b2': jnp.zeros((NUM_EXPERTS, D), jnp.float32)}
    _L1_ffn_all = _L1_ffn_setup()
    _L1_ffn_in = {k: v for k, v in _L1_ffn_all.items() if k in ('router_w', 'w1', 'b1', 'w2', 'b2')}
    del _L1_ffn_all

    def _L2_attn_setup():
        import jax, jax.numpy as jnp
        import numpy as np
        B, T, C = (16, 512, 64)
        TT = T
        LAYER_ID, N_LAYER = (3, 6)
        key = jax.random.key(seed)
        ks = jax.random.split(key, 6)
        ratio_0_to_1 = LAYER_ID / (N_LAYER - 1)
        ratio_1_to_almost0 = 1.0 - LAYER_ID / N_LAYER
        h = np.arange(TT, dtype=np.float32)
        decay_speed = -5.0 + 8.0 * (h / (TT - 1)) ** (0.7 + 1.3 * ratio_0_to_1)
        curve = -(TT - 1 - h)
        time_w = jnp.asarray(np.exp(np.clip(curve * decay_speed, -30.0, 0.0)), dtype=jnp.float32)
        i = np.arange(C, dtype=np.float32) / C
        time_mix_k = jnp.asarray((i ** ratio_1_to_almost0).reshape(1, 1, C), dtype=jnp.float32)
        time_mix_v = jnp.asarray((i ** ratio_1_to_almost0 + 0.3 * ratio_0_to_1).reshape(1, 1, C), dtype=jnp.float32)
        time_mix_r = jnp.asarray((i ** (0.5 * ratio_1_to_almost0)).reshape(1, 1, C), dtype=jnp.float32)
        x = jax.random.normal(ks[0], (B, T, C), dtype=jnp.float32)
        scale = 0.02
        Wk = scale * jax.random.normal(ks[1], (C, C), dtype=jnp.float32)
        Wv = scale * jax.random.normal(ks[2], (C, C), dtype=jnp.float32)
        Wr = scale * jax.random.normal(ks[3], (C, C), dtype=jnp.float32)
        Wo = scale * jax.random.normal(ks[4], (C, C), dtype=jnp.float32)
        return {'x': x, 'time_w': time_w, 'time_mix_k': time_mix_k, 'time_mix_v': time_mix_v, 'time_mix_r': time_mix_r, 'Wk': Wk, 'Wv': Wv, 'Wr': Wr, 'Wo': Wo}
    _L2_attn_all = _L2_attn_setup()
    _L2_attn_in = {k: v for k, v in _L2_attn_all.items() if k in ('time_w', 'time_mix_k', 'time_mix_v', 'time_mix_r', 'Wk', 'Wv', 'Wr', 'Wo')}
    del _L2_attn_all

    def _L2_ffn_setup():
        import jax, jax.numpy as jnp
        import numpy as np
        TOP_K = 2
        LN_EPS = 1e-05
        key = jax.random.key(seed)
        ks = jax.random.split(key, 8)
        B, S, D, E, H = (16, 256, 64, 8, 256)
        x = jax.random.normal(ks[0], (B, S, D), dtype=jnp.float32)
        Wr = jax.random.normal(ks[1], (D, E), dtype=jnp.float32) * 0.1
        br = jnp.zeros((E,), dtype=jnp.float32)
        ln_g = jnp.ones((E, D), dtype=jnp.float32)
        ln_b = jnp.zeros((E, D), dtype=jnp.float32)
        W1 = jax.random.normal(ks[2], (E, D, H), dtype=jnp.float32) * (1.0 / np.sqrt(D))
        b1 = jnp.zeros((E, H), dtype=jnp.float32)
        W2 = jax.random.normal(ks[3], (E, H, D), dtype=jnp.float32) * (1.0 / np.sqrt(H))
        b2 = jnp.zeros((E, D), dtype=jnp.float32)
        return {'x': x, 'Wr': Wr, 'br': br, 'ln_g': ln_g, 'ln_b': ln_b, 'W1': W1, 'b1': b1, 'W2': W2, 'b2': b2}
    _L2_ffn_all = _L2_ffn_setup()
    _L2_ffn_in = {k: v for k, v in _L2_ffn_all.items() if k in ('Wr', 'br', 'ln_g', 'ln_b', 'W1', 'b1', 'W2', 'b2')}
    del _L2_ffn_all

    def _L3_attn_setup():
        import jax, jax.numpy as jnp
        import numpy as np
        key = jax.random.key(seed)
        k1, k2, k3 = jax.random.split(key, 3)
        b, n_t, n, n_h = (8, 256, 64, 8)
        s = jax.random.normal(k1, (b, n_t, n), dtype=jnp.float32)
        Q = jax.random.normal(k2, (n_h, n, n), dtype=jnp.float32) * 0.02
        E = jax.random.normal(k3, (n_h, n, n), dtype=jnp.float32) * 0.02
        return {'s': s, 'Q': Q, 'E': E}
    _L3_attn_all = _L3_attn_setup()
    _L3_attn_in = {k: v for k, v in _L3_attn_all.items() if k in ('Q', 'E')}
    del _L3_attn_all

    def _L3_ffn_setup():
        import jax, jax.numpy as jnp
        import numpy as np
        B, S, H, F, E, K = (8, 1024, 64, 128, 16, 2)
        EPS = 1e-05
        key = jax.random.key(seed)
        ks = jax.random.split(key, 9)
        sc = 0.02
        return {'x': jax.random.normal(ks[0], (B, S, H), dtype=jnp.float32), 'gate_w': jax.random.normal(ks[1], (H, E), dtype=jnp.float32) * sc, 'gate_b': jnp.zeros((E,), dtype=jnp.float32), 'w1': jax.random.normal(ks[2], (E, H, F), dtype=jnp.float32) * sc, 'b1': jnp.zeros((E, F), dtype=jnp.float32), 'w2': jax.random.normal(ks[3], (E, F, H), dtype=jnp.float32) * sc, 'b2': jnp.zeros((E, H), dtype=jnp.float32), 'gamma': jnp.ones((H,), dtype=jnp.float32), 'beta': jnp.zeros((H,), dtype=jnp.float32)}
    _L3_ffn_all = _L3_ffn_setup()
    _L3_ffn_in = {k: v for k, v in _L3_ffn_all.items() if k in ('gate_w', 'gate_b', 'w1', 'b1', 'w2', 'b2', 'gamma', 'beta')}
    del _L3_ffn_all
    return {'x': x, 'L0_tok_W': _L0_tok_in['W'], 'L0_tok_b': _L0_tok_in['b'], 'L0_attn_w1': _L0_attn_in['w1'], 'L0_attn_w2': _L0_attn_in['w2'], 'L0_attn_w3': _L0_attn_in['w3'], 'L0_attn_b3': _L0_attn_in['b3'], 'L0_attn_w0': _L0_attn_in['w0'], 'L0_ffn_Wr': _L0_ffn_in['Wr'], 'L0_ffn_br': _L0_ffn_in['br'], 'L0_ffn_W1': _L0_ffn_in['W1'], 'L0_ffn_b1': _L0_ffn_in['b1'], 'L0_ffn_W2': _L0_ffn_in['W2'], 'L0_ffn_b2': _L0_ffn_in['b2'], 'L0_ffn_gamma': _L0_ffn_in['gamma'], 'L0_ffn_beta': _L0_ffn_in['beta'], 'L1_attn_Wq': _L1_attn_in['Wq'], 'L1_attn_Wk': _L1_attn_in['Wk'], 'L1_attn_Wv': _L1_attn_in['Wv'], 'L1_ffn_router_w': _L1_ffn_in['router_w'], 'L1_ffn_w1': _L1_ffn_in['w1'], 'L1_ffn_b1': _L1_ffn_in['b1'], 'L1_ffn_w2': _L1_ffn_in['w2'], 'L1_ffn_b2': _L1_ffn_in['b2'], 'L2_attn_time_w': _L2_attn_in['time_w'], 'L2_attn_time_mix_k': _L2_attn_in['time_mix_k'], 'L2_attn_time_mix_v': _L2_attn_in['time_mix_v'], 'L2_attn_time_mix_r': _L2_attn_in['time_mix_r'], 'L2_attn_Wk': _L2_attn_in['Wk'], 'L2_attn_Wv': _L2_attn_in['Wv'], 'L2_attn_Wr': _L2_attn_in['Wr'], 'L2_attn_Wo': _L2_attn_in['Wo'], 'L2_ffn_Wr': _L2_ffn_in['Wr'], 'L2_ffn_br': _L2_ffn_in['br'], 'L2_ffn_ln_g': _L2_ffn_in['ln_g'], 'L2_ffn_ln_b': _L2_ffn_in['ln_b'], 'L2_ffn_W1': _L2_ffn_in['W1'], 'L2_ffn_b1': _L2_ffn_in['b1'], 'L2_ffn_W2': _L2_ffn_in['W2'], 'L2_ffn_b2': _L2_ffn_in['b2'], 'L3_attn_Q': _L3_attn_in['Q'], 'L3_attn_E': _L3_attn_in['E'], 'L3_ffn_gate_w': _L3_ffn_in['gate_w'], 'L3_ffn_gate_b': _L3_ffn_in['gate_b'], 'L3_ffn_w1': _L3_ffn_in['w1'], 'L3_ffn_b1': _L3_ffn_in['b1'], 'L3_ffn_w2': _L3_ffn_in['w2'], 'L3_ffn_b2': _L3_ffn_in['b2'], 'L3_ffn_gamma': _L3_ffn_in['gamma'], 'L3_ffn_beta': _L3_ffn_in['beta']}

def reference(x, L0_tok_W, L0_tok_b, L0_attn_w1, L0_attn_w2, L0_attn_w3, L0_attn_b3, L0_attn_w0, L0_ffn_Wr, L0_ffn_br, L0_ffn_W1, L0_ffn_b1, L0_ffn_W2, L0_ffn_b2, L0_ffn_gamma, L0_ffn_beta, L1_attn_Wq, L1_attn_Wk, L1_attn_Wv, L1_ffn_router_w, L1_ffn_w1, L1_ffn_b1, L1_ffn_w2, L1_ffn_b2, L2_attn_time_w, L2_attn_time_mix_k, L2_attn_time_mix_v, L2_attn_time_mix_r, L2_attn_Wk, L2_attn_Wv, L2_attn_Wr, L2_attn_Wo, L2_ffn_Wr, L2_ffn_br, L2_ffn_ln_g, L2_ffn_ln_b, L2_ffn_W1, L2_ffn_b1, L2_ffn_W2, L2_ffn_b2, L3_attn_Q, L3_attn_E, L3_ffn_gate_w, L3_ffn_gate_b, L3_ffn_w1, L3_ffn_b1, L3_ffn_w2, L3_ffn_b2, L3_ffn_gamma, L3_ffn_beta):
    import jax
    import jax.numpy as jnp

    def _L0_tok_ref(x, W, b):
        import jax, jax.numpy as jnp
        import numpy as np
        INV_SQRT2 = 0.7071067811865476

        def haar_dwt2(x):
            lo = (x[..., ::2] + x[..., 1::2]) * INV_SQRT2
            hi = (x[..., ::2] - x[..., 1::2]) * INV_SQRT2
            cA = (lo[..., ::2, :] + lo[..., 1::2, :]) * INV_SQRT2
            cH = (lo[..., ::2, :] - lo[..., 1::2, :]) * INV_SQRT2
            cV = (hi[..., ::2, :] + hi[..., 1::2, :]) * INV_SQRT2
            cD = (hi[..., ::2, :] - hi[..., 1::2, :]) * INV_SQRT2
            return (cA, (cH, cV, cD))

        def wavedec2_maps(x, levels):
            a = x
            details = []
            for _ in range(levels):
                a, d = haar_dwt2(a)
                details.append(d)
            maps = [a]
            for d in reversed(details):
                maps.extend(d)
            return maps
        imgs = x[:, 0]
        B = imgs.shape[0]
        maps = wavedec2_maps(imgs, 2)
        proc = [jax.image.resize(m, (B, 8, 8), method='bilinear') for m in maps]
        feat = jnp.stack(proc, axis=1)
        feat = feat.reshape(B, feat.shape[1], 64).transpose(0, 2, 1)
        return feat @ W + b

    def _L0_attn_ref(emb, w1, w2, w3, b3, w0):
        import jax, jax.numpy as jnp
        import numpy as np
        L, B, E = (128, 4, 64)
        SCALE = 0.05
        Lq = emb.shape[0]
        u = jnp.einsum('lbe,fe->lbf', emb, w1)
        q = jnp.einsum('lbe,fe->lbf', emb, w2)
        c = jnp.einsum('lbe,fe->lbf', jnp.cumsum(emb, axis=0), w3) + b3
        gate = jax.nn.sigmoid(u[None, :, :, :] + (q + c)[:, None, :, :])
        scores = jnp.einsum('tibe,e->tib', gate, w0)
        causal = jnp.tril(jnp.ones((Lq, Lq), dtype=emb.dtype))
        scores = scores * causal[:, :, None]
        return jnp.einsum('tib,ibe->tbe', scores, emb)

    def _L0_ffn_ref(x, Wr, br, W1, b1, W2, b2, gamma, beta):
        import math
        import jax, jax.numpy as jnp
        import numpy as np
        CAPACITY_FACTOR = 1.25
        TOP_K = 2
        LN_EPS = 1e-05

        def _layer_norm(x, gamma, beta):
            mu = jnp.mean(x, axis=-1, keepdims=True)
            var = jnp.var(x, axis=-1, keepdims=True)
            return (x - mu) * jax.lax.rsqrt(var + LN_EPS) * gamma + beta
        B, S, D = x.shape
        E = Wr.shape[1]
        N = B * S
        K = TOP_K
        logits = jnp.mean(x, axis=1) @ Wr + br
        routing_weights = jax.nn.softmax(logits, axis=-1)
        capacity = float(math.ceil(N * CAPACITY_FACTOR / E))
        expected_loads = routing_weights.sum(axis=0) * (N / B)
        scale = jnp.where(expected_loads > capacity, capacity / expected_loads, 1.0)
        routing_weights = jax.nn.softmax(routing_weights * scale, axis=-1)
        rw_tok = jnp.broadcast_to(routing_weights[:, None, :], (B, S, E)).reshape(N, E)
        top_w, top_i = jax.lax.top_k(rw_tok, K)
        top_w = jax.nn.softmax(top_w, axis=-1)
        xf = x.reshape(N, D)
        h = jax.nn.gelu(jnp.einsum('nd,edf->enf', xf, W1) + b1[:, None, :], approximate=False)
        y = jnp.einsum('enf,efd->end', h, W2) + b2[:, None, :]
        w_dense = jnp.zeros((N, E), x.dtype).at[jnp.arange(N)[:, None], top_i].add(top_w)
        out = jnp.einsum('ne,end->nd', w_dense, y).reshape(B, S, D)
        out = _layer_norm(out + x, gamma, beta)
        return out

    def _L1_attn_ref(inputs, Wq, Wk, Wv):
        import jax, jax.numpy as jnp
        import numpy as np
        B, S, D = (4, 1024, 64)
        d = inputs.shape[-1]
        Q = jnp.einsum('bsd,de->bse', inputs, Wq)
        K = jnp.einsum('bsd,de->bse', inputs, Wk)
        V = jnp.einsum('bsd,de->bse', inputs, Wv)
        scale = 1.0 / jnp.sqrt(jnp.asarray(d, dtype=inputs.dtype))
        scores = jnp.einsum('bqe,bke->bqk', Q, K) * scale
        attn = jax.nn.softmax(scores, axis=-1)
        return jnp.einsum('bqk,bke->bqe', attn, V)

    def _L1_ffn_ref(input_embeddings, router_w, w1, b1, w2, b2):
        import jax, jax.numpy as jnp
        import numpy as np
        NUM_EXPERTS = 8
        TOP_K = 2
        B, S, D = (8, 2048, 64)

        def _moe(tokens, router_w, w1, b1, w2, b2):
            N = tokens.shape[0]
            E = router_w.shape[0]
            logits = tokens.astype(jnp.float32) @ router_w.astype(jnp.float32).T
            probs = jax.nn.softmax(logits, axis=-1)
            rw, re = jax.lax.top_k(probs, TOP_K)
            if TOP_K > 1:
                rw = rw / jnp.maximum(rw.sum(-1, keepdims=True), 1e-12)
            rw = rw.astype(tokens.dtype)
            combine = jnp.zeros((N, E), tokens.dtype).at[jnp.arange(N)[:, None], re].set(rw)
            out = tokens
            for e in range(E):
                h = jax.nn.gelu(tokens @ w1[e] + b1[e], approximate=False)
                y = h @ w2[e] + b2[e]
                out = out + combine[:, e:e + 1] * y
            return out
        b, s, d = input_embeddings.shape
        tokens = input_embeddings.reshape(b * s, d)
        return _moe(tokens, router_w, w1, b1, w2, b2).reshape(b, s, d)

    def _L2_attn_ref(x, time_w, time_mix_k, time_mix_v, time_mix_r, Wk, Wv, Wr, Wo):
        import jax, jax.numpy as jnp
        import numpy as np
        B, T, C = (16, 512, 64)
        TT = T
        LAYER_ID, N_LAYER = (3, 6)
        Bx, Tx, Cx = x.shape
        maxlen = time_w.shape[0]
        xx = jnp.pad(x, ((0, 0), (1, 0), (0, 0)))[:, :-1]
        xk = x * time_mix_k + xx * (1.0 - time_mix_k)
        xv = x * time_mix_v + xx * (1.0 - time_mix_v)
        xr = x * time_mix_r + xx * (1.0 - time_mix_r)
        k = jnp.exp(jnp.clip(xk @ Wk, -60.0, 30.0))
        v = xv @ Wv
        r = xr @ Wr
        sum_k = jnp.cumsum(k, axis=1)
        kv = k * v
        t_idx = jnp.arange(Tx)
        d = t_idx[:, None] - t_idx[None, :]
        W = jnp.where(d >= 0, time_w[jnp.clip(maxlen - 1 - d, 0, maxlen - 1)], 0.0)
        wkv = jnp.einsum('tu,buc->btc', W, kv)
        rwkv = jax.nn.sigmoid(r) * wkv / sum_k
        return rwkv @ Wo

    def _L2_ffn_ref(x, Wr, br, ln_g, ln_b, W1, b1, W2, b2):
        import jax, jax.numpy as jnp
        import numpy as np
        TOP_K = 2
        LN_EPS = 1e-05
        B, S, D = x.shape
        N = B * S
        xt = x.reshape(N, D)
        logits = xt @ Wr + br
        probs = jax.nn.softmax(logits, axis=-1)
        top_p, top_idx = jax.lax.top_k(probs, TOP_K)
        weights = top_p / top_p.sum(axis=-1, keepdims=True)
        mu = xt.mean(axis=-1, keepdims=True)
        var = ((xt - mu) ** 2).mean(axis=-1, keepdims=True)
        xn = (xt - mu) * jax.lax.rsqrt(var + LN_EPS)
        xe = xn[None, :, :] * ln_g[:, None, :] + ln_b[:, None, :]
        h = jax.nn.gelu(jnp.einsum('end,edh->enh', xe, W1) + b1[:, None, :], approximate=False)
        y = jnp.einsum('enh,ehd->end', h, W2) + b2[:, None, :]
        y_tok = jnp.transpose(y, (1, 0, 2))
        sel = jnp.take_along_axis(y_tok, top_idx[:, :, None], axis=1)
        out = (weights[:, :, None] * sel).sum(axis=1)
        return out.reshape(B, S, D)

    def _L3_attn_ref(s, Q, E):
        import jax, jax.numpy as jnp
        import numpy as np
        n_t = s.shape[1]
        qs = jnp.einsum('bti,hij->bhtj', s, Q)
        Omega = jnp.einsum('bhtj,buj->bhtu', qs, s)
        mask = jnp.tril(jnp.ones((n_t, n_t), dtype=s.dtype))
        Omega = Omega * mask
        es = jnp.einsum('hij,buj->bhui', E, s)
        r = jnp.einsum('bhtu,bhui->bti', Omega, es)
        return r

    def _L3_ffn_ref(x, gate_w, gate_b, w1, b1, w2, b2, gamma, beta):
        import jax, jax.numpy as jnp
        import numpy as np
        B, S, H, F, E, K = (8, 1024, 64, 128, 16, 2)
        EPS = 1e-05
        gate_logits = x @ gate_w + gate_b
        topk_vals, topk_idx = jax.lax.top_k(gate_logits, K)
        topk_w = jax.nn.softmax(topk_vals, axis=-1)
        h = jax.nn.relu(jnp.einsum('bsh,ehf->bsef', x, w1) + b1)
        expert_out = jnp.einsum('bsef,efh->bseh', h, w2) + b2
        sel = jnp.take_along_axis(expert_out, topk_idx[:, :, :, None], axis=2)
        moe = jnp.sum(topk_w[..., None] * sel, axis=2)
        y = x + moe
        mu = jnp.mean(y, axis=-1, keepdims=True)
        var = jnp.var(y, axis=-1, keepdims=True)
        return (y - mu) / jnp.sqrt(var + EPS) * gamma + beta
    h = _L0_tok_ref(x, L0_tok_W, L0_tok_b)
    h = h + _L0_attn_ref(_layernorm(h, axis=-1), L0_attn_w1, L0_attn_w2, L0_attn_w3, L0_attn_b3, L0_attn_w0)
    h = h + _L0_ffn_ref(_layernorm(h, axis=-1), L0_ffn_Wr, L0_ffn_br, L0_ffn_W1, L0_ffn_b1, L0_ffn_W2, L0_ffn_b2, L0_ffn_gamma, L0_ffn_beta)
    h = h + _L1_attn_ref(_layernorm(h, axis=-1), L1_attn_Wq, L1_attn_Wk, L1_attn_Wv)
    h = h + _L1_ffn_ref(_layernorm(h, axis=-1), L1_ffn_router_w, L1_ffn_w1, L1_ffn_b1, L1_ffn_w2, L1_ffn_b2)
    h = h + _L2_attn_ref(_layernorm(h, axis=-1), L2_attn_time_w, L2_attn_time_mix_k, L2_attn_time_mix_v, L2_attn_time_mix_r, L2_attn_Wk, L2_attn_Wv, L2_attn_Wr, L2_attn_Wo)
    h = h + _L2_ffn_ref(_layernorm(h, axis=-1), L2_ffn_Wr, L2_ffn_br, L2_ffn_ln_g, L2_ffn_ln_b, L2_ffn_W1, L2_ffn_b1, L2_ffn_W2, L2_ffn_b2)
    h = h + _L3_attn_ref(_layernorm(h, axis=-1), L3_attn_Q, L3_attn_E)
    h = h + _L3_ffn_ref(_layernorm(h, axis=-1), L3_ffn_gate_w, L3_ffn_gate_b, L3_ffn_w1, L3_ffn_b1, L3_ffn_w2, L3_ffn_b2, L3_ffn_gamma, L3_ffn_beta)
    return h

_drawn_inputs = setup_inputs


def setup_inputs(seed=0):
    import zlib

    import numpy as np

    out = dict(_drawn_inputs(seed))
    spreads = {'L0_tok_b': (0.0, 0.1),
     'L0_ffn_br': (0.0, 0.1),
     'L0_ffn_b1': (0.0, 0.404),
     'L0_ffn_b2': (0.0, 0.42),
     'L0_ffn_gamma': (1.0, 0.2),
     'L0_ffn_beta': (0.0, 0.298),
     'L1_ffn_b1': (0.0, 0.709),
     'L1_ffn_b2': (0.0, 0.557),
     'L2_ffn_br': (0.0, 0.364),
     'L2_ffn_ln_g': (1.0, 0.6),
     'L2_ffn_ln_b': (0.0, 0.8),
     'L2_ffn_b1': (0.0, 0.79),
     'L2_ffn_b2': (0.0, 0.676),
     'L3_ffn_gate_b': (0.0, 0.8),
     'L3_ffn_b1': (0.0, 2.0),
     'L3_ffn_b2': (0.0, 2.0),
     'L3_ffn_gamma': (1.0, 0.6),
     'L3_ffn_beta': (0.0, 0.8)}
    factors = {'L0_attn_w1': 2.839,
     'L0_attn_w2': 5.5,
     'L0_attn_b3': 8.0,
     'L1_attn_Wq': 8.0,
     'L1_attn_Wk': 8.0,
     'L2_attn_time_w': 8.0,
     'L2_attn_time_mix_k': 8.0,
     'L2_attn_time_mix_v': 8.0,
     'L2_attn_time_mix_r': 8.0,
     'L2_attn_Wk': 8.0,
     'L2_attn_Wv': 8.0,
     'L2_attn_Wr': 8.0,
     'L2_attn_Wo': 8.0,
     'L3_ffn_gate_w': 8.0,
     'L3_ffn_w1': 8.0,
     'L3_ffn_w2': 8.0}
    for name, (base, spread) in spreads.items():
        noise = np.random.default_rng([zlib.crc32(name.encode()), seed]).standard_normal(out[name].shape)
        drawn = base * np.exp(spread * noise) if base else spread * noise
        out[name] = jnp.asarray(drawn.astype(out[name].dtype))
    for name, factor in factors.items():
        out[name] = (out[name] * factor).astype(out[name].dtype)
    return out
```

```python
import numpy as np
import concourse.bass as bass
from concourse import mybir
from contextlib import ExitStack

F32 = mybir.dt.float32
F32R = mybir.dt.float32r
BF16 = mybir.dt.bfloat16
ALU = mybir.AluOpType
ACT = mybir.ActivationFunctionType
AX = mybir.AxisListType

P = 128
NI = 64
NT = 64
D = 64
NJ = NI * NT // P
NQ = 4
QJ = NJ // NQ
NG = 8
EPS = 1e-5
BIG_NEG = -3.0e38


def build(nc, a, out):
    ctx = ExitStack()
    with ctx:
        def sb(name, shape, dt=F32):
            return ctx.enter_context(nc.sbuf_tensor(name, shape, dt))

        def sem(name):
            return ctx.enter_context(nc.semaphore(name))

        H = sb("H", [P, NJ, D])
        XA = sb("XA", [P, NJ, D])
        LNB = sb("LNB", [P, 2 * NJ, D])
        XC = LNB[:, 0:NJ, :]
        SQ = LNB[:, NJ:2 * NJ, :]
        XT = sb("XT", [P, NI * NT])
        XTR = sb("XTR", [P, NI * NT], F32R)
        BIG = sb("BIG", [P, 16384])
        LNS = sb("LNS", [P, 4, NJ])
        HALFPOW = sb("HALFPOW", [P, QJ])
        RT = BIG[:, 12288:16384].rearrange("p (i j e) -> p i j e", i=8, j=NJ)
        RV = sb("RV", [P, 12, NJ])
        PS = ctx.enter_context(nc.psum_tensor("PS", [P, 8, 512], F32))

        w = {}
        early = ["rowmap", "colmap", "tokW", "tokb", "I", "IU", "bd", "b3", "w0"]
        for name, ap in list(a.items()):
            if name in ("x",) or name.startswith("w1_"):
                continue
            if name == "tokW":
                continue
            if name == "Ib" or name.startswith("sel_"):
                ap = a[name] = ap.bitcast(BF16)
            w[name] = sb("p_" + name, list(ap.shape), ap.dtype)
        WORK = sb("WORK", [P, 2048])
        w["tokW"] = WORK[0:32, :].rearrange("p (o n) -> p o n", o=4)
        W1S = sb("W1S", [P, 2048])
        WH = sb("WH", [P, 2048], F32R)
        WL = sb("WL", [P, 2048], F32R)
        scratch = nc.dram_tensor("h_scratch", (NI, NT, D), F32, kind="Internal").ap()

        s_early, s_late = sem("early_params_loaded"), sem("late_params_loaded")
        n_early, n_late = len(early), len(w) - len(early)
        s_w1 = [sem(f"w1_loaded_{i}") for i in range(4)]
        s_w1free = [sem(f"w1_staging_free_{i}") for i in range(4)]
        s_out = sem("output_stored")

        class Chain:
            def __init__(self, name):
                self.s, self.n = sem(name), 0

            def link(self, eng, ins):
                self.n += 1
                ins.then_inc(self.s, 1)
                eng.wait_ge(self.s, self.n)

        dve_chain, act_chain, pool_chain = Chain("dve_step"), Chain("act_step"), Chain("pool_step")

        LN_SRC = {}
        lns = {x: sem(f"ln_{x}") for x in ("centred", "squared", "var", "rstd", "out")}

        def ln_wait(eng, n, what, quarters):
            eng.wait_ge(lns[what], NQ * n + quarters)

        def q3(t, q):
            return t[:, q * QJ:(q + 1) * QJ, :]

        def bc_j(t, q):
            return t[:, q * QJ:(q + 1) * QJ].unsqueeze(2).broadcast_to([P, QJ, D])

        def ln_dve(v, n, src, dst, ready=lambda q: None, tail=None):
            for q in range(NQ):
                ready(q)
                ins = nc.vector.tensor_reduce(LNS[:, 0, q * QJ:(q + 1) * QJ], q3(src, q), AX.X, ALU.add)
                if q < NQ - 1:
                    ins.then_inc(dve_chain.s, 1)
                    dve_chain.n += 1
                else:
                    dve_chain.link(v, ins)
            dve_chain.link(v, nc.vector.tensor_scalar(LNS[:, 1, :], LNS[:, 0, :], 1.0 / D, None, ALU.mult))
            for q in range(NQ):
                nc.vector.tensor_tensor(q3(XC, q), q3(src, q), bc_j(LNS[:, 1, :], q), ALU.subtract).then_inc(lns["centred"], 1)
            for q in range(NQ):
                ln_wait(v, n, "squared", q + 1)
                nc.vector.tensor_reduce(LNS[:, 2, q * QJ:(q + 1) * QJ], q3(SQ, q), AX.X, ALU.add).then_inc(lns["var"], 1)
            for q in range(NQ):
                ln_wait(v, n, "rstd", q + 1)
                ln_wait(v, n, "centred", q + 1)
                ins = nc.vector.tensor_tensor(q3(dst, q), q3(XC, q), bc_j(LNS[:, 3, :], q), ALU.mult)
                ins.then_inc(lns["out"], 1)

        def ln_act(s, n):
            for q in range(NQ):
                ln_wait(s, n, "centred", q + 1)
                nc.scalar.activation(q3(SQ, q), q3(XC, q), ACT.Square).then_inc(lns["squared"], 1)

        def ln_pool(p, n):
            for q in range(NQ):
                ln_wait(p, n, "var", q + 1)
                r = LNS[:, 3, q * QJ:(q + 1) * QJ]
                pool_chain.link(p, nc.gpsimd.tensor_scalar(r, LNS[:, 2, q * QJ:(q + 1) * QJ], 1.0 / D, EPS, ALU.mult, ALU.add))
                nc.gpsimd.tensor_tensor(r, r, HALFPOW[:, 0:QJ], ALU.pow).then_inc(lns["rstd"], 1)

        UI = 8
        UN = NI // UI
        IMG = BIG[:, 0:4 * UI * 448].rearrange("p (u i c w) -> p u i c w", u=4, i=UI, c=2)
        YS = XT[:, 0:896].rearrange("p (u i w) -> p u i w", u=2, i=2)
        YTS = XT[0:112, 1024:2048].rearrange("p (u i c m) -> p u i c m", u=2, i=2, c=2)
        ZS = XT[0:32, 2048:4096].rearrange("p (b m) -> p b m", b=NI)
        s_img = [sem(f"images_loaded_{i}") for i in range(4)]
        s_rows, s_ys = sem("rows_reduced"), sem("rows_copied")
        s_yt, s_yts = sem("rows_transposed"), sem("transposed_copied")
        s_z, s_zs = sem("maps_done"), sem("maps_copied")
        s_feat, s_h0 = sem("tokens_done"), sem("tokens_in_h")

        def tok_sp(sp):
            x = a["x"].rearrange("b o (p c) w -> p b (o c) w", c=2)
            for u in range(UN):
                if u >= 4:
                    sp.wait_ge(s_rows, u - 3)
                sp.dma_start(IMG[0:112, u % 4], x[:, u * UI:(u + 1) * UI]).then_inc(s_img[u % 4], 16)

        def tok_pe(pe):
            pe.wait_ge(s_early, 16 * n_early)
            for step in range(UN + 2):
                u = step
                if u < UN:
                    pe.wait_ge(s_img[u % 4], 16 * (u // 4 + 1))
                    if u >= 2:
                        pe.wait_ge(s_ys, u - 1)
                    for c in range(2):
                        for g in range(4):
                            ins = nc.tensor.matmul(PS[32 * g:32 * g + 32, u % 2, 0:448], w["rowmap"][:, c, :],
                                                   IMG[0:112, u % 4, 2 * g:2 * g + 2, c, :], start=c == 0, stop=c == 1)
                    ins.then_inc(s_rows, 1)
                u = step - 1
                if 0 <= u < UN:
                    pe.wait_ge(s_ys, u + 1)
                    if u >= 2:
                        pe.wait_ge(s_yts, u - 1)
                    for i in range(2):
                        for c in range(2):
                            o = (2 * i + c) * 128
                            ins = nc.tensor.transpose(PS[0:112, 2 + u % 2, o:o + 128],
                                                      YS[:, u % 2, i, c * 112:c * 112 + 112], w["I"][:, :])
                    ins.then_inc(s_yt, 1)
                u = step - 2
                if 0 <= u < UN:
                    pe.wait_ge(s_yts, u + 1)
                    if u >= 2:
                        pe.wait_ge(s_zs, u - 1)
                    for c in range(2):
                        ins = nc.tensor.matmul(PS[0:32, 4 + u % 2, 0:256], w["colmap"][:, c, :], YTS[:, u % 2, :, c, :],
                                               start=c == 0, stop=c == 1)
                    ins.then_inc(s_z, 1)
            pe.wait_ge(s_zs, UN)
            for r in range(4):
                for o in range(4):
                    for h in range(2):
                        ins = nc.tensor.matmul(PS[64 * h:64 * h + 64, r, :], ZS[:, :, 8 * o + 4 * h + r],
                                               w["tokW"][:, o, :], start=o == 0, stop=o == 3)
                ins.then_inc(s_feat, 1)

        def tok_act(s):
            for u in range(UN):
                s.wait_ge(s_rows, u + 1)
                if u >= 2:
                    s.wait_ge(s_yt, u - 1)
                nc.scalar.copy(YS[:, u % 2], PS[:, u % 2, 0:448].rearrange("p (i w) -> p i w", i=2)).then_inc(s_ys, 1)

        def tok_dve(v):
            def maps(u):
                v.wait_ge(s_z, u + 1)
                src = PS[0:32, 4 + u % 2, 0:256].rearrange("p (i g m) -> p i g m", i=2, g=4)
                dst = ZS[:, u * UI:(u + 1) * UI, :].rearrange("p (g i) m -> p i g m", i=2)
                nc.vector.tensor_copy(dst, src).then_inc(s_zs, 1)

            for u in range(UN):
                v.wait_ge(s_yt, u + 1)
                if u >= 2:
                    v.wait_ge(s_z, u - 1)
                nc.vector.tensor_copy(YTS[:, u % 2], PS[0:112, 2 + u % 2, :].rearrange("p (i c m) -> p i c m", i=2, c=2)
                                      ).then_inc(s_yts, 1)
                if u >= 1:
                    maps(u - 1)
            maps(UN - 1)
            v.wait_ge(s_early, 16 * n_early)
            for r in range(4):
                v.wait_ge(s_feat, r + 1)
                nc.vector.tensor_tensor(q3(H, r), PS[:, r, :].rearrange("p (s e) -> p s e", s=8),
                                        w["tokb"][:, :].unsqueeze(1).broadcast_to([P, 8, D]), ALU.add).then_inc(s_h0, 1)

        NP = NJ
        XCT = BIG[:, 12288:16384].rearrange("p (k m) -> p k m", k=NP)
        U = XT[:, 0:2048].rearrange("p (k i) -> p k i", k=NP)
        QC = XT[:, 2048:4096].rearrange("p (k i) -> p k i", k=NP)
        GATE = BIG[:, :].rearrange("p (u t i) -> p u t i", u=4, t=NI)
        MASK = SQ
        SS = XC
        ST = BIG[:, 0:2048].rearrange("p (k t) -> p k t", k=NP)
        W0S = sb("W0S", [P, 2, 32])
        s_tc, s_tcc = sem("cumulated"), sem("cumulated_copied")
        s_uq, s_uqc = sem("projected"), sem("projected_copied")
        s_preA, s_preB = sem("preact_first"), sem("preact_second")
        s_gate, s_w0 = sem("gates_done"), sem("score_weights_staged")
        s_score = sem("pair_scored")
        s_mask, s_ss = sem("mask_ready"), sem("scores_masked")
        s_st, s_stc = sem("scores_transposed"), sem("scores_t_copied")
        s_att, s_h1 = sem("attended"), sem("attended_in_h")
        s_h1st, s_h1ld = sem("h_stored"), sem("h_loaded")

        def a0_pe(pe):
            for k in range(NP):
                hh, q = k // 16, k // 4
                ln_wait(pe, 0, "out", NQ)
                if k % 4 == 0 and q >= 4:
                    pe.wait_ge(s_tcc, q - 3)
                ins = nc.tensor.matmul(PS[:, 4 + q % 4, (k % 4) * 128:(k % 4) * 128 + 128],
                                       XA[64 * hh:64 * hh + 64, 2 * (k % 16):2 * (k % 16) + 2, :],
                                       w["IU"][64 * hh:64 * hh + 64, :], start=True, stop=True)
                if k % 4 == 3:
                    ins.then_inc(s_tc, 1)
            for q in range(4):
                pe.wait_ge(s_tcc, 2 * q + 2)
                pe.wait_ge(s_h0, 4)
                xi = XCT[:, 8 * q:8 * q + 8, 0:64]
                xc = XCT[:, 8 * q:8 * q + 8, 64:128]
                if q >= 2:
                    pe.wait_ge(s_uqc, 2 * (q - 1))
                nc.tensor.matmul(PS[:, 2 * (q % 2), :], w["bd"][:, 0, :], xi, start=True, stop=True).then_inc(s_uq, 1)
                nc.tensor.matmul(PS[:, 2 * (q % 2) + 1, :], w["bd"][:, 1, :], xi, start=True, stop=False)
                nc.tensor.matmul(PS[:, 2 * (q % 2) + 1, :], w["bd"][:, 2, :], xc, start=False, stop=True).then_inc(s_uq, 1)
            pe.wait_ge(s_uqc, 8)

            def score(k, s, first, last):
                pe.wait_ge(s_gate, 2 * k + 2)
                pe.wait_ge(s_w0, k + 1)
                for q in range(4):
                    for hh in range(2):
                        for par in range(2):
                            g = 2 * par + hh
                            ni = 16 * (q + 1)
                            ins = nc.tensor.matmul(
                                PS[32 * g:32 * g + 32, q, :].rearrange("p (t i) -> p t i", t=8)[:, :, 0:ni],
                                W0S[:, s, :],
                                GATE[:, 2 * s + hh, 16 * q:16 * q + 16, :].rearrange("p (t r) i -> p t r i", r=2)[:, :, par, 0:ni],
                                start=first, stop=last)
                ins.then_inc(s_score, 1)

            score(0, 0, True, False)
            score(1, 1, False, False)
            with pe.Fori(1, 7) as kk:
                score(2 * kk, 0, False, False)
                score(2 * kk + 1, 1, False, False)
            score(14, 0, False, False)
            score(15, 1, False, True)
            for b in range(4):
                pe.wait_ge(s_ss, 4)
                for t8 in range(8):
                    t = 8 * b + t8
                    for h in range(2):
                        ins = nc.tensor.matmul(
                            PS[64 * h:64 * h + 64, 4 + b, t8 * 64:t8 * 64 + 64], SS[:, t, :],
                            w["I"][:, :].rearrange("p (r h t) -> p r h t", r=2, h=2)[:, :, h, :], start=True, stop=True)
                ins.then_inc(s_st, 1)
            pe.wait_ge(s_stc, 4)
            for k in range(NP):
                for h in range(2):
                    ins = nc.tensor.matmul(PS[64 * h:64 * h + 64, (k // 8) ^ h, (k % 8) * 64:(k % 8) * 64 + 64],
                                           ST[64 * h:64 * h + 64, k, :], XA[64 * h:64 * h + 64, k, :], start=True, stop=True)
                if k % 16 == 15:
                    ins.then_inc(s_att, 1)

        def a0_act(s):
            for q in range(8):
                s.wait_ge(s_tc, q + 1)
                s.wait_ge(s_rows, UN)
                nc.scalar.copy(XCT[:, 4 * q:4 * q + 4, :], PS[:, 4 + q % 4, :].rearrange("p (k m) -> p k m", k=4)
                               ).then_inc(s_tcc, 1)
            for q in range(4):
                s.wait_ge(s_uq, 2 * q + 1)
                s.wait_ge(s_feat, 4)
                nc.scalar.copy(U[:, 8 * q:8 * q + 8, :], PS[:, 2 * (q % 2), :].rearrange("p (k m) -> p k m", k=8)
                               ).then_inc(s_uqc, 1)
                s.wait_ge(s_uq, 2 * q + 2)
                nc.scalar.activation(QC[:, 8 * q:8 * q + 8, :], PS[:, 2 * (q % 2) + 1, :].rearrange("p (k m) -> p k m", k=8),
                                     ACT.Identity, bias=w["b3"][:, 0:1]).then_inc(s_uqc, 1)

            def gates(k, s_, first):
                if not first:
                    s.wait_ge(s_score, k - 1)
                nc.scalar.copy(W0S[:, s_, :], w["w0"][:, bass.ds(k, 1), :].rearrange("p o m -> p (o m)")).then_inc(s_w0, 1)
                for hh, pre in ((0, s_preA), (1, s_preB)):
                    s.wait_ge(s_preA, 6 * k + (4 if hh == 0 else 6))
                    if hh == 1:
                        s.wait_ge(s_preB, 2 * k + 2)
                    for q in range(4):
                        ni = 16 * (q + 1)
                        g = GATE[:, 2 * s_ + hh, 16 * q:16 * q + 16, 0:ni]
                        ins = nc.scalar.activation(g, g, ACT.Sigmoid)
                    ins.then_inc(s_gate, 1)

            gates(0, 0, True)
            gates(1, 1, True)
            with s.Fori(1, 8) as kk:
                gates(2 * kk, 0, False)
                gates(2 * kk + 1, 1, False)
            for b in range(4):
                s.wait_ge(s_st, b + 1)
                src = PS[:, 4 + b, :].rearrange("p (t k) -> p k t", t=16)
                nc.scalar.copy(ST[:, :, 16 * b:16 * b + 16], src).then_inc(s_stc, 1)

        def preact(eng, k, s_, hh, q, signal):
            ni = 16 * (q + 1)
            pair = k + 16 * hh
            u = U[:, bass.ds(pair, 1), 0:ni].broadcast_to([P, 16, ni])
            c = QC[:, bass.ds(pair, 1), 16 * q:16 * q + 16].rearrange("p o t -> p (o t)").unsqueeze(2).broadcast_to([P, 16, ni])
            eng.tensor_tensor(GATE[:, 2 * s_ + hh, 16 * q:16 * q + 16, 0:ni], u, c, ALU.add).then_inc(signal, 1)

        def a0_dve(v):
            v.wait_ge(s_uqc, 8)

            def pre(k, s_, first):
                if not first:
                    v.wait_ge(s_score, k - 1)
                for q in range(4):
                    preact(nc.vector, k, s_, 0, q, s_preA)
                for q in range(2):
                    preact(nc.vector, k, s_, 1, q, s_preA)

            pre(0, 0, True)
            pre(1, 1, True)
            with v.Fori(1, 8) as kk:
                pre(2 * kk, 0, False)
                pre(2 * kk + 1, 1, False)
            v.wait_ge(s_mask, 1)
            v.wait_ge(s_score, 16)
            for q in range(4):
                ni = 16 * (q + 1)
                nc.vector.tensor_tensor(SS[:, 8 * q:8 * q + 8, 0:ni],
                                        PS[:, q, :].rearrange("p (t i) -> p t i", t=8)[:, :, 0:ni],
                                        MASK[:, 8 * q:8 * q + 8, 0:ni], ALU.mult).then_inc(s_ss, 1)
            for r in range(4):
                v.wait_ge(s_att, r // 2 + 1)
                for h in range(2):
                    ins = nc.vector.tensor_tensor(half(q3(H, r), h), half(q3(H, r), h), half(bank3(r ^ h), h), ALU.add)
                ins.then_inc(s_h1, 1)

        def a0_pool(p):
            ln_wait(p, 0, "var", NQ)
            pool_chain.link(p, nc.gpsimd.memset(MASK[:, :, :], 1.0))
            for par in range(2):
                m = MASK[64 * par:64 * par + 64, :, :]
                pool_chain.link(p, nc.gpsimd.affine_select(out=m, in_=m, compare_op=ALU.is_ge, fill=0.0, base=par,
                                                           pattern=[[2, 32], [-1, 64]], channel_multiplier=0))
            ln_wait(p, 0, "out", NQ)
            nc.gpsimd.memset(SS[:, :, :], 0.0).then_inc(s_mask, 1)
            p.wait_ge(s_uqc, 8)

            def pre(k, s_, first):
                if not first:
                    p.wait_ge(s_score, k - 1)
                for q in range(2, 4):
                    preact(nc.gpsimd, k, s_, 1, q, s_preB)

            pre(0, 0, True)
            pre(1, 1, True)
            with p.Fori(1, 8) as kk:
                pre(2 * kk, 0, False)
                pre(2 * kk + 1, 1, False)

        def a0_sp(sp):
            sp.wait_ge(s_h1, 4)
            for h in range(2):
                sp.dma_start(scratch[:, 32 * h:32 * h + 32, :], H[64 * h:64 * h + 64, :, :]).then_inc(s_h1st, 16)
            sp.wait_ge(s_h1st, 32)
            src = scratch.rearrange("(j b) t e -> b t j e", b=2)
            for b in range(2):
                sp.dma_start(H[64 * b:64 * b + 64, :, :], src[b]).then_inc(s_h1ld, 16)

        XS = BIG[:, 0:4096].rearrange("p (j c e) -> p j c e", j=NJ, c=2)
        HB = BIG[:, 4096:6144].rearrange("p (u n) -> p u n", u=4)
        HW = BIG[:, 6144:8192].rearrange("p (u n) -> p u n", u=4)
        YE = BIG[:, 8192:8704]
        WS = BIG[:, 8704:9728].bitcast(BF16).rearrange("p (j m) -> p j m", j=NJ)
        WT3 = BIG[:, 10240:12288].bitcast(BF16)
        B2S = sb("B2S", [48, 3, P], BF16)
        SMALL = sb("SMALL", [P, 256])

        moe_sems = {}

        class Moe:

            def __init__(self, n, nch, ne, act, before, pooled=False):
                self.n, self.nch, self.ne, self.act, self.pooled, self.before = n, nch, ne, act, pooled, before
                self.np = nch // 2
                units = NG * nch
                self.steps = dict(split=NQ, xt=NG, xtc=NG, wprep=1, b2prep=1, logits=1, gap=1, tanh=1, wsplit=1,
                                  wt=1 if pooled else NG, wtc=1 if pooled else NG, mm1=units, hact=units, wbc=units,
                                  scaled=units, mm2=units // 2, yevac=NG, ii=NG, comb=NG,
                                  r1=1 if pooled else 0, r2=1 if pooled else NG * (n == 2), r3=2 if pooled else NG * (n == 2),
                                  r4=2 if pooled else 0, r5=1 if pooled else NG * (n == 1), r6=1 if pooled else 0,
                                  lnb=int(n == 2), scaled_norm=NQ * (n in (0, 3)), added=NQ * (n in (0, 3)))
                for x in self.steps:
                    if x not in moe_sems:
                        moe_sems[x] = sem(f"moe_{x}")

            def __getitem__(self, name):
                return moe_sems[name]

            def value(self, name, count):
                return count + sum(m.steps[name] for m in self.before)

            def wait(self, eng, name, count):
                eng.wait_ge(moe_sems[name], self.value(name, count))

        def split_three(v, src, dst, tmp, part, signal):
            p0 = dst(0)
            dve_chain.link(v, nc.vector.tensor_copy(p0, src))
            dve_chain.link(v, nc.vector.tensor_tensor(tmp, src, p0, ALU.subtract))
            dve_chain.link(v, nc.vector.tensor_copy(dst(1), tmp))
            dve_chain.link(v, nc.vector.tensor_tensor(tmp, tmp, dst(1), ALU.subtract))
            nc.vector.tensor_copy(dst(2), tmp).then_inc(signal, 1)

        def top2(v, M, lg, pp, nj, act_tanh=True):
            E = M.ne
            t = [RT[0:pp, i, 0:nj, 0:E] for i in range(8)]
            r = [RV[0:pp, i, 0:nj] for i in range(12)]
            bc = lambda x: x.unsqueeze(2).broadcast_to([pp, nj, E])
            prio = w["prio"][0:pp, 16 - E:16].unsqueeze(1).broadcast_to([pp, nj, E])
            L = lambda ins: dve_chain.link(v, ins)
            L(nc.vector.tensor_reduce(r[0], lg, AX.X, ALU.max))
            L(nc.vector.tensor_tensor(t[1], lg, bc(r[0]), ALU.is_equal))
            L(nc.vector.tensor_tensor(t[1], t[1], prio, ALU.mult))
            L(nc.vector.tensor_reduce(r[1], t[1], AX.X, ALU.max))
            L(nc.vector.tensor_tensor(t[2], bc(r[1]), prio, ALU.is_equal))
            L(nc.vector.tensor_scalar(t[3], t[2], BIG_NEG, None, ALU.mult))
            L(nc.vector.tensor_tensor(t[3], t[3], lg, ALU.add))
            L(nc.vector.tensor_reduce(r[2], t[3], AX.X, ALU.max))
            nc.vector.tensor_tensor(r[3], r[2], r[0], ALU.subtract).then_inc(M["gap"], 1)
            L(nc.vector.tensor_tensor(t[4], t[3], bc(r[2]), ALU.is_equal))
            L(nc.vector.tensor_tensor(t[4], t[4], prio, ALU.mult))
            L(nc.vector.tensor_reduce(r[4], t[4], AX.X, ALU.max))
            L(nc.vector.tensor_tensor(t[5], bc(r[4]), prio, ALU.is_equal))
            M.wait(v, "tanh", 1)
            L(nc.vector.tensor_scalar(r[6], r[5], 0.5, 0.5, ALU.mult, ALU.add))
            L(nc.vector.tensor_scalar(r[7], r[5], -0.5, 0.5, ALU.mult, ALU.add))
            L(nc.vector.tensor_tensor(t[5], t[5], bc(r[6]), ALU.mult))
            L(nc.vector.tensor_tensor(t[2], t[2], bc(r[7]), ALU.mult))
            L(nc.vector.tensor_tensor(t[6], t[2], t[5], ALU.add))
            return t[6], t[7]

        def moe_act_tanh(s, M, pp, nj):
            M.wait(s, "gap", 1)
            nc.scalar.activation(RV[0:pp, 5, 0:nj], RV[0:pp, 3, 0:nj], ACT.Tanh, scale=0.5).then_inc(M["tanh"], 1)

        def moe_dve(v, M, n_ln):
            n, nch, E = M.n, M.nch, M.ne
            v.wait_ge(s_late, 16 * n_late)
            v.wait_ge(s_w1[n], 16)
            cols = nch * P
            src = W1S
            if n == 2:
                M.wait(v, "lnb", 1)
                for e in range(E):
                    ins = nc.vector.tensor_scalar(W1S[:, e * 256:(e + 1) * 256], W1S[:, e * 256:(e + 1) * 256],
                                                  w["lng"][:, e:e + 1], None, ALU.mult)
                dve_chain.link(v, ins)
                dve_chain.link(v, nc.vector.tensor_tensor(w["b1_2"][:, :], w["b1_2"][:, :], PS[:, 7, 0:16], ALU.add))
            dve_chain.link(v, nc.vector.tensor_copy(WH[:, 0:cols], W1S[:, 0:cols]))
            nc.vector.tensor_tensor(WL[:, 0:cols], W1S[:, 0:cols], WH[:, 0:cols].bitcast(F32), ALU.subtract).then_inc(M["wprep"], 1)
            e3 = 3 * E
            if n == 0:
                dve_chain.link(v, nc.vector.memset(B2S[:, :, D:P], 0.0))
            split_three(v, w[f"b2_{n}"][0:e3, :], lambda i: B2S[0:e3, i, 0:D], SMALL[0:e3, 0:64], e3, M["b2prep"])
            for q in range(NQ):
                ln_wait(v, n_ln, "out", q + 1)
                hi = XS[:, q * QJ:(q + 1) * QJ, 0, :]
                dve_chain.link(v, nc.vector.tensor_copy(hi.bitcast(F32R), q3(XN(M), q)))
                nc.vector.tensor_tensor(XS[:, q * QJ:(q + 1) * QJ, 1, :], q3(XN(M), q), hi, ALU.subtract).then_inc(M["split"], 1)
            if M.pooled:
                pooled_dve(v, M)
            else:
                M.wait(v, "logits", 1)
                lg = RT[:, 0, :, 0:E]
                rb = w[f"rb_{n}"][:, :].unsqueeze(1).broadcast_to([P, NJ, E])
                dve_chain.link(v, nc.vector.tensor_tensor(lg, PS[:, 6, 0:NJ * E].rearrange("p (j e) -> p j e", j=NJ), rb, ALU.add))
                wd, tmp = top2(v, M, lg, P, NJ)
                split_three(v, wd, lambda i: WS[:, :, i * E:(i + 1) * E], tmp, P, M["wsplit"])
            moe_main_dve(v, M)

        def XN(M):
            return XC if M.n == 2 else XA

        def pooled_dve(v, M):
            E = M.ne
            L = lambda ins: dve_chain.link(v, ins)
            M.wait(v, "r1", 1)
            nc.vector.tensor_copy(SMALL[0:64, 64:128], PS[0:64, 6, 0:64]).then_inc(M["r2"], 1)
            M.wait(v, "logits", 1)
            lg = RT[0:64, 0, 0, 0:E]
            r = [RV[0:64, i, 0:1] for i in range(8, 12)]
            L(nc.vector.tensor_tensor(lg, PS[0:64, 7, 0:E], w["rb_0"][0:64, :], ALU.add))

            def softmax(x, ex, step):
                L(nc.vector.tensor_reduce(r[0], x, AX.X, ALU.max))
                nc.vector.tensor_scalar(ex, x, r[0], None, ALU.subtract).then_inc(M["r3"], 1)
                M.wait(v, "r4", step)
                L(nc.vector.tensor_reduce(r[1], ex, AX.X, ALU.add))
                L(nc.vector.reciprocal(r[2], r[1]))
                return nc.vector.tensor_scalar(x, ex, r[2], None, ALU.mult)

            softmax(lg, RT[0:64, 1, 0, 0:E], 1).then_inc(M["r5"], 1)
            M.wait(v, "r6", 1)
            sc = RT[0:64, 2, 0, 0:E]
            tokens_per_image = float(NT)
            capacity = float(-(-NI * NT * 5 // (4 * E)))
            L(nc.vector.tensor_scalar(sc, PS[0:64, 5, 0:E], tokens_per_image, None, ALU.mult))
            L(nc.vector.reciprocal(sc, sc))
            L(nc.vector.tensor_scalar(sc, sc, capacity, 1.0, ALU.mult, ALU.min))
            L(nc.vector.tensor_tensor(lg, lg, sc, ALU.mult))
            L(softmax(lg, RT[0:64, 1, 0, 0:E], 2))
            wd, tmp = top2(v, M, RT[0:64, 0, 0:1, 0:E], 64, 1)
            split_three(v, wd, lambda i: WS[0:64, 0:1, i * E:(i + 1) * E], tmp, 64, M["wsplit"])
            M.wait(v, "wt", 1)
            src = PS[0:3 * E, 4, 0:32].bitcast(BF16)
            nc.vector.tensor_copy(WT3[0:3 * E, :].rearrange("p (b t) -> p b t", b=NI),
                                  src.unsqueeze(2).broadcast_to([3 * E, NI, NT])).then_inc(M["wtc"], 1)

        def pooled_act(s, M):
            E = M.ne
            for step in range(2):
                M.wait(s, "r3", step + 1)
                ex = RT[0:64, 1, 0, 0:E]
                nc.scalar.activation(ex, ex, ACT.Exp).then_inc(M["r4"], 1)

        def pooled_pe(pe, M):
            E = M.ne
            for j in range(NJ):
                ins = nc.tensor.matmul(PS[0:64, 6, 2 * j:2 * j + 2], XA[:, j, :], w["pool2"][:, :], start=True, stop=True)
            ins.then_inc(M["r1"], 1)
            M.wait(pe, "r2", 1)
            nc.tensor.matmul(PS[0:64, 7, 0:E], SMALL[0:64, 64:128], w["rw_0"][0:64, :], start=True, stop=True).then_inc(M["logits"], 1)
            M.wait(pe, "r5", 1)
            nc.tensor.matmul(PS[0:64, 5, 0:E], w["ones64"][:, :], RT[0:64, 0, 0, 0:E], start=True, stop=True).then_inc(M["r6"], 1)
            M.wait(pe, "wsplit", 1)
            nc.tensor.transpose(PS[0:3 * E, 4, 0:32].bitcast(BF16), WS[0:64, 0, 0:3 * E], w["Ib"][0:64, 0:64]).then_inc(M["wt"], 1)

        def moe_pe(pe, M):
            n, nch, E = M.n, M.nch, M.ne
            if n == 2:
                pe.wait_ge(s_w1[n], 16)
                pe.wait_ge(s_late, 16 * n_late)
                for c in range(nch):
                    ins = nc.tensor.matmul(PS[:, 7, c:c + 1], W1S[0:64, c * P:(c + 1) * P], w["lnb"][0:64, c // 2:c // 2 + 1],
                                           start=True, stop=True)
                ins.then_inc(M["lnb"], 1)
            for g in range(NG):
                M.wait(pe, "split", g // 2 + 1)
                if g >= 4:
                    M.wait(pe, "xtc", g - 3)
                for i in range(4):
                    ins = nc.tensor.transpose(PS[:, g % 4, i * P:(i + 1) * P],
                                              XS[:, 4 * g + i, :, :].rearrange("p c e -> p (c e)"), w["I"][:, :])
                ins.then_inc(M["xt"], 1)
            if M.pooled:
                pe.wait_ge(s_late, 16 * n_late)
                pooled_pe(pe, M)
            else:
                route_pe(pe, M)
                M.wait(pe, "wsplit", 1)
                for g in range(NG):
                    if g >= 4:
                        M.wait(pe, "wtc", g - 3)
                    for i in range(4):
                        ins = nc.tensor.transpose(PS[0:3 * E, g % 4, i * 64:(i + 1) * 64].bitcast(BF16), WS[:, 4 * g + i, 0:3 * E],
                                                  w["Ib"][:, :])
                    ins.then_inc(M["wt"], 1)
            moe_main_pe(pe, M)

        def route_pe(pe, M):
            n, E = M.n, M.ne
            if n == 2:
                for g in range(NG):
                    ln_wait(pe, 6, "out", g // 2 + 1)
                    if g < 4:
                        M.wait(pe, "xtc", g + 5)
                    else:
                        M.wait(pe, "r3", g - 3)
                    for i in range(4):
                        ins = nc.tensor.transpose(PS[0:64, g % 4, i * P:(i + 1) * P], XA[:, 4 * g + i, :], w["I"][:, :])
                    ins.then_inc(M["r2"], 1)
                M.wait(pe, "r3", NG)
                xt, k = XT, 64
            else:
                M.wait(pe, "xtc", NG)
                xt, k = XTR, P
            for j in range(NJ):
                lhs = xt[0:k, j * P:(j + 1) * P]
                if n != 2:
                    lhs = lhs.bitcast(F32)
                ins = nc.tensor.matmul(PS[:, 6, j * E:(j + 1) * E], lhs, w[f"rw_{n}"][0:k, :], start=True, stop=True)
            ins.then_inc(M["logits"], 1)

        def moe_act(s, M):
            n, nch, E = M.n, M.nch, M.ne
            for g in range(NG):
                M.wait(s, "xt", g + 1)
                nc.scalar.copy(XTR[:, g * 512:(g + 1) * 512], PS[:, g % 4, :]).then_inc(M["xtc"], 1)
            if M.pooled:
                pooled_act(s, M)
                moe_act_tanh(s, M, 64, 1)
            else:
                if n == 2:
                    for g in range(NG):
                        M.wait(s, "r2", g + 1)
                        nc.scalar.copy(XT[0:64, g * 512:(g + 1) * 512], PS[0:64, g % 4, :]).then_inc(M["r3"], 1)
                moe_act_tanh(s, M, P, NJ)
                for g in range(NG):
                    M.wait(s, "wt", g + 1)
                    src = PS[0:3 * E, g % 4, 0:256].bitcast(BF16)
                    nc.scalar.copy(WT3[0:3 * E, g * 512:(g + 1) * 512], src).then_inc(M["wtc"], 1)
            moe_main_act(s, M)

        ZB, BB, YB, TB = 0, 4, 6, 7

        def moe_main_pe(pe, M):
            n, nch, NPR, e3 = M.n, M.nch, M.np, 3 * M.ne
            M.wait(pe, "wprep", 1)
            M.wait(pe, "b2prep", 1)
            M.wait(pe, "xtc", NG)
            M.wait(pe, "wtc", 1 if M.pooled else NG)
            SEL = w[f"sel_{n}"]
            W2 = w[f"w2_{n}"]

            def up(g, p, first, fresh_banks=False, before_last=lambda: None):
                if not first and not fresh_banks:
                    M.wait(pe, "hact", g * nch + 2 * p - 2)
                for i in range(2):
                    c = 2 * p + i
                    z = PS[:, ZB + c % 4, :]
                    x = XTR[:, bass.ds(g * 512, 512)]
                    nc.tensor.matmul(z, WH[:, c * P:(c + 1) * P], x, start=True, stop=False)
                    if i == 1 and not first:
                        M.wait(pe, "scaled", g * nch + 2 * p)
                        before_last()
                    nc.tensor.matmul(z, WL[:, c * P:(c + 1) * P], x, start=False, stop=True).then_inc(M["mm1"], 1)
                for i in range(2):
                    c = 2 * p + i
                    nc.tensor.matmul(PS[:, BB + i, :], SEL[0:e3, c * P:(c + 1) * P], WT3[0:e3, bass.ds(g * 512, 512)],
                                     start=True, stop=True).then_inc(M["wbc"], 1)

            def down(g, p):
                M.wait(pe, "scaled", g * nch + 2 * p + 2)
                for i in range(2):
                    c = 2 * p + i
                    ins = nc.tensor.matmul(PS[64 * i:64 * i + 64, YB, :], W2[:, c, :], HW[:, c % 4, :],
                                           start=False, stop=(p == NPR - 1), skip_group_check=True)
                ins.then_inc(M["mm2"], 1)

            def group(g, first, last):
                def output_bank_free():
                    if not first:
                        M.wait(pe, "yevac", g)

                for p in range(NPR):
                    if p == 0:
                        up(g, 1, False, first, output_bank_free)
                        for i in range(3):
                            nc.tensor.matmul(PS[:, YB, :], B2S[0:e3, i, :], WT3[0:e3, bass.ds(g * 512, 512)],
                                             start=i == 0, stop=False, skip_group_check=True)
                    elif p < NPR - 1:
                        up(g, p + 1, False)
                    elif not last:
                        up(g + 1, 0, False)
                    down(g, p)
                M.wait(pe, "yevac", g + 1)
                if not first:
                    M.wait(pe, "comb", g)
                for i in range(4):
                    ins = nc.tensor.matmul(PS[:, TB, i * 64:i * 64 + 64], YE[:, i * P:(i + 1) * P], w["II"][:, :],
                                           start=True, stop=True)
                ins.then_inc(M["ii"], 1)

            up(0, 0, True)
            group(0, True, False)
            with pe.Fori(1, NG - 1) as g:
                group(g, False, False)
            group(NG - 1, False, True)

        def moe_main_act(s, M):
            n, nch = M.n, M.nch

            def group(g, first):
                for c in range(nch):
                    M.wait(s, "mm1", g * nch + c + 1)
                    if not (first and c < 4):
                        M.wait(s, "scaled", g * nch + c - 3)
                    nc.scalar.activation(HB[:, c % 4, :], PS[:, ZB + c % 4, :], M.act, bias=w[f"b1_{n}"][:, c:c + 1]
                                         ).then_inc(M["hact"], 1)

            M.wait(s, "wprep", 1)
            group(0, True)
            with s.Fori(1, NG) as g:
                group(g, False)

        def moe_main_dve(v, M):
            n, nch, NPR = M.n, M.nch, M.np

            def group(g, first):
                for c in range(nch):
                    M.wait(v, "hact", g * nch + c + 1)
                    M.wait(v, "wbc", g * nch + c + 1)
                    if not (first and c < 4) and c % 2 == 0:
                        M.wait(v, "mm2", g * NPR + c // 2 - 1)
                    nc.vector.tensor_tensor(HW[:, c % 4, :], HB[:, c % 4, :], PS[:, BB + c % 2, :], ALU.mult).then_inc(M["scaled"], 1)
                M.wait(v, "mm2", g * NPR + NPR)
                if not first:
                    M.wait(v, "ii", g)
                nc.vector.tensor_copy(YE[:, :], PS[:, YB, :]).then_inc(M["yevac"], 1)
                M.wait(v, "ii", g + 1)
                y = PS[:, TB, 0:256].rearrange("p (j e) -> p j e", j=4)
                hg = H[:, bass.ds(g * 4, 4), :]
                xg = XA[:, bass.ds(g * 4, 4), :]
                if n in (0, 3):
                    nc.vector.tensor_tensor(xg, xg, y, ALU.add).then_inc(M["comb"], 1)
                elif n == 1:
                    nc.vector.tensor_tensor(xg, xg, y, ALU.add).then_inc(M["r5"], 1)
                    M.wait(v, "r5", g + 1)
                    nc.vector.tensor_tensor(hg, hg, xg, ALU.add).then_inc(M["comb"], 1)
                else:
                    nc.vector.tensor_tensor(hg, hg, y, ALU.add).then_inc(M["comb"], 1)

            group(0, True)
            with v.Fori(1, NG) as g:
                group(g, False)

        def post_norm_dve(v, M, n_ln):
            ln_dve(v, n_ln, XA, XA, lambda q: M.wait(v, "comb", NG))
            gm = w[f"gamma_{M.n}"][:, :].unsqueeze(1).broadcast_to([P, QJ, D])
            bt = w[f"beta_{M.n}"][:, :].unsqueeze(1).broadcast_to([P, QJ, D])
            for q in range(NQ):
                ln_wait(v, n_ln, "out", q + 1)
                nc.vector.tensor_tensor(q3(XA, q), q3(XA, q), gm, ALU.mult).then_inc(M["scaled_norm"], 1)
            for q in range(NQ):
                M.wait(v, "scaled_norm", q + 1)
                nc.vector.tensor_tensor(q3(H, q), q3(H, q), bt, ALU.add).then_inc(dve_chain.s, 1)
                dve_chain.n += 1
            v.wait_ge(dve_chain.s, dve_chain.n)
            for q in range(NQ):
                nc.vector.tensor_tensor(q3(H, q), q3(H, q), q3(XA, q), ALU.add).then_inc(M["added"], 1)

        moes = []
        for n_, nch_, ne_, act_ in ((0, 8, 8, ACT.Gelu), (1, 4, 8, ACT.Gelu), (2, 16, 8, ACT.Gelu), (3, 16, 16, ACT.Relu)):
            moes.append(Moe(n_, nch_, ne_, act_, list(moes), pooled=n_ == 0))

        ATT = {1: "aw awc xt xtc gt gtc s v vc exp sub pt ptc norm o oh",
               2: "xt xtc coef s kv rexp kin kexp shift wkv rw rt rtc o oh",
               3: "xt xtc q qc om omc z zc r rc rr oh"}
        att = {n: {x: sem(f"att{n}_{x}") for x in names.split()} for n, names in ATT.items()}

        GT = BIG[0:64, 0:4096]
        PE_ = BIG[:, 4096:6144].rearrange("p (j k) -> p j k", j=NJ)
        PT = BIG[:, 6144:8192].rearrange("p (j k) -> p j k", j=NJ)
        VV = BIG[:, 8192:10240].rearrange("p (j k) -> p j k", j=NJ)
        AW = BIG[0:64, 10240:10304]

        def xt_pe(pe, T, n_ln):
            for g in range(NG):
                ln_wait(pe, n_ln, "out", g // 2 + 1)
                if g >= 2:
                    pe.wait_ge(T["xtc"], g - 1)
                for i in range(4):
                    ins = nc.tensor.transpose(PS[0:64, g % 2, i * P:(i + 1) * P], XA[:, 4 * g + i, :], w["I"][:, :])
                ins.then_inc(T["xt"], 1)

        def a1_pe(pe):
            T = att[1]
            pe.wait_ge(s_late, 16 * n_late)
            xt_pe(pe, T, 3)
            nc.tensor.matmul(PS[0:64, 7, 0:64], w["wqT"][:, :], w["wkT"][:, :], start=True, stop=True).then_inc(T["aw"], 1)
            pe.wait_ge(T["awc"], 1)
            pe.wait_ge(T["xtc"], NG)
            for g in range(NG):
                if g >= 2:
                    pe.wait_ge(T["gtc"], g - 1)
                nc.tensor.matmul(PS[0:64, 4 + g % 2, :], AW, XT[0:64, g * 512:(g + 1) * 512], start=True, stop=True
                                 ).then_inc(T["gt"], 1)
            for j in range(NJ):
                if j % 8 == 0:
                    pe.wait_ge(T["gtc"], 2 * (j // 8) + 2)
                for b in range(2):
                    c = j * P + b * 64
                    ins = nc.tensor.matmul(PS[64 * b:64 * b + 64, j // 8, (j % 8) * 64:(j % 8) * 64 + 64],
                                           GT[:, c:c + 64], XT[0:64, c:c + 64], start=True, stop=True)
                if j % 8 == 7:
                    ins.then_inc(T["s"], 1)
            for q in range(4):
                pe.wait_ge(T["gtc"], NG)
                for i in range(8):
                    j = 8 * q + i
                    ins = nc.tensor.matmul(PS[:, 4 + q, i * 64:i * 64 + 64], XT[0:64, j * P:(j + 1) * P], w["wv"][:, :],
                                           start=True, stop=True)
                ins.then_inc(T["v"], 1)
            for qq in range(2):
                pe.wait_ge(T["exp"], 2 * qq + 2)
                for j in range(16 * qq, 16 * qq + 16):
                    for b in range(2):
                        ins = nc.tensor.matmul(PS[64 * b:64 * b + 64, (j // 8) ^ b, (j % 8) * 64:(j % 8) * 64 + 64],
                                               PE_[64 * b:64 * b + 64, j, :], w["I"][64 * b:64 * b + 64, 64 * b:64 * b + 64],
                                               start=True, stop=True)
                ins.then_inc(T["pt"], 1)
            for qq in range(2):
                pe.wait_ge(T["ptc"], qq + 1)
                pe.wait_ge(T["vc"], 2 * qq + 2)
                for j in range(16 * qq, 16 * qq + 16):
                    for b in range(2):
                        r = slice(64 * b, 64 * b + 64)
                        ins = nc.tensor.matmul(PS[r, 4 + ((j // 8) ^ b), (j % 8) * 64:(j % 8) * 64 + 64], PT[r, j, :], VV[r, j, :],
                                               start=True, stop=True)
                ins.then_inc(T["o"], 1)

        def a1_act(s):
            T = att[1]
            for g in range(NG):
                s.wait_ge(T["xt"], g + 1)
                nc.scalar.copy(XT[0:64, g * 512:(g + 1) * 512], PS[0:64, g % 2, :]).then_inc(T["xtc"], 1)
            s.wait_ge(T["aw"], 1)
            nc.scalar.mul(AW, PS[0:64, 7, 0:64], float(D) ** -0.5).then_inc(T["awc"], 1)
            for g in range(NG):
                s.wait_ge(T["gt"], g + 1)
                nc.scalar.copy(GT[:, g * 512:(g + 1) * 512], PS[0:64, 4 + g % 2, :]).then_inc(T["gtc"], 1)
            for q in range(4):
                s.wait_ge(T["sub"], q + 1)
                nc.scalar.activation(q3(PE_, q), q3(PE_, q), ACT.Exp).then_inc(T["exp"], 1)
            for q in range(4):
                s.wait_ge(T["v"], q + 1)
                nc.scalar.copy(q3(VV, q), bank3(4 + q)).then_inc(T["vc"], 1)
            for qq in range(2):
                s.wait_ge(T["pt"], qq + 1)
                for q in (2 * qq, 2 * qq + 1):
                    for b in range(2):
                        ins = nc.scalar.copy(half(q3(PT, q), b), half(bank3(q ^ b), b))
                ins.then_inc(T["ptc"], 1)

        def half(t, b):
            return t[64 * b:64 * b + 64]

        def bank3(b):
            return PS[:, b, :].rearrange("p (j e) -> p j e", j=8)

        def a1_dve(v):
            T = att[1]
            for q in range(4):
                v.wait_ge(T["s"], q + 1)
                m = RV[:, 0, 8 * q:8 * q + 8]
                dve_chain.link(v, nc.vector.tensor_reduce(m, bank3(q), AX.X, ALU.max))
                nc.vector.tensor_tensor(q3(PE_, q), bank3(q), bc_j(RV[:, 0, :], q), ALU.subtract).then_inc(T["sub"], 1)
            for q in range(4):
                v.wait_ge(T["exp"], q + 1)
                ins = nc.vector.tensor_reduce(RV[:, 1, 8 * q:8 * q + 8], q3(PE_, q), AX.X, ALU.add)
                dve_chain.link(v, ins)
            dve_chain.link(v, nc.vector.reciprocal(RV[:, 2, :], RV[:, 1, :]))
            for q in range(4):
                v.wait_ge(T["o"], q // 2 + 1)
                for b in range(2):
                    ins = nc.vector.tensor_tensor(half(q3(XC, q), b), half(bank3(4 + (q ^ b)), b), half(bc_j(RV[:, 2, :], q), b), ALU.mult)
                ins.then_inc(T["norm"], 1)
                v.wait_ge(T["norm"], q + 1)
                nc.vector.tensor_tensor(q3(H, q), q3(H, q), q3(XC, q), ALU.add).then_inc(T["oh"], 1)

        KK = BIG[:, 0:2048].rearrange("p (j e) -> p j e", j=NJ)
        KV = BIG[:, 2048:4096].rearrange("p (j e) -> p j e", j=NJ)
        RR = BIG[:, 4096:6144].rearrange("p (j e) -> p j e", j=NJ)
        DN = BIG[:, 6144:8192].rearrange("p (j e) -> p j e", j=NJ)
        RWT = BIG[0:64, 8192:12288]
        XSH = XT

        def a2_pe(pe):
            T = att[2]
            xt_pe(pe, T, 5)
            pe.wait_ge(T["coef"], 3)
            for j in range(NJ):
                if j % 2 == 0:
                    pe.wait_ge(T["xtc"], j // 4 + 1)
                    pe.wait_ge(T["shift"], j // 4 + 1)
                if j >= 4:
                    pe.wait_ge(T["kv"], j - 3)
                    pe.wait_ge(T["rexp"], j - 3)
                nc.tensor.matmul(PS[:, 2 + j % 4, 0:192], XSH[:, j * P:(j + 1) * P], w["wkvr"][:, :], start=True, stop=True
                                 ).then_inc(T["s"], 1)
            for q in range(4):
                pe.wait_ge(T["kv"], NJ)
                pe.wait_ge(T["rexp"], NJ)
                pe.wait_ge(T["xtc"], NG)
                if q >= 2:
                    pe.wait_ge(T["rw"], q - 1)
                nc.tensor.matmul(PS[:, 2 * (q % 2), :], w["cum"][:, :], q3(KK, q), start=True, stop=True)
                nc.tensor.matmul(PS[:, 2 * (q % 2) + 1, :], w["toep"][:, :], q3(KV, q), start=True, stop=True).then_inc(T["wkv"], 1)
            for g in range(NG):
                pe.wait_ge(T["rw"], g // 2 + 1)
                if g >= 2:
                    pe.wait_ge(T["rtc"], g - 1)
                for i in range(4):
                    ins = nc.tensor.transpose(PS[0:64, 4 + g % 2, i * P:(i + 1) * P], RR[:, 4 * g + i, :], w["I"][:, :])
                ins.then_inc(T["rt"], 1)
            for q in range(4):
                pe.wait_ge(T["rtc"], 2 * q + 2)
                pe.wait_ge(T["rw"], 4)
                for i in range(8):
                    j = 8 * q + i
                    ins = nc.tensor.matmul(PS[:, q, i * 64:i * 64 + 64], RWT[:, j * P:(j + 1) * P], w["wo"][:, :], start=True, stop=True)
                ins.then_inc(T["o"], 1)

        def a2_act(s):
            T = att[2]
            for g in range(NG):
                s.wait_ge(T["xt"], g + 1)
                nc.scalar.copy(XSH[0:64, g * 512:(g + 1) * 512], PS[0:64, g % 2, :])
                shifted = XSH[64:128, g * 512:(g + 1) * 512].rearrange("p (b t) -> p b t", b=8)
                src = PS[0:64, g % 2, :].rearrange("p (b t) -> p b t", b=8)
                nc.scalar.copy(shifted[:, :, 1:NT], src[:, :, 0:NT - 1]).then_inc(T["xtc"], 1)
            for j in range(NJ):
                s.wait_ge(T["kin"], j + 1)
                nc.scalar.activation(RR[:, j, :], PS[:, 2 + j % 4, 128:192], ACT.Exp, scale=-1.0).then_inc(T["rexp"], 1)
                s.wait_ge(T["rexp"], j + 1)
                nc.scalar.activation(KK[:, j, :], KK[:, j, :], ACT.Exp).then_inc(T["kexp"], 1)
            for g in range(NG):
                s.wait_ge(T["rt"], g + 1)
                nc.scalar.copy(RWT[:, g * 512:(g + 1) * 512], PS[0:64, 4 + g % 2, :]).then_inc(T["rtc"], 1)

        def a2_dve(v):
            T = att[2]
            v.wait_ge(s_late, 16 * n_late)
            dve_chain.link(v, nc.vector.tensor_scalar(w["mix"][:, :], w["mix"][:, :], w["mixab"][:, 0:1], w["mixab"][:, 1:2],
                                                      ALU.mult, ALU.add))
            for i in range(3):
                nc.vector.tensor_scalar(w["wkvr"][:, 64 * i:64 * i + 64], w["wkvr"][:, 64 * i:64 * i + 64],
                                        w["mix"][:, i:i + 1], None, ALU.mult).then_inc(T["coef"], 1)
            for g in range(NG):
                z = XSH[64:128, g * 512:(g + 1) * 512].rearrange("p (b t) -> p b t", b=8)[:, :, 0:1]
                nc.vector.memset(z, 0.0).then_inc(T["shift"], 1)
            for j in range(NJ + 1):
                if j < NJ:
                    v.wait_ge(T["s"], j + 1)
                    nc.vector.tensor_scalar(KK[:, j, :], PS[:, 2 + j % 4, 0:64], -60.0, 30.0, ALU.max, ALU.min).then_inc(T["kin"], 1)
                if j >= 1:
                    v.wait_ge(T["kexp"], j)
                    nc.vector.tensor_tensor(KV[:, j - 1, :], KK[:, j - 1, :], PS[:, 2 + (j - 1) % 4, 64:128], ALU.mult
                                            ).then_inc(T["kv"], 1)
            v.wait_ge(T["rexp"], NJ)
            for q in range(4):
                v.wait_ge(T["wkv"], q + 1)
                dve_chain.link(v, nc.vector.scalar_tensor_tensor(out=flat(DN, q), in0=flat(RR, q), scalar=1.0, in1=PS[:, 2 * (q % 2), :],
                                                                 op0=ALU.add, op1=ALU.mult))
                dve_chain.link(v, nc.vector.reciprocal(q3(DN, q), q3(DN, q)))
                nc.vector.tensor_tensor(q3(RR, q), q3(DN, q), bank3(2 * (q % 2) + 1), ALU.mult).then_inc(T["rw"], 1)
            for q in range(4):
                v.wait_ge(T["o"], q + 1)
                nc.vector.tensor_tensor(q3(H, q), q3(H, q), bank3(q), ALU.add).then_inc(T["oh"], 1)

        def flat(t, q):
            return q3(t, q).rearrange("p j e -> p (j e)")

        QS = BIG[:, 0:16384].rearrange("p (k n) -> p k n", k=4)
        OMS = WORK[:, 0:1024].rearrange("p (u n) -> p u n", u=2)
        RTT = WORK[:, 1024:2048].rearrange("p (u n) -> p u n", u=2)
        ZT = LNB[:, :, :].rearrange("p (u k j) e -> p u k (j e)", u=2, k=4)

        def a3_pe(pe):
            T = att[3]
            xt_pe(pe, T, 8)
            for g in range(NG):
                pe.wait_ge(T["xtc"], g + 1)
                for k in range(4):
                    u = g * 4 + k
                    if u >= 2:
                        pe.wait_ge(T["qc"], u - 1)
                    nc.tensor.matmul(PS[:, 2 + u % 2, :], w["qh"][:, k * P:(k + 1) * P], XT[0:64, g * 512:(g + 1) * 512],
                                     start=True, stop=True).then_inc(T["q"], 1)
            pe.wait_ge(T["qc"], 4 * NG)
            for step in range(NJ + 4):
                j = step
                if j < NJ:
                    if j >= 2:
                        pe.wait_ge(T["omc"], j - 1)
                    for par in range(2):
                        for b in range(2):
                            c = j * P + b * 64
                            r = slice(64 * par, 64 * par + 64)
                            o = PS[64 * b:64 * b + 64, 2 * par + j % 2, 0:256].rearrange("p (k t) -> p k t", k=4)
                            ins = nc.tensor.matmul(o, XT[r, c:c + 64], QS[r, :, c:c + 64], start=True, stop=True)
                    ins.then_inc(T["om"], 1)
                j = step - 1
                if 0 <= j < NJ:
                    pe.wait_ge(T["omc"], j + 1)
                    if j >= 1:
                        pe.wait_ge(T["zc"], j)
                    for b in range(2):
                        for par in range(2):
                            r = slice(64 * b, 64 * b + 64)
                            ins = nc.tensor.matmul(PS[64 * par:64 * par + 64, 4 + b, 0:256], XA[r, j, :],
                                                   OMS[r, j % 2, par * 256:par * 256 + 256], start=True, stop=True)
                    ins.then_inc(T["z"], 1)
                j = step - 2
                if 0 <= j < NJ and j % 4 == 3:
                    g = j // 4
                    pe.wait_ge(T["zc"], j + 1)
                    if g >= 1:
                        pe.wait_ge(T["rc"], g)
                    for k in range(4):
                        h = k % 2
                        ins = nc.tensor.matmul(PS[64 * h:64 * h + 64, 6, :], w["eh"][:, k, :], ZT[:, g % 2, k, :], start=k < 2,
                                               stop=k >= 2, skip_group_check=True)
                    ins.then_inc(T["r"], 1)
                j = step - 3
                if 0 <= j < NJ and j % 4 == 3:
                    g = j // 4
                    pe.wait_ge(T["rc"], g + 1)
                    if g >= 1:
                        pe.wait_ge(T["oh"], g)
                    for i in range(4):
                        ins = nc.tensor.matmul(PS[:, 7, i * 64:i * 64 + 64], RTT[:, g % 2, i * P:(i + 1) * P], w["II"][:, :],
                                               start=True, stop=True)
                    ins.then_inc(T["rr"], 1)

        def a3_act(s):
            T = att[3]
            for g in range(NG):
                s.wait_ge(T["xt"], g + 1)
                nc.scalar.copy(XT[0:64, g * 512:(g + 1) * 512], PS[0:64, g % 2, :])
                nc.scalar.copy(XT[64:128, g * 512:(g + 1) * 512], PS[0:64, g % 2, :]).then_inc(T["xtc"], 1)
            for u in range(4 * NG):
                g, k = u // 4, u % 4
                s.wait_ge(T["q"], u + 1)
                nc.scalar.copy(QS[:, k, g * 512:(g + 1) * 512], PS[:, 2 + u % 2, :]).then_inc(T["qc"], 1)
            for j in range(NJ):
                s.wait_ge(T["z"], j + 1)
                g, i = j // 4, j % 4
                if g >= 2 and i == 0:
                    s.wait_ge(T["r"], g - 1)
                for b in range(2):
                    ins = nc.scalar.copy(ZT[:, g % 2, :, i * P + b * 64:i * P + b * 64 + 64],
                                         PS[:, 4 + b, 0:256].rearrange("p (k t) -> p k t", k=4))
                ins.then_inc(T["zc"], 1)

        def a3_dve(v):
            T = att[3]

            def tri_mask(j):
                v.wait_ge(T["om"], j + 1)
                if j >= 2:
                    v.wait_ge(T["z"], j - 1)
                tri = w["tri"][:, :].unsqueeze(1).broadcast_to([P, 4, 64])
                for par in range(2):
                    ins = nc.vector.tensor_tensor(OMS[:, j % 2, par * 256:par * 256 + 256].rearrange("p (k t) -> p k t", k=4),
                                                  PS[:, 2 * par + j % 2, 0:256].rearrange("p (k t) -> p k t", k=4), tri, ALU.mult)
                ins.then_inc(T["omc"], 1)

            for step in range(NJ + 5):
                if step < NJ:
                    tri_mask(step)
                j = step - 2
                if 0 <= j < NJ and j % 4 == 3:
                    g = j // 4
                    v.wait_ge(T["r"], g + 1)
                    if g >= 2:
                        v.wait_ge(T["rr"], g - 1)
                    nc.vector.tensor_copy(RTT[:, g % 2, :], PS[:, 6, :]).then_inc(T["rc"], 1)
                j = step - 4
                if 0 <= j < NJ and j % 4 == 3:
                    g = j // 4
                    v.wait_ge(T["rr"], g + 1)
                    hg = H[:, 4 * g:4 * g + 4, :]
                    nc.vector.tensor_tensor(hg, hg, PS[:, 7, 0:256].rearrange("p (j e) -> p j e", j=4), ALU.add
                                            ).then_inc(T["oh"], 1)

        block = ctx.enter_context(nc.Block())

        @block.sync
        def _(sp):
            tok_sp(sp)
            a0_sp(sp)
            for i in (1, 2, 3):
                moes[i - 1].wait(sp, "wprep", 1)
                cols = moes[i].nch * P
                sp.dma_start(W1S[:, 0:cols], a[f"w1_{i}"]).then_inc(s_w1[i], 16)
            dst = out.rearrange("(j b) t e -> b t j e", b=2)
            moes[3].wait(sp, "added", NQ)
            for b in range(2):
                sp.dma_start(dst[b], H[64 * b:64 * b + 64, :, :]).then_inc(s_out, 16)
            sp.wait_ge(s_out, 32)

        @block.scalar
        def _(s):
            for name in early:
                s.dma_start(w[name][:], a[name]).then_inc(s_early, 16)
            tok_act(s)
            s.wait_ge(s_early, 16 * n_early)
            ln_act(s, 0)
            a0_act(s)
            ln_act(s, 1)
            moe_act(s, moes[0])
            ln_act(s, 2)
            ln_act(s, 3)
            a1_act(s)
            s.wait_ge(s_late, 16 * n_late)
            ln_act(s, 4)
            moe_act(s, moes[1])
            ln_act(s, 5)
            a2_act(s)
            ln_act(s, 6)
            ln_act(s, 7)
            moe_act(s, moes[2])
            ln_act(s, 8)
            a3_act(s)
            ln_act(s, 9)
            moe_act(s, moes[3])
            ln_act(s, 10)

        @block.gpsimd
        def _(p):
            late = [k for k in w if k not in early]
            for name in late:
                p.dma_start(w[name][:], a[name]).then_inc(s_late, 16)
            p.dma_start(W1S[:, 0:moes[0].nch * P], a["w1_0"]).then_inc(s_w1[0], 16)
            pool_chain.link(p, nc.gpsimd.memset(HALFPOW[:, :], -0.5))
            ln_pool(p, 0)
            a0_pool(p)
            ln_pool(p, 1)
            ln_pool(p, 2)
            ln_pool(p, 3)
            ln_pool(p, 4)
            ln_pool(p, 5)
            ln_pool(p, 6)
            ln_pool(p, 7)
            ln_pool(p, 8)
            ln_pool(p, 9)
            ln_pool(p, 10)

        @block.vector
        def _(v):
            tok_dve(v)
            ln_dve(v, 0, H, XA, lambda q: v.wait_ge(s_h0, q + 1))
            a0_dve(v)
            ln_dve(v, 1, H, XA, lambda q: v.wait_ge(s_h1ld, 32))
            moe_dve(v, moes[0], 1)
            post_norm_dve(v, moes[0], 2)
            ln_dve(v, 3, H, XA, lambda q: moes[0].wait(v, "added", q + 1))
            a1_dve(v)
            ln_dve(v, 4, H, XA, lambda q: v.wait_ge(att[1]["oh"], q + 1))
            moe_dve(v, moes[1], 4)
            ln_dve(v, 5, H, XA, lambda q: moes[1].wait(v, "comb", NG))
            a2_dve(v)
            ln_dve(v, 6, H, XA, lambda q: v.wait_ge(att[2]["oh"], q + 1))
            ln_dve(v, 7, XA, XC, lambda q: ln_wait(v, 6, "out", NQ))
            moe_dve(v, moes[2], 7)
            ln_dve(v, 8, H, XA, lambda q: moes[2].wait(v, "comb", NG))
            a3_dve(v)
            ln_dve(v, 9, H, XA, lambda q: v.wait_ge(att[3]["oh"], NG))
            moe_dve(v, moes[3], 9)
            post_norm_dve(v, moes[3], 10)

        @block.tensor
        def _(pe):
            tok_pe(pe)
            a0_pe(pe)
            moe_pe(pe, moes[0])
            a1_pe(pe)
            moe_pe(pe, moes[1])
            a2_pe(pe)
            moe_pe(pe, moes[2])
            a3_pe(pe)
            moe_pe(pe, moes[3])


def resize_matrix(n, m=8):
    scale = n / m
    centre = (np.arange(m) + 0.5) * scale - 0.5
    t = np.maximum(0, 1 - np.abs(centre[:, None] - np.arange(n)[None]) / scale)
    return t / t.sum(1, keepdims=True)


def haar(n):
    lo, hi = np.zeros((n // 2, n)), np.zeros((n // 2, n))
    i = np.arange(n // 2)
    c = 0.7071067811865476
    lo[i, 2 * i] = lo[i, 2 * i + 1] = hi[i, 2 * i] = c
    hi[i, 2 * i + 1] = -c
    return lo, hi


def constants():
    lo1, hi1 = haar(224)
    lo2, hi2 = haar(112)
    r56, r112 = resize_matrix(56), resize_matrix(112)
    maps = np.concatenate([r56 @ lo2 @ lo1, r56 @ hi2 @ lo1, r112 @ lo1, r112 @ hi1])
    k = {}
    k["rowmap"] = maps.T.reshape(112, 2, 32)
    k["colmap"] = maps.T.reshape(2, 112, 32).transpose(1, 0, 2)
    eye, up = np.eye(128), np.triu(np.ones((64, 64)))
    k["I"] = eye
    k["IU"] = np.tile(np.concatenate([np.eye(64), up], 1), (2, 1))
    k["II"] = np.tile(np.eye(64), (2, 1))
    k["pool2"] = np.kron(np.eye(2), np.ones((64, 1))) / NT
    k["ones64"] = np.ones((64, 64))
    k["prio"] = np.tile(np.arange(16, 0, -1.0), (128, 1))
    k["cum"] = np.kron(np.eye(2), up)
    k["tri"] = np.tile(up, (2, 1))
    k["mixab"] = np.concatenate([np.tile([[1.0, 0.0]], (64, 1)), np.tile([[-1.0, 1.0]], (64, 1))])
    return {n: np.ascontiguousarray(v, np.float32) for n, v in k.items()}


def selectors(chunk_expert, ne):
    s = np.zeros((3 * ne, len(chunk_expert), 128), np.float32)
    for c, es in enumerate(chunk_expert):
        for half, e in enumerate(es):
            for part in range(3):
                s[part * ne + e, c, 64 * half:64 * half + 64] = 1
    return s.reshape(3 * ne, -1)


def bf16_bits(zeros_and_ones):
    return (zeros_and_ones != 0).astype(np.uint16) * np.uint16(0x3F80)


def laid_out(i):
    f = {k: np.asarray(v) for k, v in i.items()}
    a = {"x": f["x"]}
    a.update(constants())
    a["Ib"] = bf16_bits(np.eye(128))
    rep = lambda v, n=128: np.tile(v.reshape(1, -1), (n, 1))
    ops = [(0, 0), (1, 0), (0, 1), (1, 1), (3, 2), (2, 3), (3, 3)]
    tw = np.zeros((4, 8, 4, 8, 64), np.float32)
    for m, (ro, co) in enumerate(ops):
        for s in range(8):
            tw[co, s, ro, s, :] = f["L0_tok_W"][m]
    a["tokW"] = tw.reshape(32, 4, 512)
    a["tokb"] = rep(f["L0_tok_b"])
    bd = np.zeros((128, 3, 128), np.float32)
    for n, name in enumerate(("L0_attn_w1", "L0_attn_w2", "L0_attn_w3")):
        bd[:64, n, :64] = bd[64:, n, 64:] = f[name].T
    a["bd"] = bd
    a["b3"] = np.tile(f["L0_attn_b3"].reshape(-1, 1), (2, 1))
    w0 = np.zeros((128, 16, 32), np.float32)
    for k in range(16):
        w0[:64, k, 2 * k] = w0[64:, k, 2 * k + 1] = f["L0_attn_w0"]
    a["w0"] = w0
    dup = lambda v: np.concatenate([v, v], 0)

    def moe(n, w1, b1, w2, b2, rw, rb, chunk_expert):
        ne = w1.shape[0]
        nch = len(chunk_expert)
        a[f"w1_{n}"] = dup(w1.transpose(1, 0, 2).reshape(64, -1))
        a[f"b1_{n}"] = b1.reshape(nch, 128).T
        a[f"w2_{n}"] = w2.reshape(nch, 128, 64).transpose(1, 0, 2)
        a[f"b2_{n}"] = np.tile(b2, (3, 1))
        a[f"rw_{n}"] = dup(rw)
        a[f"rb_{n}"] = rep(rb)
        a[f"sel_{n}"] = bf16_bits(selectors(chunk_expert, ne))

    moe(0, f["L0_ffn_W1"], f["L0_ffn_b1"], f["L0_ffn_W2"], f["L0_ffn_b2"], f["L0_ffn_Wr"], f["L0_ffn_br"],
        [(e, e) for e in range(8)])
    moe(1, f["L1_ffn_w1"], f["L1_ffn_b1"], f["L1_ffn_w2"], f["L1_ffn_b2"], f["L1_ffn_router_w"].T, np.zeros(8, np.float32),
        [(2 * c, 2 * c + 1) for c in range(4)])
    moe(2, f["L2_ffn_W1"], f["L2_ffn_b1"], f["L2_ffn_W2"], f["L2_ffn_b2"], f["L2_ffn_Wr"], f["L2_ffn_br"],
        [(c // 2, c // 2) for c in range(16)])
    moe(3, f["L3_ffn_w1"], f["L3_ffn_b1"], f["L3_ffn_w2"], f["L3_ffn_b2"], f["L3_ffn_gate_w"], f["L3_ffn_gate_b"],
        [(c, c) for c in range(16)])
    a["lng"] = dup(f["L2_ffn_ln_g"].T)
    a["lnb"] = f["L2_ffn_ln_b"].T
    for n, l in ((0, "L0"), (3, "L3")):
        a[f"gamma_{n}"] = rep(f[l + "_ffn_gamma"])
        a[f"beta_{n}"] = rep(f[l + "_ffn_beta"])
    a["wqT"], a["wkT"], a["wv"] = f["L1_attn_Wq"].T, f["L1_attn_Wk"].T, f["L1_attn_Wv"]
    a["wkvr"] = dup(np.concatenate([f["L2_attn_Wk"], f["L2_attn_Wv"], f["L2_attn_Wr"]], 1))
    a["mix"] = dup(np.stack([f["L2_attn_time_mix_" + c].reshape(64) for c in "kvr"], 1))
    a["wo"] = f["L2_attn_Wo"]
    tw = f["L2_attn_time_w"]
    toep = np.zeros((128, 128), np.float32)
    for u in range(64):
        for t in range(u, 64):
            toep[u, t] = toep[64 + u, 64 + t] = tw[tw.shape[0] - 1 - (t - u)]
    a["toep"] = toep
    a["qh"] = f["L3_attn_Q"].transpose(1, 0, 2).reshape(64, 512)
    a["eh"] = f["L3_attn_E"].transpose(0, 2, 1).reshape(4, 128, 64).transpose(1, 0, 2)
    return {n: np.ascontiguousarray(v) for n, v in a.items()}


def kernel(**inputs):
    import concourse.bacc as _bacc
    from concourse.bass_utils import run_bass_kernel_spmd as _run

    nc = _bacc.Bacc("TRN2", target_bir_lowering=False, num_devices=1)
    arrays, aps = {}, {}
    for name, v in laid_out(inputs).items():
        arrays["in_" + name] = v
        aps[name] = nc.dram_tensor("in_" + name, v.shape, mybir.dt.from_np(v.dtype), kind="ExternalInput").ap()
    out = nc.dram_tensor("out_0", (NI, NT, D), F32, kind="ExternalOutput").ap()
    build(nc, aps, out)
    r = _run(nc, [arrays], core_ids=[0])
    return r.results[0]["out_0"]
```

```python
import numpy as np
import concourse.bass as bass
from concourse import mybir
from contextlib import ExitStack

F32 = mybir.dt.float32
F32R = mybir.dt.float32r
BF16 = mybir.dt.bfloat16
ALU = mybir.AluOpType
ACT = mybir.ActivationFunctionType
AX = mybir.AxisListType

P = 128
NI = 64
NT = 64
D = 64
NJ = NI * NT // P
NQ = 4
QJ = NJ // NQ
NG = 8
EPS = 1e-5
BIG_NEG = -3.0e38


def build(nc, a, out):
    ctx = ExitStack()
    with ctx:
        def sb(name, shape, dt=F32):
            return ctx.enter_context(nc.sbuf_tensor(name, shape, dt))

        def sem(name):
            return ctx.enter_context(nc.semaphore(name))

        H = sb("H", [P, NJ, D])
        XA = sb("XA", [P, NJ, D])
        LNB = sb("LNB", [P, 2 * NJ, D])
        XC = LNB[:, 0:NJ, :]
        SQ = LNB[:, NJ:2 * NJ, :]
        XT = sb("XT", [P, NI * NT])
        XTR = sb("XTR", [P, NI * NT], F32R)
        BIG = sb("BIG", [P, 16384])
        LNS = sb("LNS", [P, 4, NJ])
        HALFPOW = sb("HALFPOW", [P, QJ])
        RT = BIG[:, 12288:16384].rearrange("p (i j e) -> p i j e", i=8, j=NJ)
        RV = sb("RV", [P, 12, NJ])
        PS = ctx.enter_context(nc.psum_tensor("PS", [P, 8, 512], F32))

        w = {}
        early = ["rowmap", "colmap", "tokW", "tokb", "I", "IU", "bd", "b3", "w0"]
        for name, ap in list(a.items()):
            if name in ("x",) or name.startswith("w1_"):
                continue
            if name == "tokW":
                continue
            if name == "Ib" or name.startswith("sel_"):
                ap = a[name] = ap.bitcast(BF16)
            w[name] = sb("p_" + name, list(ap.shape), ap.dtype)
        WORK = sb("WORK", [P, 2048])
        w["tokW"] = WORK[0:32, :].rearrange("p (o n) -> p o n", o=4)
        W1S = sb("W1S", [P, 2048])
        WH = sb("WH", [P, 2048], F32R)
        WL = sb("WL", [P, 2048], F32R)
        scratch = nc.dram_tensor("h_scratch", (NI, NT, D), F32, kind="Internal").ap()

        s_early, s_late = sem("early_params_loaded"), sem("late_params_loaded")
        n_early, n_late = len(early), len(w) - len(early)
        s_w1 = [sem(f"w1_loaded_{i}") for i in range(4)]
        s_w1free = [sem(f"w1_staging_free_{i}") for i in range(4)]
        s_out = sem("output_stored")

        class Chain:
            def __init__(self, name):
                self.s, self.n = sem(name), 0

            def link(self, eng, ins):
                self.n += 1
                ins.then_inc(self.s, 1)
                eng.wait_ge(self.s, self.n)

        dve_chain, act_chain, pool_chain = Chain("dve_step"), Chain("act_step"), Chain("pool_step")

        LN_SRC = {}
        lns = {x: sem(f"ln_{x}") for x in ("centred", "squared", "var", "rstd", "out")}

        def ln_wait(eng, n, what, quarters):
            eng.wait_ge(lns[what], NQ * n + quarters)

        def q3(t, q):
            return t[:, q * QJ:(q + 1) * QJ, :]

        def bc_j(t, q):
            return t[:, q * QJ:(q + 1) * QJ].unsqueeze(2).broadcast_to([P, QJ, D])

        def ln_dve(v, n, src, dst, ready=lambda q: None, tail=None):
            for q in range(NQ):
                ready(q)
                ins = nc.vector.tensor_reduce(LNS[:, 0, q * QJ:(q + 1) * QJ], q3(src, q), AX.X, ALU.add)
                if q < NQ - 1:
                    ins.then_inc(dve_chain.s, 1)
                    dve_chain.n += 1
                else:
                    dve_chain.link(v, ins)
            dve_chain.link(v, nc.vector.tensor_scalar(LNS[:, 1, :], LNS[:, 0, :], 1.0 / D, None, ALU.mult))
            for q in range(NQ):
                nc.vector.tensor_tensor(q3(XC, q), q3(src, q), bc_j(LNS[:, 1, :], q), ALU.subtract).then_inc(lns["centred"], 1)
            for q in range(NQ):
                ln_wait(v, n, "squared", q + 1)
                nc.vector.tensor_reduce(LNS[:, 2, q * QJ:(q + 1) * QJ], q3(SQ, q), AX.X, ALU.add).then_inc(lns["var"], 1)
            for q in range(NQ):
                ln_wait(v, n, "rstd", q + 1)
                ln_wait(v, n, "centred", q + 1)
                ins = nc.vector.tensor_tensor(q3(dst, q), q3(XC, q), bc_j(LNS[:, 3, :], q), ALU.mult)
                ins.then_inc(lns["out"], 1)

        def ln_act(s, n):
            for q in range(NQ):
                ln_wait(s, n, "centred", q + 1)
                nc.scalar.activation(q3(SQ, q), q3(XC, q), ACT.Square).then_inc(lns["squared"], 1)

        def ln_pool(p, n):
            for q in range(NQ):
                ln_wait(p, n, "var", q + 1)
                r = LNS[:, 3, q * QJ:(q + 1) * QJ]
                pool_chain.link(p, nc.gpsimd.tensor_scalar(r, LNS[:, 2, q * QJ:(q + 1) * QJ], 1.0 / D, EPS, ALU.mult, ALU.add))
                nc.gpsimd.tensor_tensor(r, r, HALFPOW[:, 0:QJ], ALU.pow).then_inc(lns["rstd"], 1)

        UI = 8
        UN = NI // UI
        IMG = BIG[:, 0:4 * UI * 448].rearrange("p (u i c w) -> p u i c w", u=4, i=UI, c=2)
        YS = XT[:, 0:896].rearrange("p (u i w) -> p u i w", u=2, i=2)
        YTS = XT[0:112, 1024:2048].rearrange("p (u i c m) -> p u i c m", u=2, i=2, c=2)
        ZS = XT[0:32, 2048:4096].rearrange("p (b m) -> p b m", b=NI)
        s_img = [sem(f"images_loaded_{i}") for i in range(4)]
        s_rows, s_ys = sem("rows_reduced"), sem("rows_copied")
        s_yt, s_yts = sem("rows_transposed"), sem("transposed_copied")
        s_z, s_zs = sem("maps_done"), sem("maps_copied")
        s_feat, s_h0 = sem("tokens_done"), sem("tokens_in_h")

        def tok_sp(sp):
            x = a["x"].rearrange("b o (p c) w -> p b (o c) w", c=2)
            for u in range(UN):
                if u >= 4:
                    sp.wait_ge(s_rows, u - 3)
                sp.dma_start(IMG[0:112, u % 4], x[:, u * UI:(u + 1) * UI]).then_inc(s_img[u % 4], 16)

        def tok_pe(pe):
            pe.wait_ge(s_early, 16 * n_early)
            for step in range(UN + 2):
                u = step
                if u < UN:
                    pe.wait_ge(s_img[u % 4], 16 * (u // 4 + 1))
                    if u >= 2:
                        pe.wait_ge(s_ys, u - 1)
                    for c in range(2):
                        for g in range(4):
                            ins = nc.tensor.matmul(PS[32 * g:32 * g + 32, u % 2, 0:448], w["rowmap"][:, c, :],
                                                   IMG[0:112, u % 4, 2 * g:2 * g + 2, c, :], start=c == 0, stop=c == 1)
                    ins.then_inc(s_rows, 1)
                u = step - 1
                if 0 <= u < UN:
                    pe.wait_ge(s_ys, u + 1)
                    if u >= 2:
                        pe.wait_ge(s_yts, u - 1)
                    for i in range(2):
                        for c in range(2):
                            o = (2 * i + c) * 128
                            ins = nc.tensor.transpose(PS[0:112, 2 + u % 2, o:o + 128],
                                                      YS[:, u % 2, i, c * 112:c * 112 + 112], w["I"][:, :])
                    ins.then_inc(s_yt, 1)
                u = step - 2
                if 0 <= u < UN:
                    pe.wait_ge(s_yts, u + 1)
                    if u >= 2:
                        pe.wait_ge(s_zs, u - 1)
                    for c in range(2):
                        ins = nc.tensor.matmul(PS[0:32, 4 + u % 2, 0:256], w["colmap"][:, c, :], YTS[:, u % 2, :, c, :],
                                               start=c == 0, stop=c == 1)
                    ins.then_inc(s_z, 1)
            pe.wait_ge(s_zs, UN)
            for r in range(4):
                for o in range(4):
                    for h in range(2):
                        ins = nc.tensor.matmul(PS[64 * h:64 * h + 64, r, :], ZS[:, :, 8 * o + 4 * h + r],
                                               w["tokW"][:, o, :], start=o == 0, stop=o == 3)
                ins.then_inc(s_feat, 1)

        def tok_act(s):
            for u in range(UN):
                s.wait_ge(s_rows, u + 1)
                if u >= 2:
                    s.wait_ge(s_yt, u - 1)
                nc.scalar.copy(YS[:, u % 2], PS[:, u % 2, 0:448].rearrange("p (i w) -> p i w", i=2)).then_inc(s_ys, 1)

        def tok_dve(v):
            def maps(u):
                v.wait_ge(s_z, u + 1)
                src = PS[0:32, 4 + u % 2, 0:256].rearrange("p (i g m) -> p i g m", i=2, g=4)
                dst = ZS[:, u * UI:(u + 1) * UI, :].rearrange("p (g i) m -> p i g m", i=2)
                nc.vector.tensor_copy(dst, src).then_inc(s_zs, 1)

            for u in range(UN):
                v.wait_ge(s_yt, u + 1)
                if u >= 2:
                    v.wait_ge(s_z, u - 1)
                nc.vector.tensor_copy(YTS[:, u % 2], PS[0:112, 2 + u % 2, :].rearrange("p (i c m) -> p i c m", i=2, c=2)
                                      ).then_inc(s_yts, 1)
                if u >= 1:
                    maps(u - 1)
            maps(UN - 1)
            v.wait_ge(s_early, 16 * n_early)
            for r in range(4):
                v.wait_ge(s_feat, r + 1)
                nc.vector.tensor_tensor(q3(H, r), PS[:, r, :].rearrange("p (s e) -> p s e", s=8),
                                        w["tokb"][:, :].unsqueeze(1).broadcast_to([P, 8, D]), ALU.add).then_inc(s_h0, 1)

        NP = NJ
        XCT = BIG[:, 12288:16384].rearrange("p (k m) -> p k m", k=NP)
        U = XT[:, 0:2048].rearrange("p (k i) -> p k i", k=NP)
        QC = XT[:, 2048:4096].rearrange("p (k i) -> p k i", k=NP)
        GATE = BIG[:, :].rearrange("p (u t i) -> p u t i", u=4, t=NI)
        MASK = SQ
        SS = XC
        ST = BIG[:, 0:2048].rearrange("p (k t) -> p k t", k=NP)
        W0S = sb("W0S", [P, 2, 32])
        s_tc, s_tcc = sem("cumulated"), sem("cumulated_copied")
        s_uq, s_uqc = sem("projected"), sem("projected_copied")
        s_preA, s_preB = sem("preact_first"), sem("preact_second")
        s_gate, s_w0 = sem("gates_done"), sem("score_weights_staged")
        s_score = sem("pair_scored")
        s_mask, s_ss = sem("mask_ready"), sem("scores_masked")
        s_st, s_stc = sem("scores_transposed"), sem("scores_t_copied")
        s_att, s_h1 = sem("attended"), sem("attended_in_h")
        s_h1st, s_h1ld = sem("h_stored"), sem("h_loaded")

        def a0_pe(pe):
            for k in range(NP):
                hh, q = k // 16, k // 4
                ln_wait(pe, 0, "out", NQ)
                if k % 4 == 0 and q >= 4:
                    pe.wait_ge(s_tcc, q - 3)
                ins = nc.tensor.matmul(PS[:, 4 + q % 4, (k % 4) * 128:(k % 4) * 128 + 128],
                                       XA[64 * hh:64 * hh + 64, 2 * (k % 16):2 * (k % 16) + 2, :],
                                       w["IU"][64 * hh:64 * hh + 64, :], start=True, stop=True)
                if k % 4 == 3:
                    ins.then_inc(s_tc, 1)
            for q in range(4):
                pe.wait_ge(s_tcc, 2 * q + 2)
                pe.wait_ge(s_h0, 4)
                xi = XCT[:, 8 * q:8 * q + 8, 0:64]
                xc = XCT[:, 8 * q:8 * q + 8, 64:128]
                if q >= 2:
                    pe.wait_ge(s_uqc, 2 * (q - 1))
                nc.tensor.matmul(PS[:, 2 * (q % 2), :], w["bd"][:, 0, :], xi, start=True, stop=True).then_inc(s_uq, 1)
                nc.tensor.matmul(PS[:, 2 * (q % 2) + 1, :], w["bd"][:, 1, :], xi, start=True, stop=False)
                nc.tensor.matmul(PS[:, 2 * (q % 2) + 1, :], w["bd"][:, 2, :], xc, start=False, stop=True).then_inc(s_uq, 1)
            pe.wait_ge(s_uqc, 8)

            def score(k, s, first, last):
                pe.wait_ge(s_w0, k + 1)
                for q in range(4):
                    pe.wait_ge(s_gate, 8 * k + 2 * q + 2)
                    for hh in range(2):
                        for par in range(2):
                            g = 2 * par + hh
                            ni = 16 * (q + 1)
                            ins = nc.tensor.matmul(
                                PS[32 * g:32 * g + 32, q, :].rearrange("p (t i) -> p t i", t=8)[:, :, 0:ni],
                                W0S[:, s, :],
                                GATE[:, 2 * s + hh, 16 * q:16 * q + 16, :].rearrange("p (t r) i -> p t r i", r=2)[:, :, par, 0:ni],
                                start=first, stop=last)
                    ins.then_inc(s_score, 1)

            score(0, 0, True, False)
            score(1, 1, False, False)
            with pe.Fori(1, 7) as kk:
                score(2 * kk, 0, False, False)
                score(2 * kk + 1, 1, False, False)
            score(14, 0, False, False)
            score(15, 1, False, True)
            for b in range(4):
                pe.wait_ge(s_ss, 4)
                for t8 in range(8):
                    t = 8 * b + t8
                    for h in range(2):
                        ins = nc.tensor.matmul(
                            PS[64 * h:64 * h + 64, 4 + b, t8 * 64:t8 * 64 + 64], SS[:, t, :],
                            w["I"][:, :].rearrange("p (r h t) -> p r h t", r=2, h=2)[:, :, h, :], start=True, stop=True)
                ins.then_inc(s_st, 1)
            pe.wait_ge(s_stc, 4)
            for k in range(NP):
                for h in range(2):
                    ins = nc.tensor.matmul(PS[64 * h:64 * h + 64, (k // 8) ^ h, (k % 8) * 64:(k % 8) * 64 + 64],
                                           ST[64 * h:64 * h + 64, k, :], XA[64 * h:64 * h + 64, k, :], start=True, stop=True)
                if k % 16 == 15:
                    ins.then_inc(s_att, 1)

        def a0_act(s):
            for q in range(8):
                s.wait_ge(s_tc, q + 1)
                s.wait_ge(s_rows, UN)
                nc.scalar.copy(XCT[:, 4 * q:4 * q + 4, :], PS[:, 4 + q % 4, :].rearrange("p (k m) -> p k m", k=4)
                               ).then_inc(s_tcc, 1)
            for q in range(4):
                s.wait_ge(s_uq, 2 * q + 1)
                s.wait_ge(s_feat, 4)
                nc.scalar.copy(U[:, 8 * q:8 * q + 8, :], PS[:, 2 * (q % 2), :].rearrange("p (k m) -> p k m", k=8)
                               ).then_inc(s_uqc, 1)
                s.wait_ge(s_uq, 2 * q + 2)
                nc.scalar.activation(QC[:, 8 * q:8 * q + 8, :], PS[:, 2 * (q % 2) + 1, :].rearrange("p (k m) -> p k m", k=8),
                                     ACT.Identity, bias=w["b3"][:, 0:1]).then_inc(s_uqc, 1)

            def gates(k, s_, first):
                if not first:
                    s.wait_ge(s_score, 4 * k - 4)
                nc.scalar.copy(W0S[:, s_, :], w["w0"][:, bass.ds(k, 1), :].rearrange("p o m -> p (o m)")).then_inc(s_w0, 1)
                for q in range(4):
                    ni = 16 * (q + 1)
                    for hh in range(2):
                        if hh == 1 and q >= 2:
                            s.wait_ge(s_preB, 2 * k + q - 1)
                        else:
                            s.wait_ge(s_preA, 6 * k + PRE_ORDER.index((hh, q)) + 1)
                        g = GATE[:, 2 * s_ + hh, 16 * q:16 * q + 16, 0:ni]
                        nc.scalar.activation(g, g, ACT.Sigmoid).then_inc(s_gate, 1)

            gates(0, 0, True)
            gates(1, 1, True)
            with s.Fori(1, 8) as kk:
                gates(2 * kk, 0, False)
                gates(2 * kk + 1, 1, False)
            for b in range(4):
                s.wait_ge(s_st, b + 1)
                src = PS[:, 4 + b, :].rearrange("p (t k) -> p k t", t=16)
                nc.scalar.copy(ST[:, :, 16 * b:16 * b + 16], src).then_inc(s_stc, 1)

        def preact(eng, k, s_, hh, q, signal):
            ni = 16 * (q + 1)
            pair = k + 16 * hh
            u = U[:, bass.ds(pair, 1), 0:ni].broadcast_to([P, 16, ni])
            c = QC[:, bass.ds(pair, 1), 16 * q:16 * q + 16].rearrange("p o t -> p (o t)").unsqueeze(2).broadcast_to([P, 16, ni])
            eng.tensor_tensor(GATE[:, 2 * s_ + hh, 16 * q:16 * q + 16, 0:ni], u, c, ALU.add).then_inc(signal, 1)

        PRE_ORDER = [(0, 0), (1, 0), (0, 1), (1, 1), (0, 2), (0, 3)]

        def a0_dve(v):
            v.wait_ge(s_uqc, 8)

            def pre(k, s_, first):
                for hh, q in PRE_ORDER:
                    if not first and (hh == 0):
                        v.wait_ge(s_score, 4 * k - 8 + q + 1)
                    preact(nc.vector, k, s_, hh, q, s_preA)

            pre(0, 0, True)
            pre(1, 1, True)
            with v.Fori(1, 8) as kk:
                pre(2 * kk, 0, False)
                pre(2 * kk + 1, 1, False)
            v.wait_ge(s_mask, 1)
            v.wait_ge(s_score, 64)
            for q in range(4):
                ni = 16 * (q + 1)
                nc.vector.tensor_tensor(SS[:, 8 * q:8 * q + 8, 0:ni],
                                        PS[:, q, :].rearrange("p (t i) -> p t i", t=8)[:, :, 0:ni],
                                        MASK[:, 8 * q:8 * q + 8, 0:ni], ALU.mult).then_inc(s_ss, 1)
            for r in range(4):
                v.wait_ge(s_att, r // 2 + 1)
                for h in range(2):
                    ins = nc.vector.tensor_tensor(half(q3(H, r), h), half(q3(H, r), h), half(bank3(r ^ h), h), ALU.add)
                ins.then_inc(s_h1, 1)

        def a0_pool(p):
            ln_wait(p, 0, "var", NQ)
            pool_chain.link(p, nc.gpsimd.memset(MASK[:, :, :], 1.0))
            for par in range(2):
                m = MASK[64 * par:64 * par + 64, :, :]
                pool_chain.link(p, nc.gpsimd.affine_select(out=m, in_=m, compare_op=ALU.is_ge, fill=0.0, base=par,
                                                           pattern=[[2, 32], [-1, 64]], channel_multiplier=0))
            ln_wait(p, 0, "out", NQ)
            nc.gpsimd.memset(SS[:, :, :], 0.0).then_inc(s_mask, 1)
            p.wait_ge(s_uqc, 8)

            def pre(k, s_, first):
                for q in range(2, 4):
                    if not first:
                        p.wait_ge(s_score, 4 * k - 8 + q + 1)
                    preact(nc.gpsimd, k, s_, 1, q, s_preB)

            pre(0, 0, True)
            pre(1, 1, True)
            with p.Fori(1, 8) as kk:
                pre(2 * kk, 0, False)
                pre(2 * kk + 1, 1, False)

        def a0_sp(sp):
            sp.wait_ge(s_h1, 4)
            for h in range(2):
                sp.dma_start(scratch[:, 32 * h:32 * h + 32, :], H[64 * h:64 * h + 64, :, :]).then_inc(s_h1st, 16)
            sp.wait_ge(s_h1st, 32)
            src = scratch.rearrange("(j b) t e -> b t j e", b=2)
            for b in range(2):
                sp.dma_start(H[64 * b:64 * b + 64, :, :], src[b]).then_inc(s_h1ld, 16)

        XS = BIG[:, 0:4096].rearrange("p (j c e) -> p j c e", j=NJ, c=2)
        HB = BIG[:, 4096:6144].rearrange("p (u n) -> p u n", u=4)
        HW = BIG[:, 6144:8192].rearrange("p (u n) -> p u n", u=4)
        YE = BIG[:, 8192:8704]
        WS = BIG[:, 8704:9728].bitcast(BF16).rearrange("p (j m) -> p j m", j=NJ)
        WT3 = BIG[:, 10240:12288].bitcast(BF16)
        B2S = sb("B2S", [48, 3, P], BF16)
        SMALL = sb("SMALL", [P, 256])

        moe_sems = {}

        class Moe:

            def __init__(self, n, nch, ne, act, before, pooled=False):
                self.n, self.nch, self.ne, self.act, self.pooled, self.before = n, nch, ne, act, pooled, before
                self.np = nch // 2
                units = NG * nch
                self.steps = dict(split=NQ, xt=NG, xtc=NG, wprep=1, b2prep=1, logits=1, gap=1, tanh=1, wsplit=1,
                                  wt=1 if pooled else NG, wtc=1 if pooled else NG, mm1=units, hact=units, wbc=units,
                                  scaled=units, mm2=units // 2, yevac=NG, ii=NG, comb=NG,
                                  r1=1 if pooled else 0, r2=1 if pooled else NG * (n == 2), r3=2 if pooled else NG * (n == 2),
                                  r4=2 if pooled else 0, r5=1 if pooled else NG * (n == 1), r6=1 if pooled else 0,
                                  lnb=int(n == 2), b1prep=int(n == 2), added=NG * (n == 3), affine=NG * (n == 0),
                                  hsum=NG * (n == 0), hcopy=NG * (n != 3), na_step=4 * NG, na_var=NG, na_rstd=NG, na_out=NG,
                                  nb_step=4 * NG * (n == 0), nb_var=NG * (n == 0), nb_rstd=NG * (n == 0), nb_out=NG * (n == 0))
                for x in self.steps:
                    if x not in moe_sems:
                        moe_sems[x] = sem(f"moe_{x}")

            def __getitem__(self, name):
                return moe_sems[name]

            def value(self, name, count):
                return count + sum(m.steps[name] for m in self.before)

            def wait(self, eng, name, count):
                eng.wait_ge(moe_sems[name], self.value(name, count))

        def split_three(v, src, dst, tmp, part, signal):
            p0 = dst(0)
            dve_chain.link(v, nc.vector.tensor_copy(p0, src))
            dve_chain.link(v, nc.vector.tensor_tensor(tmp, src, p0, ALU.subtract))
            dve_chain.link(v, nc.vector.tensor_copy(dst(1), tmp))
            dve_chain.link(v, nc.vector.tensor_tensor(tmp, tmp, dst(1), ALU.subtract))
            nc.vector.tensor_copy(dst(2), tmp).then_inc(signal, 1)

        def top2(v, M, lg, pp, nj, act_tanh=True):
            E = M.ne
            t = [RT[0:pp, i, 0:nj, 0:E] for i in range(8)]
            r = [RV[0:pp, i, 0:nj] for i in range(12)]
            bc = lambda x: x.unsqueeze(2).broadcast_to([pp, nj, E])
            prio = w["prio"][0:pp, 16 - E:16].unsqueeze(1).broadcast_to([pp, nj, E])
            L = lambda ins: dve_chain.link(v, ins)
            L(nc.vector.tensor_reduce(r[0], lg, AX.X, ALU.max))
            L(nc.vector.tensor_tensor(t[1], lg, bc(r[0]), ALU.is_equal))
            L(nc.vector.tensor_tensor(t[1], t[1], prio, ALU.mult))
            L(nc.vector.tensor_reduce(r[1], t[1], AX.X, ALU.max))
            L(nc.vector.tensor_tensor(t[2], bc(r[1]), prio, ALU.is_equal))
            L(nc.vector.tensor_scalar(t[3], t[2], BIG_NEG, None, ALU.mult))
            L(nc.vector.tensor_tensor(t[3], t[3], lg, ALU.add))
            L(nc.vector.tensor_reduce(r[2], t[3], AX.X, ALU.max))
            nc.vector.tensor_tensor(r[3], r[2], r[0], ALU.subtract).then_inc(M["gap"], 1)
            L(nc.vector.tensor_tensor(t[4], t[3], bc(r[2]), ALU.is_equal))
            L(nc.vector.tensor_tensor(t[4], t[4], prio, ALU.mult))
            L(nc.vector.tensor_reduce(r[4], t[4], AX.X, ALU.max))
            L(nc.vector.tensor_tensor(t[5], bc(r[4]), prio, ALU.is_equal))
            M.wait(v, "tanh", 1)
            L(nc.vector.tensor_scalar(r[6], r[5], 0.5, 0.5, ALU.mult, ALU.add))
            L(nc.vector.tensor_scalar(r[7], r[5], -0.5, 0.5, ALU.mult, ALU.add))
            L(nc.vector.tensor_tensor(t[5], t[5], bc(r[6]), ALU.mult))
            L(nc.vector.tensor_tensor(t[2], t[2], bc(r[7]), ALU.mult))
            L(nc.vector.tensor_tensor(t[6], t[2], t[5], ALU.add))
            return t[6], t[7]

        def moe_act_tanh(s, M, pp, nj):
            M.wait(s, "gap", 1)
            nc.scalar.activation(RV[0:pp, 5, 0:nj], RV[0:pp, 3, 0:nj], ACT.Tanh, scale=0.5).then_inc(M["tanh"], 1)

        def moe_weights(p, M):
            n, nch, E = M.n, M.nch, M.ne
            L = lambda ins: pool_chain.link(p, ins)
            p.wait_ge(s_late, 16 * n_late)
            p.wait_ge(s_w1[n], 16)
            cols = nch * P
            if n > 0:
                moes[n - 1].wait(p, "mm2", NG * moes[n - 1].np)
            if n == 2:
                M.wait(p, "lnb", 1)
                for e in range(E):
                    L(nc.gpsimd.tensor_scalar(W1S[:, e * 256:(e + 1) * 256], W1S[:, e * 256:(e + 1) * 256],
                                              w["lng"][:, e:e + 1], None, ALU.mult))
            L(nc.gpsimd.tensor_copy(WH[:, 0:cols], W1S[:, 0:cols]))
            nc.gpsimd.tensor_tensor(WL[:, 0:cols], W1S[:, 0:cols], WH[:, 0:cols].bitcast(F32), ALU.subtract).then_inc(M["wprep"], 1)
            e3 = 3 * E
            if n == 0:
                L(nc.gpsimd.memset(B2S[:, :, D:P], 0.0))
            src, tmp = w[f"b2_{n}"][0:e3, :], SMALL[0:e3, 0:64]
            L(nc.gpsimd.tensor_copy(B2S[0:e3, 0, 0:D], src))
            L(nc.gpsimd.tensor_tensor(tmp, src, B2S[0:e3, 0, 0:D], ALU.subtract))
            L(nc.gpsimd.tensor_copy(B2S[0:e3, 1, 0:D], tmp))
            L(nc.gpsimd.tensor_tensor(tmp, tmp, B2S[0:e3, 1, 0:D], ALU.subtract))
            nc.gpsimd.tensor_copy(B2S[0:e3, 2, 0:D], tmp).then_inc(M["b2prep"], 1)

        def moe_dve(v, M, n_ln):
            n, nch, E = M.n, M.nch, M.ne
            if n == 2:
                M.wait(v, "lnb", 1)
                nc.vector.tensor_tensor(w["b1_2"][:, :], w["b1_2"][:, :], PS[:, 7, 0:16], ALU.add).then_inc(M["b1prep"], 1)
            for q in range(NQ):
                ln_wait(v, n_ln, "out", q + 1)
                hi = XS[:, q * QJ:(q + 1) * QJ, 0, :]
                dve_chain.link(v, nc.vector.tensor_copy(hi.bitcast(F32R), q3(XN(M), q)))
                nc.vector.tensor_tensor(XS[:, q * QJ:(q + 1) * QJ, 1, :], q3(XN(M), q), hi, ALU.subtract).then_inc(M["split"], 1)
            if M.pooled:
                pooled_dve(v, M)
            else:
                M.wait(v, "logits", 1)
                lg = RT[:, 0, :, 0:E]
                rb = w[f"rb_{n}"][:, :].unsqueeze(1).broadcast_to([P, NJ, E])
                dve_chain.link(v, nc.vector.tensor_tensor(lg, PS[:, 6, 0:NJ * E].rearrange("p (j e) -> p j e", j=NJ), rb, ALU.add))
                wd, tmp = top2(v, M, lg, P, NJ)
                split_three(v, wd, lambda i: WS[:, :, i * E:(i + 1) * E], tmp, P, M["wsplit"])
            moe_main_dve(v, M)

        def XN(M):
            return XC if M.n == 2 else XA

        def pooled_dve(v, M):
            E = M.ne
            L = lambda ins: dve_chain.link(v, ins)
            M.wait(v, "r1", 1)
            nc.vector.tensor_copy(SMALL[0:64, 64:128], PS[0:64, 6, 0:64]).then_inc(M["r2"], 1)
            M.wait(v, "logits", 1)
            lg = RT[0:64, 0, 0, 0:E]
            r = [RV[0:64, i, 0:1] for i in range(8, 12)]
            L(nc.vector.tensor_tensor(lg, PS[0:64, 7, 0:E], w["rb_0"][0:64, :], ALU.add))

            def softmax(x, ex, step):
                L(nc.vector.tensor_reduce(r[0], x, AX.X, ALU.max))
                nc.vector.tensor_scalar(ex, x, r[0], None, ALU.subtract).then_inc(M["r3"], 1)
                M.wait(v, "r4", step)
                L(nc.vector.tensor_reduce(r[1], ex, AX.X, ALU.add))
                L(nc.vector.reciprocal(r[2], r[1]))
                return nc.vector.tensor_scalar(x, ex, r[2], None, ALU.mult)

            softmax(lg, RT[0:64, 1, 0, 0:E], 1).then_inc(M["r5"], 1)
            M.wait(v, "r6", 1)
            sc = RT[0:64, 2, 0, 0:E]
            tokens_per_image = float(NT)
            capacity = float(-(-NI * NT * 5 // (4 * E)))
            L(nc.vector.tensor_scalar(sc, PS[0:64, 5, 0:E], tokens_per_image, None, ALU.mult))
            L(nc.vector.reciprocal(sc, sc))
            L(nc.vector.tensor_scalar(sc, sc, capacity, 1.0, ALU.mult, ALU.min))
            L(nc.vector.tensor_tensor(lg, lg, sc, ALU.mult))
            L(softmax(lg, RT[0:64, 1, 0, 0:E], 2))
            wd, tmp = top2(v, M, RT[0:64, 0, 0:1, 0:E], 64, 1)
            split_three(v, wd, lambda i: WS[0:64, 0:1, i * E:(i + 1) * E], tmp, 64, M["wsplit"])
            M.wait(v, "wt", 1)
            src = PS[0:3 * E, 4, 0:32].bitcast(BF16)
            nc.vector.tensor_copy(WT3[0:3 * E, :].rearrange("p (b t) -> p b t", b=NI),
                                  src.unsqueeze(2).broadcast_to([3 * E, NI, NT])).then_inc(M["wtc"], 1)

        def pooled_act(s, M):
            E = M.ne
            for step in range(2):
                M.wait(s, "r3", step + 1)
                ex = RT[0:64, 1, 0, 0:E]
                nc.scalar.activation(ex, ex, ACT.Exp).then_inc(M["r4"], 1)

        def pooled_pe(pe, M):
            E = M.ne
            for j in range(NJ):
                ins = nc.tensor.matmul(PS[0:64, 6, 2 * j:2 * j + 2], XA[:, j, :], w["pool2"][:, :], start=True, stop=True)
            ins.then_inc(M["r1"], 1)
            M.wait(pe, "r2", 1)
            nc.tensor.matmul(PS[0:64, 7, 0:E], SMALL[0:64, 64:128], w["rw_0"][0:64, :], start=True, stop=True).then_inc(M["logits"], 1)
            M.wait(pe, "r5", 1)
            nc.tensor.matmul(PS[0:64, 5, 0:E], w["ones64"][:, :], RT[0:64, 0, 0, 0:E], start=True, stop=True).then_inc(M["r6"], 1)
            M.wait(pe, "wsplit", 1)
            nc.tensor.transpose(PS[0:3 * E, 4, 0:32].bitcast(BF16), WS[0:64, 0, 0:3 * E], w["Ib"][0:64, 0:64]).then_inc(M["wt"], 1)

        def moe_pe(pe, M):
            n, nch, E = M.n, M.nch, M.ne
            for g in range(NG):
                M.wait(pe, "split", g // 2 + 1)
                if g >= 4:
                    M.wait(pe, "xtc", g - 3)
                for i in range(4):
                    ins = nc.tensor.transpose(PS[:, g % 4, i * P:(i + 1) * P],
                                              XS[:, 4 * g + i, :, :].rearrange("p c e -> p (c e)"), w["I"][:, :])
                ins.then_inc(M["xt"], 1)
            if M.pooled:
                pe.wait_ge(s_late, 16 * n_late)
                pooled_pe(pe, M)
            else:
                route_pe(pe, M)
                M.wait(pe, "wsplit", 1)
                for g in range(NG):
                    if g >= 4:
                        M.wait(pe, "wtc", g - 3)
                    for i in range(4):
                        ins = nc.tensor.transpose(PS[0:3 * E, g % 4, i * 64:(i + 1) * 64].bitcast(BF16), WS[:, 4 * g + i, 0:3 * E],
                                                  w["Ib"][:, :])
                    ins.then_inc(M["wt"], 1)
            moe_main_pe(pe, M)

        def route_pe(pe, M):
            n, E = M.n, M.ne
            if n == 2:
                for g in range(NG):
                    ln_wait(pe, 3, "out", g // 2 + 1)
                    if g < 4:
                        M.wait(pe, "xtc", g + 5)
                    else:
                        M.wait(pe, "r3", g - 3)
                    for i in range(4):
                        ins = nc.tensor.transpose(PS[0:64, g % 4, i * P:(i + 1) * P], XA[:, 4 * g + i, :], w["I"][:, :])
                    ins.then_inc(M["r2"], 1)
                M.wait(pe, "r3", NG)
                xt, k = XT, 64
            else:
                M.wait(pe, "xtc", NG)
                xt, k = XTR, P
            for j in range(NJ):
                lhs = xt[0:k, j * P:(j + 1) * P]
                if n != 2:
                    lhs = lhs.bitcast(F32)
                ins = nc.tensor.matmul(PS[:, 6, j * E:(j + 1) * E], lhs, w[f"rw_{n}"][0:k, :], start=True, stop=True)
            ins.then_inc(M["logits"], 1)

        def moe_act(s, M):
            n, nch, E = M.n, M.nch, M.ne
            for g in range(NG):
                M.wait(s, "xt", g + 1)
                nc.scalar.copy(XTR[:, g * 512:(g + 1) * 512], PS[:, g % 4, :]).then_inc(M["xtc"], 1)
            if M.pooled:
                pooled_act(s, M)
                moe_act_tanh(s, M, 64, 1)
            else:
                if n == 2:
                    for g in range(NG):
                        M.wait(s, "r2", g + 1)
                        nc.scalar.copy(XT[0:64, g * 512:(g + 1) * 512], PS[0:64, g % 4, :]).then_inc(M["r3"], 1)
                moe_act_tanh(s, M, P, NJ)
                for g in range(NG):
                    M.wait(s, "wt", g + 1)
                    src = PS[0:3 * E, g % 4, 0:256].bitcast(BF16)
                    nc.scalar.copy(WT3[0:3 * E, g * 512:(g + 1) * 512], src).then_inc(M["wtc"], 1)
            moe_main_act(s, M)

        ZB, BB, YB, TB = 0, 4, 6, 7

        def moe_main_pe(pe, M):
            n, nch, NPR, e3 = M.n, M.nch, M.np, 3 * M.ne
            M.wait(pe, "wprep", 1)
            M.wait(pe, "b2prep", 1)
            M.wait(pe, "xtc", NG)
            M.wait(pe, "wtc", 1 if M.pooled else NG)
            SEL = w[f"sel_{n}"]
            W2 = w[f"w2_{n}"]

            def up(g, p, first, fresh_banks=False, before_last=lambda: None):
                if not first and not fresh_banks:
                    M.wait(pe, "hact", g * nch + 2 * p - 2)
                for i in range(2):
                    c = 2 * p + i
                    z = PS[:, ZB + c % 4, :]
                    x = XTR[:, bass.ds(g * 512, 512)]
                    nc.tensor.matmul(z, WH[:, c * P:(c + 1) * P], x, start=True, stop=False)
                    if i == 1 and not first:
                        M.wait(pe, "scaled", g * nch + 2 * p)
                        before_last()
                    nc.tensor.matmul(z, WL[:, c * P:(c + 1) * P], x, start=False, stop=True).then_inc(M["mm1"], 1)
                for i in range(2):
                    c = 2 * p + i
                    nc.tensor.matmul(PS[:, BB + i, :], SEL[0:e3, c * P:(c + 1) * P], WT3[0:e3, bass.ds(g * 512, 512)],
                                     start=True, stop=True).then_inc(M["wbc"], 1)

            def down(g, p):
                M.wait(pe, "scaled", g * nch + 2 * p + 2)
                for i in range(2):
                    c = 2 * p + i
                    ins = nc.tensor.matmul(PS[64 * i:64 * i + 64, YB, :], W2[:, c, :], HW[:, c % 4, :],
                                           start=False, stop=(p == NPR - 1), skip_group_check=True)
                ins.then_inc(M["mm2"], 1)

            def group(g, first, last):
                def output_bank_free():
                    if not first:
                        M.wait(pe, "yevac", g)

                for p in range(NPR):
                    if p == 0:
                        up(g, 1, False, first, output_bank_free)
                        for i in range(3):
                            nc.tensor.matmul(PS[:, YB, :], B2S[0:e3, i, :], WT3[0:e3, bass.ds(g * 512, 512)],
                                             start=i == 0, stop=False, skip_group_check=True)
                    elif p < NPR - 1:
                        up(g, p + 1, False)
                    elif not last:
                        up(g + 1, 0, False)
                    down(g, p)
                    if p == 0 and not first:
                        turn_back(g - 1)

            def turn_back(g):
                M.wait(pe, "yevac", g + 1)
                for i in range(4):
                    ins = nc.tensor.matmul(PS[:, TB, i * 64:i * 64 + 64], YE[:, i * P:(i + 1) * P], w["II"][:, :],
                                           start=True, stop=True)
                ins.then_inc(M["ii"], 1)

            up(0, 0, True)
            group(0, True, False)
            with pe.Fori(1, NG - 1) as g:
                group(g, False, False)
            group(NG - 1, False, True)
            turn_back(NG - 1)

        def moe_main_act(s, M):
            n, nch = M.n, M.nch

            def group(g, first):
                for c in range(nch):
                    M.wait(s, "mm1", g * nch + c + 1)
                    if not (first and c < 4):
                        M.wait(s, "scaled", g * nch + c - 3)
                    nc.scalar.activation(HB[:, c % 4, :], PS[:, ZB + c % 4, :], M.act, bias=w[f"b1_{n}"][:, c:c + 1]
                                         ).then_inc(M["hact"], 1)

            if n == 2:
                M.wait(s, "b1prep", 1)
            group(0, True)
            with s.Fori(1, NG) as g:
                group(g, False)

        def moe_main_dve(v, M):
            n, nch, NPR = M.n, M.nch, M.np

            first_norm = Norm(v, M, "na", WORK[:, 0:768], LNS[:, 0:2, 0:12])
            second_norm = Norm(v, M, "nb", WORK[:, 768:1536], LNS[:, 2:4, 0:12])

            take, comb, scale = [("take", 0)], [("combine", 0)], [("scale", 0)]
            a = lambda k: [("stats", k)]
            b = lambda k: [("stats_b", k)]
            if nch == 4:
                plan = {1: take, 3: comb + a(0), 4: a(1) + a(2), 5: a(3) + a(4), 8: scale}
            else:
                plan = {1: take, 3: comb, 4: a(0), 5: a(1), 6: a(2), 7: a(3), 8: a(4), 11: scale}
            if n == 0:
                plan.update({14: [("add", 0)], 15: b(0), 16: b(1), 17: b(2), 18: b(3), 19: b(4), 22: [("scale_b", 0)]})

            def finish(g, c, groups):
                for lag in groups:
                    m = g - lag
                    for what, k in plan.get((lag - 1) * nch + c, []):
                        if what == "take":
                            take_out(m)
                        elif what == "combine":
                            combine(m)
                        elif what == "add":
                            add_to_h(m)
                        elif what == "stats":
                            first_norm.stats(m, k, "comb")
                        elif what == "stats_b":
                            second_norm.stats(m, k, "hsum")
                        elif what == "scale":
                            first_norm.scale(m)
                        else:
                            second_norm.scale(m)

            def group(g, age):
                for c in range(nch):
                    M.wait(v, "hact", g * nch + c + 1)
                    M.wait(v, "wbc", g * nch + c + 1)
                    if not (age == 0 and c < 4) and c % 2 == 0:
                        M.wait(v, "mm2", g * NPR + c // 2 - 1)
                    nc.vector.tensor_tensor(HW[:, c % 4, :], HB[:, c % 4, :], PS[:, BB + c % 2, :], ALU.mult).then_inc(M["scaled"], 1)
                    finish(g, c, [lag for lag in (3, 2, 1) if lag <= age])

            def take_out(g):
                M.wait(v, "mm2", g * NPR + NPR)
                nc.vector.tensor_copy(YE[:, :], PS[:, YB, :]).then_inc(M["yevac"], 1)

            def is_first(g):
                return isinstance(g, int) and g == 0

            def combine(g):
                y = PS[:, TB, 0:256].rearrange("p (j e) -> p j e", j=4)
                hg = H[:, bass.ds(g * 4, 4), :]
                xg = XA[:, bass.ds(g * 4, 4), :]
                if n in (1, 2) and not is_first(g):
                    M.wait(v, "hcopy", g)
                M.wait(v, "ii", g + 1)
                if n in (0, 3):
                    nc.vector.tensor_tensor(first_norm.x, xg, y, ALU.add).then_inc(M["comb"], 1)
                elif n == 1:
                    nc.vector.tensor_tensor(xg, xg, y, ALU.add).then_inc(M["r5"], 1)
                    M.wait(v, "r5", g + 1)
                    nc.vector.tensor_tensor(first_norm.x, hg, xg, ALU.add).then_inc(M["comb"], 1)
                else:
                    nc.vector.tensor_tensor(first_norm.x, hg, y, ALU.add).then_inc(M["comb"], 1)

            def add_to_h(g):
                M.wait(v, "affine", g + 1)
                if not is_first(g):
                    M.wait(v, "hcopy", g)
                hg = H[:, bass.ds(g * 4, 4), :]
                xg = XA[:, bass.ds(g * 4, 4), :]
                nc.vector.tensor_tensor(second_norm.x, hg, xg, ALU.add).then_inc(M["hsum"], 1)

            group(0, 0)
            group(1, 1)
            group(2, 2)
            with v.Fori(3, NG) as g:
                group(g, 3)
            for g in range(NG, NG + 3):
                for c in range(nch):
                    finish(g, c, [lag for lag in (3, 2, 1) if 0 <= g - lag < NG])

        class Norm:

            def __init__(self, v, M, tag, tiles, sums):
                t = tiles.rearrange("p (i j e) -> p i j e", i=3, j=4)
                self.v, self.M, self.tag = v, M, tag
                self.x, self.centred, self.square = (t[:, i] for i in range(3))
                self.sum, self.mean, self.var = (sums[:, 0, 4 * i:4 * i + 4] for i in range(3))
                self.rstd = sums[:, 1, 0:4]

            def bc(self, t):
                return t.unsqueeze(2).broadcast_to([P, 4, D])

            def stats(self, g, k, ready):
                if k == 0:
                    self.M.wait(self.v, ready, g + 1)
                else:
                    self.M.wait(self.v, self.tag + "_step", 4 * g + k)
                if k == 0:
                    ins = nc.vector.tensor_reduce(self.sum, self.x, AX.X, ALU.add)
                elif k == 1:
                    ins = nc.vector.tensor_scalar(self.mean, self.sum, 1.0 / D, None, ALU.mult)
                elif k == 2:
                    ins = nc.vector.tensor_tensor(self.centred, self.x, self.bc(self.mean), ALU.subtract)
                elif k == 3:
                    ins = nc.vector.tensor_tensor(self.square, self.centred, self.centred, ALU.mult)
                else:
                    ins = nc.vector.tensor_reduce(self.var, self.square, AX.X, ALU.add)
                ins.then_inc(self.M[self.tag + ("_step" if k < 4 else "_var")], 1)

            def scale(self, g):
                self.M.wait(self.v, self.tag + "_rstd", g + 1)
                nc.vector.tensor_tensor(XA[:, bass.ds(g * 4, 4), :], self.centred, self.bc(self.rstd), ALU.mult
                                        ).then_inc(self.M[self.tag + "_out"], 1)

        def moe_main_pool(p, M):
            n = M.n
            norms = {"na": Norm(p, M, "na", WORK[:, 0:768], LNS[:, 0:2, 0:12]),
                     "nb": Norm(p, M, "nb", WORK[:, 768:1536], LNS[:, 2:4, 0:12])}

            def rstd(tag, g):
                N = norms[tag]
                M.wait(p, tag + "_var", g + 1)
                pool_chain.link(p, nc.gpsimd.tensor_scalar(N.rstd, N.var, 1.0 / D, EPS, ALU.mult, ALU.add))
                nc.gpsimd.tensor_tensor(N.rstd, N.rstd, HALFPOW[:, 0:4], ALU.pow).then_inc(M[tag + "_rstd"], 1)

            def tiles(t, g):
                return t[:, 4 * g:4 * g + 4, :]

            def affine(g):
                M.wait(p, "na_out", g + 1)
                row = lambda name: w[f"{name}_{n}"][:, :].unsqueeze(1).broadcast_to([P, 4, D])
                pool_chain.link(p, nc.gpsimd.tensor_tensor(tiles(XA, g), tiles(XA, g), row("gamma"), ALU.mult))
                ins = nc.gpsimd.tensor_tensor(tiles(XA, g), tiles(XA, g), row("beta"), ALU.add)
                if n == 0:
                    ins.then_inc(M["affine"], 1)
                else:
                    pool_chain.link(p, ins)
                    nc.gpsimd.tensor_tensor(tiles(H, g), tiles(H, g), tiles(XA, g), ALU.add).then_inc(M["added"], 1)

            def h_from(tag, ready, g):
                M.wait(p, ready, g + 1)
                nc.gpsimd.tensor_copy(tiles(H, g), norms[tag].x).then_inc(M["hcopy"], 1)

            for g in range(NG + 1):
                if n in (0, 3) and g >= 1:
                    affine(g - 1)
                if g < NG:
                    if n in (1, 2):
                        h_from("na", "comb", g)
                    rstd("na", g)
                if n == 0 and g >= 1:
                    h_from("nb", "hsum", g - 1)
                    rstd("nb", g - 1)

        moes = []
        for n_, nch_, ne_, act_ in ((0, 8, 8, ACT.Gelu), (1, 4, 8, ACT.Gelu), (2, 16, 8, ACT.Gelu), (3, 16, 16, ACT.Relu)):
            moes.append(Moe(n_, nch_, ne_, act_, list(moes), pooled=n_ == 0))

        ATT = {1: "aw awc xt xtc gt gtc s v vc exp sub pt ptc norm o oh",
               2: "xt xtc coef s kv rexp kin kexp shift wkv rw rt rtc o oh",
               3: "xt xtc q qc om omc z zc r rc rr oh"}
        att = {n: {x: sem(f"att{n}_{x}") for x in names.split()} for n, names in ATT.items()}

        GT = BIG[0:64, 0:4096]
        PE_ = BIG[:, 4096:6144].rearrange("p (j k) -> p j k", j=NJ)
        PT = BIG[:, 6144:8192].rearrange("p (j k) -> p j k", j=NJ)
        VV = BIG[:, 8192:10240].rearrange("p (j k) -> p j k", j=NJ)
        AW = BIG[0:64, 10240:10304]

        def xt_pe(pe, T, M, normed):
            for g in range(NG):
                M.wait(pe, normed, g + 1)
                if g >= 2:
                    pe.wait_ge(T["xtc"], g - 1)
                for i in range(4):
                    ins = nc.tensor.transpose(PS[0:64, g % 2, i * P:(i + 1) * P], XA[:, 4 * g + i, :], w["I"][:, :])
                ins.then_inc(T["xt"], 1)

        def a1_pe(pe):
            T = att[1]
            pe.wait_ge(s_late, 16 * n_late)
            xt_pe(pe, T, moes[0], "nb_out")
            nc.tensor.matmul(PS[0:64, 7, 0:64], w["wqT"][:, :], w["wkT"][:, :], start=True, stop=True).then_inc(T["aw"], 1)
            pe.wait_ge(T["awc"], 1)
            pe.wait_ge(T["xtc"], NG)
            for g in range(NG):
                if g >= 2:
                    pe.wait_ge(T["gtc"], g - 1)
                nc.tensor.matmul(PS[0:64, 4 + g % 2, :], AW, XT[0:64, g * 512:(g + 1) * 512], start=True, stop=True
                                 ).then_inc(T["gt"], 1)
            for j in range(NJ):
                if j % 8 == 0:
                    pe.wait_ge(T["gtc"], 2 * (j // 8) + 2)
                for b in range(2):
                    c = j * P + b * 64
                    ins = nc.tensor.matmul(PS[64 * b:64 * b + 64, j // 8, (j % 8) * 64:(j % 8) * 64 + 64],
                                           GT[:, c:c + 64], XT[0:64, c:c + 64], start=True, stop=True)
                if j % 8 == 7:
                    ins.then_inc(T["s"], 1)
            for q in range(4):
                pe.wait_ge(T["gtc"], NG)
                for i in range(8):
                    j = 8 * q + i
                    ins = nc.tensor.matmul(PS[:, 4 + q, i * 64:i * 64 + 64], XT[0:64, j * P:(j + 1) * P], w["wv"][:, :],
                                           start=True, stop=True)
                ins.then_inc(T["v"], 1)
            for qq in range(2):
                pe.wait_ge(T["exp"], 2 * qq + 2)
                for j in range(16 * qq, 16 * qq + 16):
                    for b in range(2):
                        ins = nc.tensor.matmul(PS[64 * b:64 * b + 64, (j // 8) ^ b, (j % 8) * 64:(j % 8) * 64 + 64],
                                               PE_[64 * b:64 * b + 64, j, :], w["I"][64 * b:64 * b + 64, 64 * b:64 * b + 64],
                                               start=True, stop=True)
                ins.then_inc(T["pt"], 1)
            for qq in range(2):
                pe.wait_ge(T["ptc"], qq + 1)
                pe.wait_ge(T["vc"], 2 * qq + 2)
                for j in range(16 * qq, 16 * qq + 16):
                    for b in range(2):
                        r = slice(64 * b, 64 * b + 64)
                        ins = nc.tensor.matmul(PS[r, 4 + ((j // 8) ^ b), (j % 8) * 64:(j % 8) * 64 + 64], PT[r, j, :], VV[r, j, :],
                                               start=True, stop=True)
                ins.then_inc(T["o"], 1)

        def a1_act(s):
            T = att[1]
            for g in range(NG):
                s.wait_ge(T["xt"], g + 1)
                nc.scalar.copy(XT[0:64, g * 512:(g + 1) * 512], PS[0:64, g % 2, :]).then_inc(T["xtc"], 1)
            s.wait_ge(T["aw"], 1)
            nc.scalar.mul(AW, PS[0:64, 7, 0:64], float(D) ** -0.5).then_inc(T["awc"], 1)
            for g in range(NG):
                s.wait_ge(T["gt"], g + 1)
                nc.scalar.copy(GT[:, g * 512:(g + 1) * 512], PS[0:64, 4 + g % 2, :]).then_inc(T["gtc"], 1)
            for q in range(4):
                s.wait_ge(T["sub"], q + 1)
                nc.scalar.activation(q3(PE_, q), q3(PE_, q), ACT.Exp).then_inc(T["exp"], 1)
            for q in range(4):
                s.wait_ge(T["v"], q + 1)
                nc.scalar.copy(q3(VV, q), bank3(4 + q)).then_inc(T["vc"], 1)
            for qq in range(2):
                s.wait_ge(T["pt"], qq + 1)
                for q in (2 * qq, 2 * qq + 1):
                    for b in range(2):
                        ins = nc.scalar.copy(half(q3(PT, q), b), half(bank3(q ^ b), b))
                ins.then_inc(T["ptc"], 1)

        def half(t, b):
            return t[64 * b:64 * b + 64]

        def bank3(b):
            return PS[:, b, :].rearrange("p (j e) -> p j e", j=8)

        def a1_dve(v):
            T = att[1]
            moes[0].wait(v, "hcopy", NG)
            for q in range(4):
                v.wait_ge(T["s"], q + 1)
                m = RV[:, 0, 8 * q:8 * q + 8]
                dve_chain.link(v, nc.vector.tensor_reduce(m, bank3(q), AX.X, ALU.max))
                nc.vector.tensor_tensor(q3(PE_, q), bank3(q), bc_j(RV[:, 0, :], q), ALU.subtract).then_inc(T["sub"], 1)
            for q in range(4):
                v.wait_ge(T["exp"], q + 1)
                ins = nc.vector.tensor_reduce(RV[:, 1, 8 * q:8 * q + 8], q3(PE_, q), AX.X, ALU.add)
                dve_chain.link(v, ins)
            dve_chain.link(v, nc.vector.reciprocal(RV[:, 2, :], RV[:, 1, :]))
            for q in range(4):
                v.wait_ge(T["o"], q // 2 + 1)
                for b in range(2):
                    ins = nc.vector.tensor_tensor(half(q3(XC, q), b), half(bank3(4 + (q ^ b)), b), half(bc_j(RV[:, 2, :], q), b), ALU.mult)
                ins.then_inc(T["norm"], 1)
                v.wait_ge(T["norm"], q + 1)
                nc.vector.tensor_tensor(q3(H, q), q3(H, q), q3(XC, q), ALU.add).then_inc(T["oh"], 1)

        KK = BIG[:, 0:2048].rearrange("p (j e) -> p j e", j=NJ)
        KV = BIG[:, 2048:4096].rearrange("p (j e) -> p j e", j=NJ)
        RR = BIG[:, 4096:6144].rearrange("p (j e) -> p j e", j=NJ)
        DN = BIG[:, 6144:8192].rearrange("p (j e) -> p j e", j=NJ)
        RWT = BIG[0:64, 8192:12288]
        XSH = XT

        def a2_pe(pe):
            T = att[2]
            xt_pe(pe, T, moes[1], "na_out")
            pe.wait_ge(s_w1[2], 16)
            pe.wait_ge(s_late, 16 * n_late)
            for c in range(moes[2].nch):
                ins = nc.tensor.matmul(PS[:, 7, c:c + 1], W1S[0:64, c * P:(c + 1) * P], w["lnb"][0:64, c // 2:c // 2 + 1],
                                       start=True, stop=True)
            ins.then_inc(moes[2]["lnb"], 1)
            pe.wait_ge(T["coef"], 3)
            for j in range(NJ):
                if j % 2 == 0:
                    pe.wait_ge(T["xtc"], j // 4 + 1)
                    pe.wait_ge(T["shift"], j // 4 + 1)
                if j >= 4:
                    pe.wait_ge(T["kv"], j - 3)
                    pe.wait_ge(T["rexp"], j - 3)
                nc.tensor.matmul(PS[:, 2 + j % 4, 0:192], XSH[:, j * P:(j + 1) * P], w["wkvr"][:, :], start=True, stop=True
                                 ).then_inc(T["s"], 1)
            for q in range(4):
                pe.wait_ge(T["kv"], NJ)
                pe.wait_ge(T["rexp"], NJ)
                pe.wait_ge(T["xtc"], NG)
                if q >= 2:
                    pe.wait_ge(T["rw"], q - 1)
                nc.tensor.matmul(PS[:, 2 * (q % 2), :], w["cum"][:, :], q3(KK, q), start=True, stop=True)
                nc.tensor.matmul(PS[:, 2 * (q % 2) + 1, :], w["toep"][:, :], q3(KV, q), start=True, stop=True).then_inc(T["wkv"], 1)
            for g in range(NG):
                pe.wait_ge(T["rw"], g // 2 + 1)
                if g >= 2:
                    pe.wait_ge(T["rtc"], g - 1)
                for i in range(4):
                    ins = nc.tensor.transpose(PS[0:64, 4 + g % 2, i * P:(i + 1) * P], RR[:, 4 * g + i, :], w["I"][:, :])
                ins.then_inc(T["rt"], 1)
            for q in range(4):
                pe.wait_ge(T["rtc"], 2 * q + 2)
                pe.wait_ge(T["rw"], 4)
                for i in range(8):
                    j = 8 * q + i
                    ins = nc.tensor.matmul(PS[:, q, i * 64:i * 64 + 64], RWT[:, j * P:(j + 1) * P], w["wo"][:, :], start=True, stop=True)
                ins.then_inc(T["o"], 1)

        def a2_act(s):
            T = att[2]
            for g in range(NG):
                s.wait_ge(T["xt"], g + 1)
                nc.scalar.copy(XSH[0:64, g * 512:(g + 1) * 512], PS[0:64, g % 2, :])
                shifted = XSH[64:128, g * 512:(g + 1) * 512].rearrange("p (b t) -> p b t", b=8)
                src = PS[0:64, g % 2, :].rearrange("p (b t) -> p b t", b=8)
                nc.scalar.copy(shifted[:, :, 1:NT], src[:, :, 0:NT - 1]).then_inc(T["xtc"], 1)
            for j in range(NJ):
                s.wait_ge(T["kin"], j + 1)
                nc.scalar.activation(RR[:, j, :], PS[:, 2 + j % 4, 128:192], ACT.Exp, scale=-1.0).then_inc(T["rexp"], 1)
                s.wait_ge(T["rexp"], j + 1)
                nc.scalar.activation(KK[:, j, :], KK[:, j, :], ACT.Exp).then_inc(T["kexp"], 1)
            for g in range(NG):
                s.wait_ge(T["rt"], g + 1)
                nc.scalar.copy(RWT[:, g * 512:(g + 1) * 512], PS[0:64, 4 + g % 2, :]).then_inc(T["rtc"], 1)

        def a2_dve(v):
            T = att[2]
            v.wait_ge(s_late, 16 * n_late)
            dve_chain.link(v, nc.vector.tensor_scalar(w["mix"][:, :], w["mix"][:, :], w["mixab"][:, 0:1], w["mixab"][:, 1:2],
                                                      ALU.mult, ALU.add))
            for i in range(3):
                nc.vector.tensor_scalar(w["wkvr"][:, 64 * i:64 * i + 64], w["wkvr"][:, 64 * i:64 * i + 64],
                                        w["mix"][:, i:i + 1], None, ALU.mult).then_inc(T["coef"], 1)
            for g in range(NG):
                z = XSH[64:128, g * 512:(g + 1) * 512].rearrange("p (b t) -> p b t", b=8)[:, :, 0:1]
                nc.vector.memset(z, 0.0).then_inc(T["shift"], 1)
            for j in range(NJ + 1):
                if j < NJ:
                    v.wait_ge(T["s"], j + 1)
                    nc.vector.tensor_scalar(KK[:, j, :], PS[:, 2 + j % 4, 0:64], -60.0, 30.0, ALU.max, ALU.min).then_inc(T["kin"], 1)
                if j >= 1:
                    v.wait_ge(T["kexp"], j)
                    nc.vector.tensor_tensor(KV[:, j - 1, :], KK[:, j - 1, :], PS[:, 2 + (j - 1) % 4, 64:128], ALU.mult
                                            ).then_inc(T["kv"], 1)
            v.wait_ge(T["rexp"], NJ)
            moes[1].wait(v, "hcopy", NG)
            for q in range(4):
                v.wait_ge(T["wkv"], q + 1)
                dve_chain.link(v, nc.vector.scalar_tensor_tensor(out=flat(DN, q), in0=flat(RR, q), scalar=1.0, in1=PS[:, 2 * (q % 2), :],
                                                                 op0=ALU.add, op1=ALU.mult))
                dve_chain.link(v, nc.vector.reciprocal(q3(DN, q), q3(DN, q)))
                nc.vector.tensor_tensor(q3(RR, q), q3(DN, q), bank3(2 * (q % 2) + 1), ALU.mult).then_inc(T["rw"], 1)
            for q in range(4):
                v.wait_ge(T["o"], q + 1)
                nc.vector.tensor_tensor(q3(H, q), q3(H, q), bank3(q), ALU.add).then_inc(T["oh"], 1)

        def flat(t, q):
            return q3(t, q).rearrange("p j e -> p (j e)")

        QS = BIG[:, 0:16384].rearrange("p (k n) -> p k n", k=4)
        OMS = WORK[:, 0:1024].rearrange("p (u n) -> p u n", u=2)
        RTT = WORK[:, 1024:2048].rearrange("p (u n) -> p u n", u=2)
        ZT = LNB[:, :, :].rearrange("p (u k j) e -> p u k (j e)", u=2, k=4)

        def a3_pe(pe):
            T = att[3]
            xt_pe(pe, T, moes[2], "na_out")
            for g in range(NG):
                pe.wait_ge(T["xtc"], g + 1)
                for k in range(4):
                    u = g * 4 + k
                    if u >= 2:
                        pe.wait_ge(T["qc"], u - 1)
                    nc.tensor.matmul(PS[:, 2 + u % 2, :], w["qh"][:, k * P:(k + 1) * P], XT[0:64, g * 512:(g + 1) * 512],
                                     start=True, stop=True).then_inc(T["q"], 1)
            pe.wait_ge(T["qc"], 4 * NG)
            for step in range(NJ + 4):
                j = step
                if j < NJ:
                    if j >= 2:
                        pe.wait_ge(T["omc"], j - 1)
                    for par in range(2):
                        for b in range(2):
                            c = j * P + b * 64
                            r = slice(64 * par, 64 * par + 64)
                            o = PS[64 * b:64 * b + 64, 2 * par + j % 2, 0:256].rearrange("p (k t) -> p k t", k=4)
                            ins = nc.tensor.matmul(o, XT[r, c:c + 64], QS[r, :, c:c + 64], start=True, stop=True)
                    ins.then_inc(T["om"], 1)
                j = step - 1
                if 0 <= j < NJ:
                    pe.wait_ge(T["omc"], j + 1)
                    if j >= 1:
                        pe.wait_ge(T["zc"], j)
                    for b in range(2):
                        for par in range(2):
                            r = slice(64 * b, 64 * b + 64)
                            ins = nc.tensor.matmul(PS[64 * par:64 * par + 64, 4 + b, 0:256], XA[r, j, :],
                                                   OMS[r, j % 2, par * 256:par * 256 + 256], start=True, stop=True)
                    ins.then_inc(T["z"], 1)
                j = step - 2
                if 0 <= j < NJ and j % 4 == 3:
                    g = j // 4
                    pe.wait_ge(T["zc"], j + 1)
                    if g >= 1:
                        pe.wait_ge(T["rc"], g)
                    for k in range(4):
                        h = k % 2
                        ins = nc.tensor.matmul(PS[64 * h:64 * h + 64, 6, :], w["eh"][:, k, :], ZT[:, g % 2, k, :], start=k < 2,
                                               stop=k >= 2, skip_group_check=True)
                    ins.then_inc(T["r"], 1)
                j = step - 3
                if 0 <= j < NJ and j % 4 == 3:
                    g = j // 4
                    pe.wait_ge(T["rc"], g + 1)
                    if g >= 1:
                        pe.wait_ge(T["oh"], g)
                    for i in range(4):
                        ins = nc.tensor.matmul(PS[:, 7, i * 64:i * 64 + 64], RTT[:, g % 2, i * P:(i + 1) * P], w["II"][:, :],
                                               start=True, stop=True)
                    ins.then_inc(T["rr"], 1)

        def a3_act(s):
            T = att[3]
            for g in range(NG):
                s.wait_ge(T["xt"], g + 1)
                nc.scalar.copy(XT[0:64, g * 512:(g + 1) * 512], PS[0:64, g % 2, :])
                nc.scalar.copy(XT[64:128, g * 512:(g + 1) * 512], PS[0:64, g % 2, :]).then_inc(T["xtc"], 1)
            for u in range(4 * NG):
                g, k = u // 4, u % 4
                s.wait_ge(T["q"], u + 1)
                nc.scalar.copy(QS[:, k, g * 512:(g + 1) * 512], PS[:, 2 + u % 2, :]).then_inc(T["qc"], 1)
            for j in range(NJ):
                s.wait_ge(T["z"], j + 1)
                g, i = j // 4, j % 4
                if g >= 2 and i == 0:
                    s.wait_ge(T["r"], g - 1)
                for b in range(2):
                    ins = nc.scalar.copy(ZT[:, g % 2, :, i * P + b * 64:i * P + b * 64 + 64],
                                         PS[:, 4 + b, 0:256].rearrange("p (k t) -> p k t", k=4))
                ins.then_inc(T["zc"], 1)

        def a3_dve(v):
            T = att[3]

            def tri_mask(j):
                v.wait_ge(T["om"], j + 1)
                if j == 0:
                    moes[2].wait(v, "hcopy", NG)
                if j >= 2:
                    v.wait_ge(T["z"], j - 1)
                tri = w["tri"][:, :].unsqueeze(1).broadcast_to([P, 4, 64])
                for par in range(2):
                    ins = nc.vector.tensor_tensor(OMS[:, j % 2, par * 256:par * 256 + 256].rearrange("p (k t) -> p k t", k=4),
                                                  PS[:, 2 * par + j % 2, 0:256].rearrange("p (k t) -> p k t", k=4), tri, ALU.mult)
                ins.then_inc(T["omc"], 1)

            for step in range(NJ + 5):
                if step < NJ:
                    tri_mask(step)
                j = step - 2
                if 0 <= j < NJ and j % 4 == 3:
                    g = j // 4
                    v.wait_ge(T["r"], g + 1)
                    if g >= 2:
                        v.wait_ge(T["rr"], g - 1)
                    nc.vector.tensor_copy(RTT[:, g % 2, :], PS[:, 6, :]).then_inc(T["rc"], 1)
                j = step - 4
                if 0 <= j < NJ and j % 4 == 3:
                    g = j // 4
                    v.wait_ge(T["rr"], g + 1)
                    hg = H[:, 4 * g:4 * g + 4, :]
                    nc.vector.tensor_tensor(hg, hg, PS[:, 7, 0:256].rearrange("p (j e) -> p j e", j=4), ALU.add
                                            ).then_inc(T["oh"], 1)

        block = ctx.enter_context(nc.Block())

        @block.sync
        def _(sp):
            tok_sp(sp)
            a0_sp(sp)
            for i in (1, 2, 3):
                moes[i - 1].wait(sp, "wprep", 1)
                cols = moes[i].nch * P
                sp.dma_start(W1S[:, 0:cols], a[f"w1_{i}"]).then_inc(s_w1[i], 16)
            dst = out.rearrange("(j b) t e -> b t j e", b=2)
            moes[3].wait(sp, "added", NG)
            for b in range(2):
                sp.dma_start(dst[b], H[64 * b:64 * b + 64, :, :]).then_inc(s_out, 16)
            sp.wait_ge(s_out, 32)

        @block.scalar
        def _(s):
            for name in early:
                s.dma_start(w[name][:], a[name]).then_inc(s_early, 16)
            tok_act(s)
            s.wait_ge(s_early, 16 * n_early)
            ln_act(s, 0)
            a0_act(s)
            ln_act(s, 1)
            moe_act(s, moes[0])
            a1_act(s)
            s.wait_ge(s_late, 16 * n_late)
            ln_act(s, 2)
            moe_act(s, moes[1])
            a2_act(s)
            ln_act(s, 3)
            ln_act(s, 4)
            moe_act(s, moes[2])
            a3_act(s)
            ln_act(s, 5)
            moe_act(s, moes[3])

        @block.gpsimd
        def _(p):
            late = [k for k in w if k not in early]
            for name in late:
                p.dma_start(w[name][:], a[name]).then_inc(s_late, 16)
            p.dma_start(W1S[:, 0:moes[0].nch * P], a["w1_0"]).then_inc(s_w1[0], 16)
            pool_chain.link(p, nc.gpsimd.memset(HALFPOW[:, :], -0.5))
            moe_weights(p, moes[0])
            ln_pool(p, 0)
            a0_pool(p)
            ln_pool(p, 1)
            moe_main_pool(p, moes[0])
            moe_weights(p, moes[1])
            ln_pool(p, 2)
            moe_main_pool(p, moes[1])
            moe_weights(p, moes[2])
            ln_pool(p, 3)
            ln_pool(p, 4)
            moe_main_pool(p, moes[2])
            moe_weights(p, moes[3])
            ln_pool(p, 5)
            moe_main_pool(p, moes[3])

        @block.vector
        def _(v):
            tok_dve(v)
            ln_dve(v, 0, H, XA, lambda q: v.wait_ge(s_h0, q + 1))
            a0_dve(v)
            ln_dve(v, 1, H, XA, lambda q: v.wait_ge(s_h1ld, 32))
            moe_dve(v, moes[0], 1)
            a1_dve(v)
            ln_dve(v, 2, H, XA, lambda q: v.wait_ge(att[1]["oh"], q + 1))
            moe_dve(v, moes[1], 2)
            a2_dve(v)
            ln_dve(v, 3, H, XA, lambda q: v.wait_ge(att[2]["oh"], q + 1))
            ln_dve(v, 4, XA, XC, lambda q: ln_wait(v, 3, "out", NQ))
            moe_dve(v, moes[2], 4)
            a3_dve(v)
            ln_dve(v, 5, H, XA, lambda q: v.wait_ge(att[3]["oh"], NG))
            moe_dve(v, moes[3], 5)

        @block.tensor
        def _(pe):
            tok_pe(pe)
            a0_pe(pe)
            moe_pe(pe, moes[0])
            a1_pe(pe)
            moe_pe(pe, moes[1])
            a2_pe(pe)
            moe_pe(pe, moes[2])
            a3_pe(pe)
            moe_pe(pe, moes[3])


def resize_matrix(n, m=8):
    scale = n / m
    centre = (np.arange(m) + 0.5) * scale - 0.5
    t = np.maximum(0, 1 - np.abs(centre[:, None] - np.arange(n)[None]) / scale)
    return t / t.sum(1, keepdims=True)


def haar(n):
    lo, hi = np.zeros((n // 2, n)), np.zeros((n // 2, n))
    i = np.arange(n // 2)
    c = 0.7071067811865476
    lo[i, 2 * i] = lo[i, 2 * i + 1] = hi[i, 2 * i] = c
    hi[i, 2 * i + 1] = -c
    return lo, hi


def constants():
    lo1, hi1 = haar(224)
    lo2, hi2 = haar(112)
    r56, r112 = resize_matrix(56), resize_matrix(112)
    maps = np.concatenate([r56 @ lo2 @ lo1, r56 @ hi2 @ lo1, r112 @ lo1, r112 @ hi1])
    k = {}
    k["rowmap"] = maps.T.reshape(112, 2, 32)
    k["colmap"] = maps.T.reshape(2, 112, 32).transpose(1, 0, 2)
    eye, up = np.eye(128), np.triu(np.ones((64, 64)))
    k["I"] = eye
    k["IU"] = np.tile(np.concatenate([np.eye(64), up], 1), (2, 1))
    k["II"] = np.tile(np.eye(64), (2, 1))
    k["pool2"] = np.kron(np.eye(2), np.ones((64, 1))) / NT
    k["ones64"] = np.ones((64, 64))
    k["prio"] = np.tile(np.arange(16, 0, -1.0), (128, 1))
    k["cum"] = np.kron(np.eye(2), up)
    k["tri"] = np.tile(up, (2, 1))
    k["mixab"] = np.concatenate([np.tile([[1.0, 0.0]], (64, 1)), np.tile([[-1.0, 1.0]], (64, 1))])
    return {n: np.ascontiguousarray(v, np.float32) for n, v in k.items()}


def selectors(chunk_expert, ne):
    s = np.zeros((3 * ne, len(chunk_expert), 128), np.float32)
    for c, es in enumerate(chunk_expert):
        for half, e in enumerate(es):
            for part in range(3):
                s[part * ne + e, c, 64 * half:64 * half + 64] = 1
    return s.reshape(3 * ne, -1)


def bf16_bits(zeros_and_ones):
    return (zeros_and_ones != 0).astype(np.uint16) * np.uint16(0x3F80)


def laid_out(i):
    f = {k: np.asarray(v) for k, v in i.items()}
    a = {"x": f["x"]}
    a.update(constants())
    a["Ib"] = bf16_bits(np.eye(128))
    rep = lambda v, n=128: np.tile(v.reshape(1, -1), (n, 1))
    ops = [(0, 0), (1, 0), (0, 1), (1, 1), (3, 2), (2, 3), (3, 3)]
    tw = np.zeros((4, 8, 4, 8, 64), np.float32)
    for m, (ro, co) in enumerate(ops):
        for s in range(8):
            tw[co, s, ro, s, :] = f["L0_tok_W"][m]
    a["tokW"] = tw.reshape(32, 4, 512)
    a["tokb"] = rep(f["L0_tok_b"])
    bd = np.zeros((128, 3, 128), np.float32)
    for n, name in enumerate(("L0_attn_w1", "L0_attn_w2", "L0_attn_w3")):
        bd[:64, n, :64] = bd[64:, n, 64:] = f[name].T
    a["bd"] = bd
    a["b3"] = np.tile(f["L0_attn_b3"].reshape(-1, 1), (2, 1))
    w0 = np.zeros((128, 16, 32), np.float32)
    for k in range(16):
        w0[:64, k, 2 * k] = w0[64:, k, 2 * k + 1] = f["L0_attn_w0"]
    a["w0"] = w0
    dup = lambda v: np.concatenate([v, v], 0)

    def moe(n, w1, b1, w2, b2, rw, rb, chunk_expert):
        ne = w1.shape[0]
        nch = len(chunk_expert)
        a[f"w1_{n}"] = dup(w1.transpose(1, 0, 2).reshape(64, -1))
        a[f"b1_{n}"] = b1.reshape(nch, 128).T
        a[f"w2_{n}"] = w2.reshape(nch, 128, 64).transpose(1, 0, 2)
        a[f"b2_{n}"] = np.tile(b2, (3, 1))
        a[f"rw_{n}"] = dup(rw)
        a[f"rb_{n}"] = rep(rb)
        a[f"sel_{n}"] = bf16_bits(selectors(chunk_expert, ne))

    moe(0, f["L0_ffn_W1"], f["L0_ffn_b1"], f["L0_ffn_W2"], f["L0_ffn_b2"], f["L0_ffn_Wr"], f["L0_ffn_br"],
        [(e, e) for e in range(8)])
    moe(1, f["L1_ffn_w1"], f["L1_ffn_b1"], f["L1_ffn_w2"], f["L1_ffn_b2"], f["L1_ffn_router_w"].T, np.zeros(8, np.float32),
        [(2 * c, 2 * c + 1) for c in range(4)])
    moe(2, f["L2_ffn_W1"], f["L2_ffn_b1"], f["L2_ffn_W2"], f["L2_ffn_b2"], f["L2_ffn_Wr"], f["L2_ffn_br"],
        [(c // 2, c // 2) for c in range(16)])
    moe(3, f["L3_ffn_w1"], f["L3_ffn_b1"], f["L3_ffn_w2"], f["L3_ffn_b2"], f["L3_ffn_gate_w"], f["L3_ffn_gate_b"],
        [(c, c) for c in range(16)])
    a["lng"] = dup(f["L2_ffn_ln_g"].T)
    a["lnb"] = f["L2_ffn_ln_b"].T
    for n, l in ((0, "L0"), (3, "L3")):
        a[f"gamma_{n}"] = rep(f[l + "_ffn_gamma"])
        a[f"beta_{n}"] = rep(f[l + "_ffn_beta"])
    a["wqT"], a["wkT"], a["wv"] = f["L1_attn_Wq"].T, f["L1_attn_Wk"].T, f["L1_attn_Wv"]
    a["wkvr"] = dup(np.concatenate([f["L2_attn_Wk"], f["L2_attn_Wv"], f["L2_attn_Wr"]], 1))
    a["mix"] = dup(np.stack([f["L2_attn_time_mix_" + c].reshape(64) for c in "kvr"], 1))
    a["wo"] = f["L2_attn_Wo"]
    tw = f["L2_attn_time_w"]
    toep = np.zeros((128, 128), np.float32)
    for u in range(64):
        for t in range(u, 64):
            toep[u, t] = toep[64 + u, 64 + t] = tw[tw.shape[0] - 1 - (t - u)]
    a["toep"] = toep
    a["qh"] = f["L3_attn_Q"].transpose(1, 0, 2).reshape(64, 512)
    a["eh"] = f["L3_attn_E"].transpose(0, 2, 1).reshape(4, 128, 64).transpose(1, 0, 2)
    return {n: np.ascontiguousarray(v) for n, v in a.items()}


def kernel(**inputs):
    import concourse.bacc as _bacc
    from concourse.bass_utils import run_bass_kernel_spmd as _run

    nc = _bacc.Bacc("TRN2", target_bir_lowering=False, num_devices=1)
    arrays, aps = {}, {}
    for name, v in laid_out(inputs).items():
        arrays["in_" + name] = v
        aps[name] = nc.dram_tensor("in_" + name, v.shape, mybir.dt.from_np(v.dtype), kind="ExternalInput").ap()
    out = nc.dram_tensor("out_0", (NI, NT, D), F32, kind="ExternalOutput").ap()
    build(nc, aps, out)
    r = _run(nc, [arrays], core_ids=[0])
    return r.results[0]["out_0"]
```

```python
import numpy as np
import concourse.bass as bass
from concourse import mybir
from contextlib import ExitStack

F32 = mybir.dt.float32
F32R = mybir.dt.float32r
BF16 = mybir.dt.bfloat16
ALU = mybir.AluOpType
ACT = mybir.ActivationFunctionType
AX = mybir.AxisListType

P = 128
NI = 64
NT = 64
D = 64
NJ = NI * NT // P
NQ = 4
QJ = NJ // NQ
HJ = NJ // 2
NG = 8
EPS = 1e-5
BIG_NEG = -3.0e38


def build(nc, a, out):
    ctx = ExitStack()
    with ctx:
        def sb(name, shape, dt=F32):
            return ctx.enter_context(nc.sbuf_tensor(name, shape, dt))

        def sem(name):
            return ctx.enter_context(nc.semaphore(name))

        H = sb("H", [P, NJ, D])
        XA = sb("XA", [P, NJ, D])
        LNB = sb("LNB", [P, 2 * NJ, D])
        XC = LNB[:, 0:NJ, :]
        SQ = LNB[:, NJ:2 * NJ, :]
        XT = sb("XT", [P, NI * NT])
        XTR = sb("XTR", [P, NI * NT], F32R)
        BIG = sb("BIG", [P, 16384])
        LNS = sb("LNS", [P, 4, NJ])
        HALFPOW = sb("HALFPOW", [P, QJ])
        RT = BIG[:, 12288:16384].rearrange("p (i j e) -> p i j e", i=8, j=NJ)
        RV = sb("RV", [P, 12, NJ])
        PS = ctx.enter_context(nc.psum_tensor("PS", [P, 8, 512], F32))

        w = {}
        maps = ["rowmap", "colmap", "I"]
        early = ["tokW", "tokb", "IU", "bd", "b3", "w0"]
        for name, ap in list(a.items()):
            if name in ("x",) or name.startswith("w1_"):
                continue
            if name == "tokW":
                continue
            if name == "Ib" or name.startswith("sel_"):
                ap = a[name] = ap.bitcast(BF16)
            w[name] = sb("p_" + name, list(ap.shape), ap.dtype)
        WORK = sb("WORK", [P, 2048])
        w["tokW"] = WORK[0:32, :].rearrange("p (o n) -> p o n", o=4)
        W1S = sb("W1S", [P, 2048])
        WH = sb("WH", [P, 2048], F32R)
        WL = sb("WL", [P, 2048], F32R)
        scratch = nc.dram_tensor("h_scratch", (NI, NT, D), F32, kind="Internal").ap()

        s_maps, s_early, s_late = sem("maps_loaded"), sem("early_params_loaded"), sem("late_params_loaded")
        n_maps, n_early, n_late = len(maps), len(early), len(w) - len(early) - len(maps)
        s_w1 = [sem(f"w1_loaded_{i}") for i in range(4)]
        s_w1free = [sem(f"w1_staging_free_{i}") for i in range(4)]
        s_out = sem("output_stored")

        class Chain:
            def __init__(self, name):
                self.s, self.n = sem(name), 0

            def link(self, eng, ins):
                self.n += 1
                ins.then_inc(self.s, 1)
                eng.wait_ge(self.s, self.n)

        dve_chain, pool_chain = Chain("dve_step"), Chain("pool_step")

        lns = {x: sem(f"ln_{x}") for x in ("sum", "mean", "centred", "squared", "var", "rstd", "out")}

        def ln_wait(eng, n, what, quarters):
            eng.wait_ge(lns[what], NQ * n + quarters)

        def q3(t, q):
            return t[:, q * QJ:(q + 1) * QJ, :]

        def bc_j(t, q):
            return t[:, q * QJ:(q + 1) * QJ].unsqueeze(2).broadcast_to([P, QJ, D])

        def ln_dve(v, n, src, dst, ready=lambda q: None, behind=lambda q: None):
            for step in range(NQ + 3):
                if step < NQ:
                    q = step
                    ready(q)
                    nc.vector.tensor_reduce(LNS[:, 0, q * QJ:(q + 1) * QJ], q3(src, q), AX.X, ALU.add).then_inc(lns["sum"], 1)
                if 0 <= step - 1 < NQ:
                    q = step - 1
                    ln_wait(v, n, "squared", q + 1)
                    nc.vector.tensor_reduce(LNS[:, 2, q * QJ:(q + 1) * QJ], q3(SQ, q), AX.X, ALU.add).then_inc(lns["var"], 1)
                if step < NQ:
                    q = step
                    ln_wait(v, n, "sum", q + 1)
                    nc.vector.tensor_scalar(LNS[:, 1, q * QJ:(q + 1) * QJ], LNS[:, 0, q * QJ:(q + 1) * QJ], 1.0 / D, None, ALU.mult
                                            ).then_inc(lns["mean"], 1)
                    ln_wait(v, n, "mean", q + 1)
                    nc.vector.tensor_tensor(q3(XC, q), q3(src, q), bc_j(LNS[:, 1, :], q), ALU.subtract).then_inc(lns["centred"], 1)
                if 0 <= step - 2 < NQ:
                    q = step - 2
                    ln_wait(v, n, "rstd", q + 1)
                    ln_wait(v, n, "centred", q + 1)
                    nc.vector.tensor_tensor(q3(dst, q), q3(XC, q), bc_j(LNS[:, 3, :], q), ALU.mult).then_inc(lns["out"], 1)
                if 0 <= step - 3 < NQ:
                    behind(step - 3)

        def ln_act(s, n, behind=lambda q: None):
            for step in range(NQ + 2):
                if step < NQ:
                    ln_wait(s, n, "centred", step + 1)
                    nc.scalar.activation(q3(SQ, step), q3(XC, step), ACT.Square).then_inc(lns["squared"], 1)
                if 0 <= step - 2 < NQ:
                    behind(step - 2)

        def ln_pool(p, n):
            for q in range(NQ):
                ln_wait(p, n, "var", q + 1)
                r = LNS[:, 3, q * QJ:(q + 1) * QJ]
                pool_chain.link(p, nc.gpsimd.tensor_scalar(r, LNS[:, 2, q * QJ:(q + 1) * QJ], 1.0 / D, EPS, ALU.mult, ALU.add))
                nc.gpsimd.tensor_tensor(r, r, HALFPOW[:, 0:QJ], ALU.pow).then_inc(lns["rstd"], 1)

        UI = 8
        UN = NI // UI
        IMG = BIG[:, 0:4 * UI * 448].rearrange("p (u i c w) -> p u i c w", u=4, i=UI, c=2)
        YS = XT[:, 0:896].rearrange("p (u i w) -> p u i w", u=2, i=2)
        YTS = XT[0:112, 1024:2048].rearrange("p (u i c m) -> p u i c m", u=2, i=2, c=2)
        ZS = XT[0:32, 2048:4096].rearrange("p (b m) -> p b m", b=NI)
        s_img = [sem(f"images_loaded_{i}") for i in range(4)]
        s_rows, s_ys = sem("rows_reduced"), sem("rows_copied")
        s_yt, s_yts = sem("rows_transposed"), sem("transposed_copied")
        s_z, s_zs = sem("maps_done"), sem("maps_copied")
        s_feat, s_h0 = sem("tokens_done"), sem("tokens_in_h")

        def tok_sp(sp):
            x = a["x"].rearrange("b o (p c) w -> p b (o c) w", c=2)
            for u in range(UN):
                if u >= 4:
                    sp.wait_ge(s_rows, u - 3)
                sp.dma_start(IMG[0:112, u % 4], x[:, u * UI:(u + 1) * UI]).then_inc(s_img[u % 4], 16)

        def tok_pe(pe):
            pe.wait_ge(s_maps, 16 * n_maps)
            for step in range(UN + 2):
                u = step
                if u < UN:
                    pe.wait_ge(s_img[u % 4], 16 * (u // 4 + 1))
                    if u >= 2:
                        pe.wait_ge(s_ys, u - 1)
                    for c in range(2):
                        for g in range(4):
                            ins = nc.tensor.matmul(PS[32 * g:32 * g + 32, u % 2, 0:448], w["rowmap"][:, c, :],
                                                   IMG[0:112, u % 4, 2 * g:2 * g + 2, c, :], start=c == 0, stop=c == 1)
                    ins.then_inc(s_rows, 1)
                u = step - 1
                if 0 <= u < UN:
                    pe.wait_ge(s_ys, u + 1)
                    if u >= 2:
                        pe.wait_ge(s_yts, u - 1)
                    for i in range(2):
                        for c in range(2):
                            o = (2 * i + c) * 128
                            ins = nc.tensor.transpose(PS[0:112, 2 + u % 2, o:o + 128],
                                                      YS[:, u % 2, i, c * 112:c * 112 + 112], w["I"][:, :])
                    ins.then_inc(s_yt, 1)
                u = step - 2
                if 0 <= u < UN:
                    pe.wait_ge(s_yts, u + 1)
                    if u >= 2:
                        pe.wait_ge(s_zs, u - 1)
                    for c in range(2):
                        ins = nc.tensor.matmul(PS[0:32, 4 + u % 2, 0:256], w["colmap"][:, c, :], YTS[:, u % 2, :, c, :],
                                               start=c == 0, stop=c == 1)
                    ins.then_inc(s_z, 1)
            pe.wait_ge(s_early, 16 * n_early)
            pe.wait_ge(s_zs, UN)
            for r in range(4):
                for o in range(4):
                    for h in range(2):
                        ins = nc.tensor.matmul(PS[64 * h:64 * h + 64, r, :], ZS[:, :, 8 * o + 4 * h + r],
                                               w["tokW"][:, o, :], start=o == 0, stop=o == 3)
                ins.then_inc(s_feat, 1)

        def tok_act(s):
            for u in range(UN):
                s.wait_ge(s_rows, u + 1)
                if u >= 2:
                    s.wait_ge(s_yt, u - 1)
                nc.scalar.copy(YS[:, u % 2], PS[:, u % 2, 0:448].rearrange("p (i w) -> p i w", i=2)).then_inc(s_ys, 1)

        def tok_dve(v):
            def maps(u):
                v.wait_ge(s_z, u + 1)
                src = PS[0:32, 4 + u % 2, 0:256].rearrange("p (i g m) -> p i g m", i=2, g=4)
                dst = ZS[:, u * UI:(u + 1) * UI, :].rearrange("p (g i) m -> p i g m", i=2)
                nc.vector.tensor_copy(dst, src).then_inc(s_zs, 1)

            for u in range(UN):
                v.wait_ge(s_yt, u + 1)
                if u >= 2:
                    v.wait_ge(s_z, u - 1)
                nc.vector.tensor_copy(YTS[:, u % 2], PS[0:112, 2 + u % 2, :].rearrange("p (i c m) -> p i c m", i=2, c=2)
                                      ).then_inc(s_yts, 1)
                if u >= 1:
                    maps(u - 1)
            maps(UN - 1)
            v.wait_ge(s_early, 16 * n_early)
            for r in range(4):
                v.wait_ge(s_feat, r + 1)
                nc.vector.tensor_tensor(q3(H, r), PS[:, r, :].rearrange("p (s e) -> p s e", s=8),
                                        w["tokb"][:, :].unsqueeze(1).broadcast_to([P, 8, D]), ALU.add).then_inc(s_h0, 1)

        NP = NJ
        XCT = BIG[:, 12288:16384].rearrange("p (k m) -> p k m", k=NP)
        U = XT[:, 0:2048].rearrange("p (k i) -> p k i", k=NP)
        QC = XT[:, 2048:4096].rearrange("p (k i) -> p k i", k=NP)
        GATE = BIG[:, :].rearrange("p (u t i) -> p u t i", u=4, t=NI)
        MASK = SQ
        SS = XC
        ST = BIG[:, 0:2048].rearrange("p (k t) -> p k t", k=NP)
        W0S = sb("W0S", [P, 2, 32])
        s_tc, s_tcc = sem("cumulated"), sem("cumulated_copied")
        s_uq, s_uqc = sem("projected"), sem("projected_copied")
        s_preA, s_preB = sem("preact_first"), sem("preact_second")
        s_gate, s_w0 = sem("gates_done"), sem("score_weights_staged")
        s_score = sem("pair_scored")
        s_mask, s_ss = sem("mask_ready"), sem("scores_masked")
        s_st, s_stc = sem("scores_transposed"), sem("scores_t_copied")
        s_att, s_h1 = sem("attended"), sem("attended_in_h")
        s_h1st, s_h1ld = sem("h_stored"), [sem(f"h_loaded_{i}") for i in range(2)]

        def a0_pe(pe):
            for k in range(NP):
                hh, q = k // 16, k // 4
                if k % 4 == 0:
                    ln_wait(pe, 0, "out", q % 4 + 1)
                if k % 4 == 0 and q >= 4:
                    pe.wait_ge(s_tcc, q - 3)
                ins = nc.tensor.matmul(PS[:, 4 + q % 4, (k % 4) * 128:(k % 4) * 128 + 128],
                                       XA[64 * hh:64 * hh + 64, 2 * (k % 16):2 * (k % 16) + 2, :],
                                       w["IU"][64 * hh:64 * hh + 64, :], start=True, stop=True)
                if k % 4 == 3:
                    ins.then_inc(s_tc, 1)
            for i, q in enumerate(PROJ_ORDER):
                pe.wait_ge(s_tcc, 2 * q + 2)
                pe.wait_ge(s_h0, 4)
                xi = XCT[:, 8 * q:8 * q + 8, 0:64]
                xc = XCT[:, 8 * q:8 * q + 8, 64:128]
                if i >= 2:
                    pe.wait_ge(s_uqc, 2 * (i - 1))
                nc.tensor.matmul(PS[:, 2 * (i % 2), :], w["bd"][:, 0, :], xi, start=True, stop=True).then_inc(s_uq, 1)
                nc.tensor.matmul(PS[:, 2 * (i % 2) + 1, :], w["bd"][:, 1, :], xi, start=True, stop=False)
                nc.tensor.matmul(PS[:, 2 * (i % 2) + 1, :], w["bd"][:, 2, :], xc, start=False, stop=True).then_inc(s_uq, 1)
            pe.wait_ge(s_uqc, 8)

            def score(k, s, first, last):
                pe.wait_ge(s_w0, k + 1)
                for q in range(4):
                    pe.wait_ge(s_gate, 8 * k + 2 * q + 2)
                    for hh in range(2):
                        for par in range(2):
                            g = 2 * par + hh
                            ni = 16 * (q + 1)
                            ins = nc.tensor.matmul(
                                PS[32 * g:32 * g + 32, q, :].rearrange("p (t i) -> p t i", t=8)[:, :, 0:ni],
                                W0S[:, s, :],
                                GATE[:, 2 * s + hh, 16 * q:16 * q + 16, :].rearrange("p (t r) i -> p t r i", r=2)[:, :, par, 0:ni],
                                start=first, stop=last)
                    ins.then_inc(s_score, 1)

            score(0, 0, True, False)
            score(1, 1, False, False)
            with pe.Fori(1, 7) as kk:
                score(2 * kk, 0, False, False)
                score(2 * kk + 1, 1, False, False)
            score(14, 0, False, False)
            score(15, 1, False, True)
            for b in range(4):
                pe.wait_ge(s_ss, b + 1)
                for t8 in range(8):
                    t = 8 * b + t8
                    for h in range(2):
                        ins = nc.tensor.matmul(
                            PS[64 * h:64 * h + 64, 4 + b, t8 * 64:t8 * 64 + 64], SS[:, t, :],
                            w["I"][:, :].rearrange("p (r h t) -> p r h t", r=2, h=2)[:, :, h, :], start=True, stop=True)
                ins.then_inc(s_st, 1)
            pe.wait_ge(s_stc, 4)
            for k in range(NP):
                for h in range(2):
                    ins = nc.tensor.matmul(PS[64 * h:64 * h + 64, (k // 8) ^ h, (k % 8) * 64:(k % 8) * 64 + 64],
                                           ST[64 * h:64 * h + 64, k, :], XA[64 * h:64 * h + 64, k, :], start=True, stop=True)
                if k % 16 == 15:
                    ins.then_inc(s_att, 1)

        def a0_act(s):
            for q in range(8):
                s.wait_ge(s_tc, q + 1)
                s.wait_ge(s_rows, UN)
                nc.scalar.copy(XCT[:, 4 * q:4 * q + 4, :], PS[:, 4 + q % 4, :].rearrange("p (k m) -> p k m", k=4)
                               ).then_inc(s_tcc, 1)
            for i, q in enumerate(PROJ_ORDER):
                s.wait_ge(s_uq, 2 * i + 1)
                s.wait_ge(s_feat, 4)
                nc.scalar.copy(U[:, 8 * q:8 * q + 8, :], PS[:, 2 * (i % 2), :].rearrange("p (k m) -> p k m", k=8)
                               ).then_inc(s_uqc, 1)
                s.wait_ge(s_uq, 2 * i + 2)
                nc.scalar.activation(QC[:, 8 * q:8 * q + 8, :], PS[:, 2 * (i % 2) + 1, :].rearrange("p (k m) -> p k m", k=8),
                                     ACT.Identity, bias=w["b3"][:, 0:1]).then_inc(s_uqc, 1)

            def gates(k, s_, first):
                if not first:
                    s.wait_ge(s_score, 4 * k - 4)
                nc.scalar.copy(W0S[:, s_, :], w["w0"][:, bass.ds(k, 1), :].rearrange("p o m -> p (o m)")).then_inc(s_w0, 1)
                for q in range(4):
                    ni = 16 * (q + 1)
                    for hh in range(2):
                        if hh == 1 and q >= 2:
                            s.wait_ge(s_preB, 2 * k + q - 1)
                        else:
                            s.wait_ge(s_preA, 6 * k + PRE_ORDER.index((hh, q)) + 1)
                        g = GATE[:, 2 * s_ + hh, 16 * q:16 * q + 16, 0:ni]
                        nc.scalar.activation(g, g, ACT.Sigmoid).then_inc(s_gate, 1)

            gates(0, 0, True)
            gates(1, 1, True)
            with s.Fori(1, 8) as kk:
                gates(2 * kk, 0, False)
                gates(2 * kk + 1, 1, False)
            for b in range(4):
                s.wait_ge(s_st, b + 1)
                src = PS[:, 4 + b, :].rearrange("p (t k) -> p k t", t=16)
                nc.scalar.copy(ST[:, :, 16 * b:16 * b + 16], src).then_inc(s_stc, 1)

        def preact(eng, k, s_, hh, q, signal):
            ni = 16 * (q + 1)
            pair = k + 16 * hh
            u = U[:, bass.ds(pair, 1), 0:ni].broadcast_to([P, 16, ni])
            c = QC[:, bass.ds(pair, 1), 16 * q:16 * q + 16].rearrange("p o t -> p (o t)").unsqueeze(2).broadcast_to([P, 16, ni])
            eng.tensor_tensor(GATE[:, 2 * s_ + hh, 16 * q:16 * q + 16, 0:ni], u, c, ALU.add).then_inc(signal, 1)

        PROJ_ORDER = (0, 2, 1, 3)
        PRE_ORDER = [(0, 0), (1, 0), (0, 1), (1, 1), (0, 2), (0, 3)]

        def a0_dve(v):
            v.wait_ge(s_uqc, 4)
            v.wait_ge(s_rows, UN)

            def pre(k, s_, first):
                for hh, q in PRE_ORDER:
                    if not first and (hh == 0):
                        v.wait_ge(s_score, 4 * k - 8 + q + 1)
                    preact(nc.vector, k, s_, hh, q, s_preA)

            pre(0, 0, True)
            v.wait_ge(s_uqc, 8)
            pre(1, 1, True)
            with v.Fori(1, 8) as kk:
                pre(2 * kk, 0, False)
                pre(2 * kk + 1, 1, False)
            v.wait_ge(s_mask, 1)
            v.wait_ge(s_score, 64)
            for q in range(4):
                ni = 16 * (q + 1)
                nc.vector.tensor_tensor(SS[:, 8 * q:8 * q + 8, 0:ni],
                                        PS[:, q, :].rearrange("p (t i) -> p t i", t=8)[:, :, 0:ni],
                                        MASK[:, 8 * q:8 * q + 8, 0:ni], ALU.mult).then_inc(s_ss, 1)
            for r in range(4):
                v.wait_ge(s_att, r // 2 + 1)
                for h in range(2):
                    ins = nc.vector.tensor_tensor(half(q3(H, r), h), half(q3(H, r), h), half(bank3(r ^ h), h), ALU.add)
                ins.then_inc(s_h1, 1)

        def a0_pool(p):
            ln_wait(p, 0, "var", NQ)
            pool_chain.link(p, nc.gpsimd.memset(MASK[:, :, :], 1.0))
            for par in range(2):
                m = MASK[64 * par:64 * par + 64, :, :]
                pool_chain.link(p, nc.gpsimd.affine_select(out=m, in_=m, compare_op=ALU.is_ge, fill=0.0, base=par,
                                                           pattern=[[2, 32], [-1, 64]], channel_multiplier=0))
            ln_wait(p, 0, "out", NQ)
            nc.gpsimd.memset(SS[:, :, :], 0.0).then_inc(s_mask, 1)
            moe_weights(p, moes[0])
            p.wait_ge(s_uqc, 4)
            p.wait_ge(s_rows, UN)

            def pre(k, s_, first):
                for q in range(2, 4):
                    if not first:
                        p.wait_ge(s_score, 4 * k - 8 + q + 1)
                    preact(nc.gpsimd, k, s_, 1, q, s_preB)

            pre(0, 0, True)
            p.wait_ge(s_uqc, 8)
            pre(1, 1, True)
            with p.Fori(1, 8) as kk:
                pre(2 * kk, 0, False)
                pre(2 * kk + 1, 1, False)

        def a0_sp(sp):
            for r in range(4):
                sp.wait_ge(s_h1, r + 1)
                for h in range(2):
                    sp.dma_start(scratch[:, 32 * h + 8 * r:32 * h + 8 * r + 8, :], H[64 * h:64 * h + 64, 8 * r:8 * r + 8, :]
                                 ).then_inc(s_h1st, 16)
            h1_load(sp, 0)

        def h1_load(eng, b):
            eng.wait_ge(s_h1st, 16 * 8)
            src = scratch.rearrange("(j b) t e -> b t j e", b=2)
            for jh in range(2):
                j = slice(jh * HJ, jh * HJ + HJ)
                eng.dma_start(H[64 * b:64 * b + 64, j, :], src[b][:, j, :]).then_inc(s_h1ld[jh], 16)

        XS = BIG[:, 0:4096].rearrange("p (j c e) -> p j c e", j=NJ, c=2)
        HB = BIG[:, 4096:6144].rearrange("p (u n) -> p u n", u=4)
        HW = BIG[:, 6144:8192].rearrange("p (u n) -> p u n", u=4)
        YE = BIG[:, 8192:8704]
        WS = BIG[:, 8704:9728].bitcast(BF16).rearrange("p (j m) -> p j m", j=NJ)
        WT3 = BIG[:, 10240:12288].bitcast(BF16)
        B2S = sb("B2S", [48, 3, P], BF16)
        SMALL = sb("SMALL", [P, 256])

        moe_sems = {}

        class Moe:

            def __init__(self, n, nch, ne, act, before, pooled=False):
                self.n, self.nch, self.ne, self.act, self.pooled, self.before = n, nch, ne, act, pooled, before
                self.np = nch // 2
                units = NG * nch
                self.steps = dict(hi=NQ, split=NQ, xt=NG, xtc=NG, wprep=1, b2prep=1, **{x: 1 if pooled else 2 for x in ("logits", "gap", "tanh", "wsplit")},
                                  wt=1 if pooled else NG, wtc=1 if pooled else NG, mm1=units, hact=units, wbc=units,
                                  scaled=units, mm2=units // 2, yevac=NG, ii=NG, comb=NG,
                                  img_mean=int(pooled), img_mean_copied=int(pooled), shifted=2 * pooled, exped=2 * pooled,
                                  probs=int(pooled), load=int(pooled), router_xt=NG * (n == 2), router_xtc=NG * (n == 2),
                                  experts_added=NG * (n == 1),
                                  lnb=int(n == 2), b1prep=int(n == 2), added=NG * (n == 3), affine=NG * (n == 0),
                                  hsum=NG * (n == 0), hcopy=NG * (n != 3), na_step=4 * NG, na_var=NG, na_rstd=NG, na_out=NG,
                                  nb_step=4 * NG * (n == 0), nb_var=NG * (n == 0), nb_rstd=NG * (n == 0), nb_out=NG * (n == 0))
                for x in self.steps:
                    if x not in moe_sems:
                        moe_sems[x] = sem(f"moe_{x}")

            def __getitem__(self, name):
                return moe_sems[name]

            def value(self, name, count):
                return count + sum(m.steps[name] for m in self.before)

            def wait(self, eng, name, count):
                eng.wait_ge(moe_sems[name], self.value(name, count))

        def split_three(v, src, dst, tmp, part, signal):
            p0 = dst(0)
            dve_chain.link(v, nc.vector.tensor_copy(p0, src))
            dve_chain.link(v, nc.vector.tensor_tensor(tmp, src, p0, ALU.subtract))
            dve_chain.link(v, nc.vector.tensor_copy(dst(1), tmp))
            dve_chain.link(v, nc.vector.tensor_tensor(tmp, tmp, dst(1), ALU.subtract))
            nc.vector.tensor_copy(dst(2), tmp).then_inc(signal, 1)

        def top2(v, M, lg, pp, nj, j0=0, half_=0):
            E = M.ne
            t = [RT[0:pp, i, j0:j0 + nj, 0:E] for i in range(8)]
            r = [RV[0:pp, i, j0:j0 + nj] for i in range(12)]
            bc = lambda x: x.unsqueeze(2).broadcast_to([pp, nj, E])
            prio = w["prio"][0:pp, 16 - E:16].unsqueeze(1).broadcast_to([pp, nj, E])
            L = lambda ins: dve_chain.link(v, ins)
            L(nc.vector.tensor_reduce(r[0], lg, AX.X, ALU.max))
            L(nc.vector.tensor_tensor(t[1], lg, bc(r[0]), ALU.is_equal))
            L(nc.vector.tensor_tensor(t[1], t[1], prio, ALU.mult))
            L(nc.vector.tensor_reduce(r[1], t[1], AX.X, ALU.max))
            L(nc.vector.tensor_tensor(t[2], bc(r[1]), prio, ALU.is_equal))
            L(nc.vector.scalar_tensor_tensor(out=t[3], in0=t[2], scalar=BIG_NEG, in1=lg, op0=ALU.mult, op1=ALU.add))
            L(nc.vector.tensor_reduce(r[2], t[3], AX.X, ALU.max))
            nc.vector.tensor_tensor(r[3], r[2], r[0], ALU.subtract).then_inc(M["gap"], 1)
            L(nc.vector.tensor_tensor(t[4], t[3], bc(r[2]), ALU.is_equal))
            L(nc.vector.tensor_tensor(t[4], t[4], prio, ALU.mult))
            L(nc.vector.tensor_reduce(r[4], t[4], AX.X, ALU.max))
            L(nc.vector.tensor_tensor(t[5], bc(r[4]), prio, ALU.is_equal))
            M.wait(v, "tanh", half_ + 1)
            L(nc.vector.tensor_scalar(r[6], r[5], 0.5, 0.5, ALU.mult, ALU.add))
            L(nc.vector.tensor_scalar(r[7], r[5], -0.5, 0.5, ALU.mult, ALU.add))
            L(nc.vector.tensor_tensor(t[5], t[5], bc(r[6]), ALU.mult))
            L(nc.vector.tensor_tensor(t[2], t[2], bc(r[7]), ALU.mult))
            L(nc.vector.tensor_tensor(t[6], t[2], t[5], ALU.add))
            return t[6], t[7]

        def moe_act_tanh(s, M, pp, nj, j0=0, half_=0):
            M.wait(s, "gap", half_ + 1)
            nc.scalar.activation(RV[0:pp, 5, j0:j0 + nj], RV[0:pp, 3, j0:j0 + nj], ACT.Tanh, scale=0.5).then_inc(M["tanh"], 1)

        def moe_weights(p, M):
            n, nch, E = M.n, M.nch, M.ne
            L = lambda ins: pool_chain.link(p, ins)
            p.wait_ge(s_late, 16 * n_late)
            p.wait_ge(s_w1[n], 16)
            cols = nch * P
            if n > 0:
                moes[n - 1].wait(p, "mm2", NG * moes[n - 1].np)
            if n == 2:
                M.wait(p, "lnb", 1)
                for e in range(E):
                    L(nc.gpsimd.tensor_scalar(W1S[:, e * 256:(e + 1) * 256], W1S[:, e * 256:(e + 1) * 256],
                                              w["lng"][:, e:e + 1], None, ALU.mult))
            L(nc.gpsimd.tensor_copy(WH[:, 0:cols], W1S[:, 0:cols]))
            nc.gpsimd.tensor_tensor(WL[:, 0:cols], W1S[:, 0:cols], WH[:, 0:cols].bitcast(F32), ALU.subtract).then_inc(M["wprep"], 1)
            e3 = 3 * E
            if n == 0:
                L(nc.gpsimd.memset(B2S[:, :, D:P], 0.0))
            src, tmp = w[f"b2_{n}"][0:e3, :], SMALL[0:e3, 0:64]
            L(nc.gpsimd.tensor_copy(B2S[0:e3, 0, 0:D], src))
            L(nc.gpsimd.tensor_tensor(tmp, src, B2S[0:e3, 0, 0:D], ALU.subtract))
            L(nc.gpsimd.tensor_copy(B2S[0:e3, 1, 0:D], tmp))
            L(nc.gpsimd.tensor_tensor(tmp, tmp, B2S[0:e3, 1, 0:D], ALU.subtract))
            nc.gpsimd.tensor_copy(B2S[0:e3, 2, 0:D], tmp).then_inc(M["b2prep"], 1)

        def split_low(v, M):
            def quarter(q):
                M.wait(v, "hi", q + 1)
                nc.vector.tensor_tensor(XS[:, q * QJ:(q + 1) * QJ, 1, :], q3(XN(M), q), XS[:, q * QJ:(q + 1) * QJ, 0, :],
                                        ALU.subtract).then_inc(M["split"], 1)
            return quarter

        def split_high(s, M):
            def quarter(q):
                ln_wait(s, (1, 2, 4, 5)[M.n], "out", q + 1)
                nc.scalar.copy(XS[:, q * QJ:(q + 1) * QJ, 0, :].bitcast(F32R), q3(XN(M), q)).then_inc(M["hi"], 1)
            return quarter

        def moe_dve(v, M):
            n, nch, E = M.n, M.nch, M.ne
            if M.pooled:
                pooled_dve(v, M)
            else:
                for hf in range(2):
                    M.wait(v, "logits", hf + 1)
                    tiles = slice(hf * HJ, hf * HJ + HJ)
                    lg = RT[:, 0, tiles, 0:E]
                    rb = w[f"rb_{n}"][:, :].unsqueeze(1).broadcast_to([P, HJ, E])
                    dve_chain.link(v, nc.vector.tensor_tensor(lg, PS[:, 6 + hf, 0:HJ * E].rearrange("p (j e) -> p j e", j=HJ), rb,
                                                              ALU.add))
                    wd, tmp = top2(v, M, lg, P, HJ, hf * HJ, hf)
                    split_three(v, wd, lambda i: WS[:, tiles, i * E:(i + 1) * E], tmp, P, M["wsplit"])
            moe_main_dve(v, M)

        def XN(M):
            return XC if M.n == 2 else XA

        def pooled_dve(v, M):
            E = M.ne
            L = lambda ins: dve_chain.link(v, ins)
            M.wait(v, "img_mean", 1)
            nc.vector.tensor_copy(SMALL[0:64, 64:128], PS[0:64, 6, 0:64]).then_inc(M["img_mean_copied"], 1)
            M.wait(v, "logits", 1)
            lg = RT[0:64, 0, 0, 0:E]
            r = [RV[0:64, i, 0:1] for i in range(8, 12)]
            L(nc.vector.tensor_tensor(lg, PS[0:64, 7, 0:E], w["rb_0"][0:64, :], ALU.add))

            def softmax(x, ex, step):
                L(nc.vector.tensor_reduce(r[0], x, AX.X, ALU.max))
                nc.vector.tensor_scalar(ex, x, r[0], None, ALU.subtract).then_inc(M["shifted"], 1)
                M.wait(v, "exped", step)
                L(nc.vector.tensor_reduce(r[1], ex, AX.X, ALU.add))
                L(nc.vector.reciprocal(r[2], r[1]))
                return nc.vector.tensor_scalar(x, ex, r[2], None, ALU.mult)

            softmax(lg, RT[0:64, 1, 0, 0:E], 1).then_inc(M["probs"], 1)
            M.wait(v, "load", 1)
            sc = RT[0:64, 2, 0, 0:E]
            tokens_per_image = float(NT)
            capacity = float(-(-NI * NT * 5 // (4 * E)))
            L(nc.vector.tensor_scalar(sc, PS[0:64, 5, 0:E], tokens_per_image, None, ALU.mult))
            L(nc.vector.reciprocal(sc, sc))
            L(nc.vector.tensor_scalar(sc, sc, capacity, 1.0, ALU.mult, ALU.min))
            L(nc.vector.tensor_tensor(lg, lg, sc, ALU.mult))
            L(softmax(lg, RT[0:64, 1, 0, 0:E], 2))
            wd, tmp = top2(v, M, RT[0:64, 0, 0:1, 0:E], 64, 1)
            split_three(v, wd, lambda i: WS[0:64, 0:1, i * E:(i + 1) * E], tmp, 64, M["wsplit"])
            M.wait(v, "wt", 1)
            src = PS[0:3 * E, 4, 0:32].bitcast(BF16)
            nc.vector.tensor_copy(WT3[0:3 * E, :].rearrange("p (b t) -> p b t", b=NI),
                                  src.unsqueeze(2).broadcast_to([3 * E, NI, NT])).then_inc(M["wtc"], 1)

        def pooled_act(s, M):
            E = M.ne
            for step in range(2):
                M.wait(s, "shifted", step + 1)
                ex = RT[0:64, 1, 0, 0:E]
                nc.scalar.activation(ex, ex, ACT.Exp).then_inc(M["exped"], 1)

        def pooled_pe(pe, M):
            E = M.ne
            for j in range(NJ):
                ins = nc.tensor.matmul(PS[0:64, 6, 2 * j:2 * j + 2], XA[:, j, :], w["pool2"][:, :], start=True, stop=True)
            ins.then_inc(M["img_mean"], 1)
            M.wait(pe, "img_mean_copied", 1)
            nc.tensor.matmul(PS[0:64, 7, 0:E], SMALL[0:64, 64:128], w["rw_0"][0:64, :], start=True, stop=True).then_inc(M["logits"], 1)
            M.wait(pe, "probs", 1)
            nc.tensor.matmul(PS[0:64, 5, 0:E], w["ones64"][:, :], RT[0:64, 0, 0, 0:E], start=True, stop=True).then_inc(M["load"], 1)
            M.wait(pe, "wsplit", 1)
            nc.tensor.transpose(PS[0:3 * E, 4, 0:32].bitcast(BF16), WS[0:64, 0, 0:3 * E], w["Ib"][0:64, 0:64]).then_inc(M["wt"], 1)

        def moe_pe(pe, M):
            n, nch, E = M.n, M.nch, M.ne
            if n == 2:
                route_pe(pe, M)
            for g in range(NG):
                M.wait(pe, "split", g // 2 + 1)
                if n == 2 and g < 4:
                    M.wait(pe, "router_xtc", g + 5)
                if g >= 4:
                    M.wait(pe, "xtc", g - 3)
                for i in range(4):
                    ins = nc.tensor.transpose(PS[:, g % 4, i * P:(i + 1) * P],
                                              XS[:, 4 * g + i, :, :].rearrange("p c e -> p (c e)"), w["I"][:, :])
                ins.then_inc(M["xt"], 1)
            if M.pooled:
                pe.wait_ge(s_late, 16 * n_late)
                pooled_pe(pe, M)
            else:
                if n != 2:
                    route_pe(pe, M)
                for g in range(NG):
                    M.wait(pe, "wsplit", g // (NG // 2) + 1)
                    if g >= 4:
                        M.wait(pe, "wtc", g - 3)
                    for i in range(4):
                        ins = nc.tensor.transpose(PS[0:3 * E, g % 4, i * 64:(i + 1) * 64].bitcast(BF16), WS[:, 4 * g + i, 0:3 * E],
                                                  w["Ib"][:, :])
                    ins.then_inc(M["wt"], 1)
            moe_main_pe(pe, M)

        def route_pe(pe, M):
            n, E = M.n, M.ne
            if n == 2:
                for g in range(NG):
                    ln_wait(pe, 3, "out", g // 2 + 1)
                    if g >= 4:
                        M.wait(pe, "router_xtc", g - 3)
                    for i in range(4):
                        ins = nc.tensor.transpose(PS[0:64, g % 4, i * P:(i + 1) * P], XA[:, 4 * g + i, :], w["I"][:, :])
                    ins.then_inc(M["router_xt"], 1)
                M.wait(pe, "b1prep", 1)
                xt, k, copied = XT, 64, "router_xtc"
            else:
                xt, k, copied = XTR, P, "xtc"
            for j in range(NJ):
                if j % HJ == 0:
                    M.wait(pe, copied, NG // 2 * (j // HJ + 1))
                lhs = xt[0:k, j * P:(j + 1) * P]
                if n != 2:
                    lhs = lhs.bitcast(F32)
                jj = j % HJ
                ins = nc.tensor.matmul(PS[:, 6 + j // HJ, jj * E:(jj + 1) * E], lhs, w[f"rw_{n}"][0:k, :], start=True, stop=True)
                if jj == HJ - 1:
                    ins.then_inc(M["logits"], 1)

        def router_copies(s, M):
            for g in range(NG):
                M.wait(s, "router_xt", g + 1)
                nc.scalar.copy(XT[0:64, g * 512:(g + 1) * 512], PS[0:64, g % 4, :]).then_inc(M["router_xtc"], 1)

        def moe_act(s, M):
            n, nch, E = M.n, M.nch, M.ne
            for g in range(NG):
                M.wait(s, "xt", g + 1)
                nc.scalar.copy(XTR[:, g * 512:(g + 1) * 512], PS[:, g % 4, :]).then_inc(M["xtc"], 1)
            if M.pooled:
                pooled_act(s, M)
                moe_act_tanh(s, M, 64, 1)
            else:
                for hf in range(2):
                    moe_act_tanh(s, M, P, HJ, hf * HJ, hf)
                for g in range(NG):
                    M.wait(s, "wt", g + 1)
                    src = PS[0:3 * E, g % 4, 0:256].bitcast(BF16)
                    nc.scalar.copy(WT3[0:3 * E, g * 512:(g + 1) * 512], src).then_inc(M["wtc"], 1)
            moe_main_act(s, M)

        ZB, BB, YB, TB = 0, 4, 6, 7

        def moe_main_pe(pe, M):
            n, nch, NPR, e3 = M.n, M.nch, M.np, 3 * M.ne
            M.wait(pe, "wprep", 1)
            M.wait(pe, "b2prep", 1)
            M.wait(pe, "xtc", NG)
            M.wait(pe, "wtc", 1 if M.pooled else NG)
            SEL = w[f"sel_{n}"]
            W2 = w[f"w2_{n}"]

            def up(g, p, first, fresh_banks=False, before_last=lambda: None):
                if not first and not fresh_banks:
                    M.wait(pe, "hact", g * nch + 2 * p - 2)
                for i in range(2):
                    c = 2 * p + i
                    z = PS[:, ZB + c % 4, :]
                    x = XTR[:, bass.ds(g * 512, 512)]
                    nc.tensor.matmul(z, WH[:, c * P:(c + 1) * P], x, start=True, stop=False)
                    if not first:
                        M.wait(pe, "scaled", g * nch + 2 * p - 1 + i)
                    if i == 1:
                        before_last()
                    nc.tensor.matmul(z, WL[:, c * P:(c + 1) * P], x, start=False, stop=True).then_inc(M["mm1"], 1)
                    nc.tensor.matmul(PS[:, BB + i, :], SEL[0:e3, c * P:(c + 1) * P], WT3[0:e3, bass.ds(g * 512, 512)],
                                     start=True, stop=True).then_inc(M["wbc"], 1)

            def down(g, p):
                M.wait(pe, "scaled", g * nch + 2 * p + 2)
                for i in range(2):
                    c = 2 * p + i
                    ins = nc.tensor.matmul(PS[64 * i:64 * i + 64, YB, :], W2[:, c, :], HW[:, c % 4, :],
                                           start=False, stop=(p == NPR - 1), skip_group_check=True)
                ins.then_inc(M["mm2"], 1)

            def group(g, first, last):
                def output_bank_free():
                    if not first:
                        M.wait(pe, "yevac", g)

                for p in range(NPR):
                    if p == 0:
                        up(g, 1, False, first, output_bank_free)
                        for i in range(3):
                            nc.tensor.matmul(PS[:, YB, :], B2S[0:e3, i, :], WT3[0:e3, bass.ds(g * 512, 512)],
                                             start=i == 0, stop=False, skip_group_check=True)
                    elif p < NPR - 1:
                        up(g, p + 1, False)
                    elif not last:
                        up(g + 1, 0, False)
                    down(g, p)
                    if p == 0 and not first:
                        turn_back(g - 1)

            def turn_back(g):
                M.wait(pe, "yevac", g + 1)
                for i in range(4):
                    ins = nc.tensor.matmul(PS[:, TB, i * 64:i * 64 + 64], YE[:, i * P:(i + 1) * P], w["II"][:, :],
                                           start=True, stop=True)
                ins.then_inc(M["ii"], 1)

            up(0, 0, True)
            group(0, True, False)
            with pe.Fori(1, NG - 1) as g:
                group(g, False, False)
            group(NG - 1, False, True)
            turn_back(NG - 1)

        def moe_main_act(s, M):
            n, nch = M.n, M.nch

            def group(g, first):
                for c in range(nch):
                    M.wait(s, "mm1", g * nch + c + 1)
                    if not (first and c < 4):
                        M.wait(s, "scaled", g * nch + c - 3)
                    nc.scalar.activation(HB[:, c % 4, :], PS[:, ZB + c % 4, :], M.act, bias=w[f"b1_{n}"][:, c:c + 1]
                                         ).then_inc(M["hact"], 1)

            if n == 2:
                M.wait(s, "b1prep", 1)
            group(0, True)
            with s.Fori(1, NG) as g:
                group(g, False)

        def moe_main_dve(v, M):
            n, nch, NPR = M.n, M.nch, M.np

            first_norm = Norm(v, M, "na", WORK[:, 0:768], LNS[:, 0:2, 0:12])
            second_norm = Norm(v, M, "nb", WORK[:, 768:1536], LNS[:, 2:4, 0:12])

            take, comb, scale = [("take", 0)], [("combine", 0)], [("scale", 0)]
            a = lambda k: [("stats", k)]
            b = lambda k: [("stats_b", k)]
            if nch == 4:
                plan = {1: take, 3: comb + a(0), 4: a(1) + a(2), 5: a(3) + a(4), 8: scale}
            else:
                plan = {1: take, 3: comb, 4: a(0), 5: a(1), 6: a(2), 7: a(3), 8: a(4), 11: scale}
            if n == 0:
                plan.update({14: [("add", 0)], 15: b(0), 16: b(1), 17: b(2), 18: b(3), 19: b(4), 22: [("scale_b", 0)]})

            def finish(g, c, groups):
                for lag in groups:
                    m = g - lag
                    for what, k in plan.get((lag - 1) * nch + c, []):
                        if what == "take":
                            take_out(m)
                        elif what == "combine":
                            combine(m)
                        elif what == "add":
                            add_to_h(m)
                        elif what == "stats":
                            first_norm.stats(m, k, "comb")
                        elif what == "stats_b":
                            second_norm.stats(m, k, "hsum")
                        elif what == "scale":
                            first_norm.scale(m)
                        else:
                            second_norm.scale(m)

            def group(g, age):
                for c in range(nch):
                    M.wait(v, "hact", g * nch + c + 1)
                    M.wait(v, "wbc", g * nch + c + 1)
                    if not (age == 0 and c < 4) and c % 2 == 0:
                        M.wait(v, "mm2", g * NPR + c // 2 - 1)
                    nc.vector.tensor_tensor(HW[:, c % 4, :], HB[:, c % 4, :], PS[:, BB + c % 2, :], ALU.mult).then_inc(M["scaled"], 1)
                    finish(g, c, [lag for lag in (3, 2, 1) if lag <= age])

            def take_out(g):
                M.wait(v, "mm2", g * NPR + NPR)
                nc.vector.tensor_copy(YE[:, :], PS[:, YB, :]).then_inc(M["yevac"], 1)

            def is_first(g):
                return isinstance(g, int) and g == 0

            def combine(g):
                y = PS[:, TB, 0:256].rearrange("p (j e) -> p j e", j=4)
                hg = H[:, bass.ds(g * 4, 4), :]
                xg = XA[:, bass.ds(g * 4, 4), :]
                if n in (1, 2) and not is_first(g):
                    M.wait(v, "hcopy", g)
                M.wait(v, "ii", g + 1)
                if n in (0, 3):
                    nc.vector.tensor_tensor(first_norm.x, xg, y, ALU.add).then_inc(M["comb"], 1)
                elif n == 1:
                    nc.vector.tensor_tensor(xg, xg, y, ALU.add).then_inc(M["experts_added"], 1)
                    M.wait(v, "experts_added", g + 1)
                    nc.vector.tensor_tensor(first_norm.x, hg, xg, ALU.add).then_inc(M["comb"], 1)
                else:
                    nc.vector.tensor_tensor(first_norm.x, hg, y, ALU.add).then_inc(M["comb"], 1)

            def add_to_h(g):
                M.wait(v, "affine", g + 1)
                if not is_first(g):
                    M.wait(v, "hcopy", g)
                hg = H[:, bass.ds(g * 4, 4), :]
                xg = XA[:, bass.ds(g * 4, 4), :]
                nc.vector.tensor_tensor(second_norm.x, hg, xg, ALU.add).then_inc(M["hsum"], 1)

            group(0, 0)
            group(1, 1)
            group(2, 2)
            with v.Fori(3, NG) as g:
                group(g, 3)
            for g in range(NG, NG + 3):
                for c in range(nch):
                    finish(g, c, [lag for lag in (3, 2, 1) if 0 <= g - lag < NG])

        class Norm:

            def __init__(self, v, M, tag, tiles, sums):
                t = tiles.rearrange("p (i j e) -> p i j e", i=3, j=4)
                self.v, self.M, self.tag = v, M, tag
                self.x, self.centred, self.square = (t[:, i] for i in range(3))
                self.sum, self.mean, self.var = (sums[:, 0, 4 * i:4 * i + 4] for i in range(3))
                self.rstd = sums[:, 1, 0:4]

            def bc(self, t):
                return t.unsqueeze(2).broadcast_to([P, 4, D])

            def stats(self, g, k, ready):
                if k == 0:
                    self.M.wait(self.v, ready, g + 1)
                else:
                    self.M.wait(self.v, self.tag + "_step", 4 * g + k)
                if k == 0:
                    ins = nc.vector.tensor_reduce(self.sum, self.x, AX.X, ALU.add)
                elif k == 1:
                    ins = nc.vector.tensor_scalar(self.mean, self.sum, 1.0 / D, None, ALU.mult)
                elif k == 2:
                    ins = nc.vector.tensor_tensor(self.centred, self.x, self.bc(self.mean), ALU.subtract)
                elif k == 3:
                    ins = nc.vector.tensor_tensor(self.square, self.centred, self.centred, ALU.mult)
                else:
                    ins = nc.vector.tensor_reduce(self.var, self.square, AX.X, ALU.add)
                ins.then_inc(self.M[self.tag + ("_step" if k < 4 else "_var")], 1)

            def scale(self, g):
                self.M.wait(self.v, self.tag + "_rstd", g + 1)
                nc.vector.tensor_tensor(XA[:, bass.ds(g * 4, 4), :], self.centred, self.bc(self.rstd), ALU.mult
                                        ).then_inc(self.M[self.tag + "_out"], 1)

        def moe_main_pool(p, M):
            n = M.n
            norms = {"na": Norm(p, M, "na", WORK[:, 0:768], LNS[:, 0:2, 0:12]),
                     "nb": Norm(p, M, "nb", WORK[:, 768:1536], LNS[:, 2:4, 0:12])}

            def rstd(tag, g):
                N = norms[tag]
                M.wait(p, tag + "_var", g + 1)
                pool_chain.link(p, nc.gpsimd.tensor_scalar(N.rstd, N.var, 1.0 / D, EPS, ALU.mult, ALU.add))
                nc.gpsimd.tensor_tensor(N.rstd, N.rstd, HALFPOW[:, 0:4], ALU.pow).then_inc(M[tag + "_rstd"], 1)

            def tiles(t, g):
                return t[:, 4 * g:4 * g + 4, :]

            def affine(g):
                M.wait(p, "na_out", g + 1)
                row = lambda name: w[f"{name}_{n}"][:, :].unsqueeze(1).broadcast_to([P, 4, D])
                pool_chain.link(p, nc.gpsimd.tensor_tensor(tiles(XA, g), tiles(XA, g), row("gamma"), ALU.mult))
                ins = nc.gpsimd.tensor_tensor(tiles(XA, g), tiles(XA, g), row("beta"), ALU.add)
                if n == 0:
                    ins.then_inc(M["affine"], 1)
                else:
                    pool_chain.link(p, ins)
                    nc.gpsimd.tensor_tensor(tiles(H, g), tiles(H, g), tiles(XA, g), ALU.add).then_inc(M["added"], 1)

            def h_from(tag, ready, g):
                M.wait(p, ready, g + 1)
                nc.gpsimd.tensor_copy(tiles(H, g), norms[tag].x).then_inc(M["hcopy"], 1)

            for g in range(NG + 1):
                if n in (0, 3) and g >= 1:
                    affine(g - 1)
                if g < NG:
                    if n in (1, 2):
                        h_from("na", "comb", g)
                    rstd("na", g)
                if n == 0 and g >= 1:
                    h_from("nb", "hsum", g - 1)
                    rstd("nb", g - 1)

        moes = []
        for n_, nch_, ne_, act_ in ((0, 8, 8, ACT.Gelu), (1, 4, 8, ACT.Gelu), (2, 16, 8, ACT.Gelu), (3, 16, 16, ACT.Relu)):
            moes.append(Moe(n_, nch_, ne_, act_, list(moes), pooled=n_ == 0))

        ATT = {1: "aw awc xt xtc gt gtc s v vc exp sub pt ptc norm o oh",
               2: "xt xtc coef s kv rexp kin kexp shift wkv rw rt rtc o oh",
               3: "xt xtc q qc om omc z zc r rc rr oh"}
        att = {n: {x: sem(f"att{n}_{x}") for x in names.split()} for n, names in ATT.items()}

        GT = BIG[0:64, 0:4096]
        PE_ = BIG[:, 4096:6144].rearrange("p (j k) -> p j k", j=NJ)
        PT = BIG[:, 6144:8192].rearrange("p (j k) -> p j k", j=NJ)
        VV = BIG[:, 8192:10240].rearrange("p (j k) -> p j k", j=NJ)
        AW = BIG[0:64, 10240:10304]

        def xt_pe(pe, T, M, normed):
            for g in range(NG):
                M.wait(pe, normed, g + 1)
                if g >= 2:
                    pe.wait_ge(T["xtc"], g - 1)
                for i in range(4):
                    ins = nc.tensor.transpose(PS[0:64, g % 2, i * P:(i + 1) * P], XA[:, 4 * g + i, :], w["I"][:, :])
                ins.then_inc(T["xt"], 1)

        def a1_pe(pe):
            T = att[1]
            pe.wait_ge(s_late, 16 * n_late)
            xt_pe(pe, T, moes[0], "nb_out")
            nc.tensor.matmul(PS[0:64, 7, 0:64], w["wqT"][:, :], w["wkT"][:, :], start=True, stop=True).then_inc(T["aw"], 1)
            pe.wait_ge(T["awc"], 1)
            for g in range(NG):
                pe.wait_ge(T["xtc"], g + 1)
                if g >= 2:
                    pe.wait_ge(T["gtc"], g - 1)
                nc.tensor.matmul(PS[0:64, 4 + g % 2, :], AW, XT[0:64, g * 512:(g + 1) * 512], start=True, stop=True
                                 ).then_inc(T["gt"], 1)
            for j in range(NJ):
                if j % 8 == 0:
                    pe.wait_ge(T["gtc"], 2 * (j // 8) + 2)
                for b in range(2):
                    c = j * P + b * 64
                    ins = nc.tensor.matmul(PS[64 * b:64 * b + 64, j // 8, (j % 8) * 64:(j % 8) * 64 + 64],
                                           GT[:, c:c + 64], XT[0:64, c:c + 64], start=True, stop=True)
                if j % 8 == 7:
                    ins.then_inc(T["s"], 1)
            for q in range(4):
                pe.wait_ge(T["gtc"], NG)
                for i in range(8):
                    j = 8 * q + i
                    ins = nc.tensor.matmul(PS[:, 4 + q, i * 64:i * 64 + 64], XT[0:64, j * P:(j + 1) * P], w["wv"][:, :],
                                           start=True, stop=True)
                ins.then_inc(T["v"], 1)
            for qq in range(2):
                pe.wait_ge(T["exp"], 2 * qq + 2)
                for j in range(16 * qq, 16 * qq + 16):
                    for b in range(2):
                        ins = nc.tensor.matmul(PS[64 * b:64 * b + 64, (j // 8) ^ b, (j % 8) * 64:(j % 8) * 64 + 64],
                                               PE_[64 * b:64 * b + 64, j, :], w["I"][64 * b:64 * b + 64, 64 * b:64 * b + 64],
                                               start=True, stop=True)
                ins.then_inc(T["pt"], 1)
            for qq in range(2):
                pe.wait_ge(T["ptc"], qq + 1)
                pe.wait_ge(T["vc"], 2 * qq + 2)
                for j in range(16 * qq, 16 * qq + 16):
                    for b in range(2):
                        r = slice(64 * b, 64 * b + 64)
                        ins = nc.tensor.matmul(PS[r, 4 + ((j // 8) ^ b), (j % 8) * 64:(j % 8) * 64 + 64], PT[r, j, :], VV[r, j, :],
                                               start=True, stop=True)
                ins.then_inc(T["o"], 1)

        def a1_act(s):
            T = att[1]
            for g in range(NG):
                s.wait_ge(T["xt"], g + 1)
                nc.scalar.copy(XT[0:64, g * 512:(g + 1) * 512], PS[0:64, g % 2, :]).then_inc(T["xtc"], 1)
            s.wait_ge(T["aw"], 1)
            nc.scalar.mul(AW, PS[0:64, 7, 0:64], float(D) ** -0.5).then_inc(T["awc"], 1)
            for g in range(NG):
                s.wait_ge(T["gt"], g + 1)
                nc.scalar.copy(GT[:, g * 512:(g + 1) * 512], PS[0:64, 4 + g % 2, :]).then_inc(T["gtc"], 1)
            for q in range(4):
                s.wait_ge(T["sub"], q + 1)
                nc.scalar.activation(q3(PE_, q), q3(PE_, q), ACT.Exp).then_inc(T["exp"], 1)
            for qq in range(2):
                s.wait_ge(T["pt"], qq + 1)
                for q in (2 * qq, 2 * qq + 1):
                    for b in range(2):
                        ins = nc.scalar.copy(half(q3(PT, q), b), half(bank3(q ^ b), b))
                ins.then_inc(T["ptc"], 1)

        def half(t, b):
            return t[64 * b:64 * b + 64]

        def bank3(b):
            return PS[:, b, :].rearrange("p (j e) -> p j e", j=8)

        def a1_dve(v):
            T = att[1]
            moes[0].wait(v, "hcopy", NG)
            for q in range(4):
                v.wait_ge(T["s"], q + 1)
                m = RV[:, 0, 8 * q:8 * q + 8]
                dve_chain.link(v, nc.vector.tensor_reduce(m, bank3(q), AX.X, ALU.max))
                nc.vector.tensor_tensor(q3(PE_, q), bank3(q), bc_j(RV[:, 0, :], q), ALU.subtract).then_inc(T["sub"], 1)
            for q in range(4):
                v.wait_ge(T["v"], q + 1)
                nc.vector.tensor_copy(q3(VV, q), bank3(4 + q)).then_inc(T["vc"], 1)
            for q in range(4):
                v.wait_ge(T["exp"], q + 1)
                ins = nc.vector.tensor_reduce(RV[:, 1, 8 * q:8 * q + 8], q3(PE_, q), AX.X, ALU.add)
                dve_chain.link(v, ins)
            dve_chain.link(v, nc.vector.reciprocal(RV[:, 2, :], RV[:, 1, :]))
            for q in range(4):
                v.wait_ge(T["o"], q // 2 + 1)
                for b in range(2):
                    ins = nc.vector.tensor_tensor(half(q3(XC, q), b), half(bank3(4 + (q ^ b)), b), half(bc_j(RV[:, 2, :], q), b), ALU.mult)
                ins.then_inc(T["norm"], 1)
                v.wait_ge(T["norm"], q + 1)
                nc.vector.tensor_tensor(q3(H, q), q3(H, q), q3(XC, q), ALU.add).then_inc(T["oh"], 1)

        KK = BIG[:, 0:2048].rearrange("p (j e) -> p j e", j=NJ)
        KV = BIG[:, 2048:4096].rearrange("p (j e) -> p j e", j=NJ)
        RR = BIG[:, 4096:6144].rearrange("p (j e) -> p j e", j=NJ)
        DN = BIG[:, 6144:8192].rearrange("p (j e) -> p j e", j=NJ)
        RWT = BIG[0:64, 8192:12288]
        XSH = XT

        def a2_pe(pe):
            T = att[2]
            xt_pe(pe, T, moes[1], "na_out")
            pe.wait_ge(s_w1[2], 16)
            pe.wait_ge(s_late, 16 * n_late)
            for c in range(moes[2].nch):
                ins = nc.tensor.matmul(PS[:, 7, c:c + 1], W1S[0:64, c * P:(c + 1) * P], w["lnb"][0:64, c // 2:c // 2 + 1],
                                       start=True, stop=True)
            ins.then_inc(moes[2]["lnb"], 1)
            pe.wait_ge(T["coef"], 3)
            for j in range(NJ):
                if j % 2 == 0:
                    pe.wait_ge(T["xtc"], j // 4 + 1)
                    pe.wait_ge(T["shift"], j // 4 + 1)
                if j >= 4:
                    pe.wait_ge(T["kv"], j - 3)
                    pe.wait_ge(T["rexp"], j - 3)
                nc.tensor.matmul(PS[:, 2 + j % 4, 0:192], XSH[:, j * P:(j + 1) * P], w["wkvr"][:, :], start=True, stop=True
                                 ).then_inc(T["s"], 1)
            for q in range(4):
                pe.wait_ge(T["kv"], NJ)
                pe.wait_ge(T["rexp"], NJ)
                pe.wait_ge(T["xtc"], NG)
                if q >= 2:
                    pe.wait_ge(T["rw"], q - 1)
                nc.tensor.matmul(PS[:, 2 * (q % 2), :], w["cum"][:, :], q3(KK, q), start=True, stop=True)
                nc.tensor.matmul(PS[:, 2 * (q % 2) + 1, :], w["toep"][:, :], q3(KV, q), start=True, stop=True).then_inc(T["wkv"], 1)
            for g in range(NG):
                pe.wait_ge(T["rw"], g // 2 + 1)
                if g >= 2:
                    pe.wait_ge(T["rtc"], g - 1)
                for i in range(4):
                    ins = nc.tensor.transpose(PS[0:64, 4 + g % 2, i * P:(i + 1) * P], RR[:, 4 * g + i, :], w["I"][:, :])
                ins.then_inc(T["rt"], 1)
            for q in range(4):
                pe.wait_ge(T["rtc"], 2 * q + 2)
                pe.wait_ge(T["rw"], 4)
                for i in range(8):
                    j = 8 * q + i
                    ins = nc.tensor.matmul(PS[:, q, i * 64:i * 64 + 64], RWT[:, j * P:(j + 1) * P], w["wo"][:, :], start=True, stop=True)
                ins.then_inc(T["o"], 1)

        def a2_act(s):
            T = att[2]
            for g in range(NG):
                s.wait_ge(T["xt"], g + 1)
                nc.scalar.copy(XSH[0:64, g * 512:(g + 1) * 512], PS[0:64, g % 2, :])
                shifted = XSH[64:128, g * 512:(g + 1) * 512].rearrange("p (b t) -> p b t", b=8)
                src = PS[0:64, g % 2, :].rearrange("p (b t) -> p b t", b=8)
                nc.scalar.copy(shifted[:, :, 1:NT], src[:, :, 0:NT - 1]).then_inc(T["xtc"], 1)
            for j in range(NJ):
                s.wait_ge(T["kin"], j + 1)
                nc.scalar.activation(RR[:, j, :], PS[:, 2 + j % 4, 128:192], ACT.Exp, scale=-1.0).then_inc(T["rexp"], 1)
                s.wait_ge(T["rexp"], j + 1)
                nc.scalar.activation(KK[:, j, :], KK[:, j, :], ACT.Exp).then_inc(T["kexp"], 1)
            for g in range(NG):
                s.wait_ge(T["rt"], g + 1)
                nc.scalar.copy(RWT[:, g * 512:(g + 1) * 512], PS[0:64, 4 + g % 2, :]).then_inc(T["rtc"], 1)

        def a2_dve(v):
            T = att[2]
            v.wait_ge(s_late, 16 * n_late)
            dve_chain.link(v, nc.vector.tensor_scalar(w["mix"][:, :], w["mix"][:, :], w["mixab"][:, 0:1], w["mixab"][:, 1:2],
                                                      ALU.mult, ALU.add))
            for i in range(3):
                nc.vector.tensor_scalar(w["wkvr"][:, 64 * i:64 * i + 64], w["wkvr"][:, 64 * i:64 * i + 64],
                                        w["mix"][:, i:i + 1], None, ALU.mult).then_inc(T["coef"], 1)
            for g in range(NG):
                z = XSH[64:128, g * 512:(g + 1) * 512].rearrange("p (b t) -> p b t", b=8)[:, :, 0:1]
                nc.vector.memset(z, 0.0).then_inc(T["shift"], 1)
            for j in range(NJ + 1):
                if j < NJ:
                    v.wait_ge(T["s"], j + 1)
                    nc.vector.tensor_scalar(KK[:, j, :], PS[:, 2 + j % 4, 0:64], -60.0, 30.0, ALU.max, ALU.min).then_inc(T["kin"], 1)
                if j >= 1:
                    v.wait_ge(T["kexp"], j)
                    nc.vector.tensor_tensor(KV[:, j - 1, :], KK[:, j - 1, :], PS[:, 2 + (j - 1) % 4, 64:128], ALU.mult
                                            ).then_inc(T["kv"], 1)
            v.wait_ge(T["rexp"], NJ)
            moes[1].wait(v, "hcopy", NG)
            moes[2].wait(v, "lnb", 1)
            nc.vector.tensor_tensor(w["b1_2"][:, :], w["b1_2"][:, :], PS[:, 7, 0:16], ALU.add).then_inc(moes[2]["b1prep"], 1)
            for q in range(4):
                v.wait_ge(T["wkv"], q + 1)
                dve_chain.link(v, nc.vector.scalar_tensor_tensor(out=flat(DN, q), in0=flat(RR, q), scalar=1.0, in1=PS[:, 2 * (q % 2), :],
                                                                 op0=ALU.add, op1=ALU.mult))
                dve_chain.link(v, nc.vector.reciprocal(q3(DN, q), q3(DN, q)))
                nc.vector.tensor_tensor(q3(RR, q), q3(DN, q), bank3(2 * (q % 2) + 1), ALU.mult).then_inc(T["rw"], 1)
            for q in range(4):
                v.wait_ge(T["o"], q + 1)
                nc.vector.tensor_tensor(q3(H, q), q3(H, q), bank3(q), ALU.add).then_inc(T["oh"], 1)

        def flat(t, q):
            return q3(t, q).rearrange("p j e -> p (j e)")

        QS = BIG[:, 0:16384].rearrange("p (k n) -> p k n", k=4)
        OMS = WORK[:, 0:1024].rearrange("p (u n) -> p u n", u=2)
        RTT = WORK[:, 1024:2048].rearrange("p (u n) -> p u n", u=2)
        ZT = LNB[:, :, :].rearrange("p (u k j) e -> p u k (j e)", u=2, k=4)

        def a3_pe(pe):
            T = att[3]
            xt_pe(pe, T, moes[2], "na_out")
            for g in range(NG):
                pe.wait_ge(T["xtc"], g + 1)
                for k in range(4):
                    u = g * 4 + k
                    if u >= 2:
                        pe.wait_ge(T["qc"], u - 1)
                    nc.tensor.matmul(PS[:, 2 + u % 2, :], w["qh"][:, k * P:(k + 1) * P], XT[0:64, g * 512:(g + 1) * 512],
                                     start=True, stop=True).then_inc(T["q"], 1)
            pe.wait_ge(T["qc"], 4 * NG)
            for step in range(NJ + 4):
                j = step
                if j < NJ:
                    if j >= 2:
                        pe.wait_ge(T["omc"], j - 1)
                    for par in range(2):
                        for b in range(2):
                            c = j * P + b * 64
                            r = slice(64 * par, 64 * par + 64)
                            o = PS[64 * b:64 * b + 64, 2 * par + j % 2, 0:256].rearrange("p (k t) -> p k t", k=4)
                            ins = nc.tensor.matmul(o, XT[r, c:c + 64], QS[r, :, c:c + 64], start=True, stop=True)
                    ins.then_inc(T["om"], 1)
                j = step - 1
                if 0 <= j < NJ:
                    pe.wait_ge(T["omc"], j + 1)
                    if j >= 1:
                        pe.wait_ge(T["zc"], j)
                    for b in range(2):
                        for par in range(2):
                            r = slice(64 * b, 64 * b + 64)
                            ins = nc.tensor.matmul(PS[64 * par:64 * par + 64, 4 + b, 0:256], XA[r, j, :],
                                                   OMS[r, j % 2, par * 256:par * 256 + 256], start=True, stop=True)
                    ins.then_inc(T["z"], 1)
                j = step - 2
                if 0 <= j < NJ and j % 4 == 3:
                    g = j // 4
                    pe.wait_ge(T["zc"], j + 1)
                    if g >= 1:
                        pe.wait_ge(T["rc"], g)
                    for k in range(4):
                        h = k % 2
                        ins = nc.tensor.matmul(PS[64 * h:64 * h + 64, 6, :], w["eh"][:, k, :], ZT[:, g % 2, k, :], start=k < 2,
                                               stop=k >= 2, skip_group_check=True)
                    ins.then_inc(T["r"], 1)
                j = step - 3
                if 0 <= j < NJ and j % 4 == 3:
                    g = j // 4
                    pe.wait_ge(T["rc"], g + 1)
                    if g >= 1:
                        pe.wait_ge(T["oh"], g)
                    for i in range(4):
                        ins = nc.tensor.matmul(PS[:, 7, i * 64:i * 64 + 64], RTT[:, g % 2, i * P:(i + 1) * P], w["II"][:, :],
                                               start=True, stop=True)
                    ins.then_inc(T["rr"], 1)

        def a3_act(s):
            T = att[3]
            for g in range(NG):
                s.wait_ge(T["xt"], g + 1)
                nc.scalar.copy(XT[0:64, g * 512:(g + 1) * 512], PS[0:64, g % 2, :])
                nc.scalar.copy(XT[64:128, g * 512:(g + 1) * 512], PS[0:64, g % 2, :]).then_inc(T["xtc"], 1)
            for u in range(4 * NG):
                g, k = u // 4, u % 4
                s.wait_ge(T["q"], u + 1)
                nc.scalar.copy(QS[:, k, g * 512:(g + 1) * 512], PS[:, 2 + u % 2, :]).then_inc(T["qc"], 1)
            for j in range(NJ):
                s.wait_ge(T["z"], j + 1)
                g, i = j // 4, j % 4
                if g >= 2 and i == 0:
                    s.wait_ge(T["r"], g - 1)
                for b in range(2):
                    ins = nc.scalar.copy(ZT[:, g % 2, :, i * P + b * 64:i * P + b * 64 + 64],
                                         PS[:, 4 + b, 0:256].rearrange("p (k t) -> p k t", k=4))
                ins.then_inc(T["zc"], 1)

        def a3_dve(v):
            T = att[3]

            def tri_mask(j):
                v.wait_ge(T["om"], j + 1)
                if j == 0:
                    moes[2].wait(v, "hcopy", NG)
                if j >= 2:
                    v.wait_ge(T["z"], j - 1)
                tri = w["tri"][:, :].unsqueeze(1).broadcast_to([P, 4, 64])
                for par in range(2):
                    ins = nc.vector.tensor_tensor(OMS[:, j % 2, par * 256:par * 256 + 256].rearrange("p (k t) -> p k t", k=4),
                                                  PS[:, 2 * par + j % 2, 0:256].rearrange("p (k t) -> p k t", k=4), tri, ALU.mult)
                ins.then_inc(T["omc"], 1)

            for step in range(NJ + 5):
                if step < NJ:
                    tri_mask(step)
                j = step - 2
                if 0 <= j < NJ and j % 4 == 3:
                    g = j // 4
                    v.wait_ge(T["r"], g + 1)
                    if g >= 2:
                        v.wait_ge(T["rr"], g - 1)
                    nc.vector.tensor_copy(RTT[:, g % 2, :], PS[:, 6, :]).then_inc(T["rc"], 1)
                j = step - 4
                if 0 <= j < NJ and j % 4 == 3:
                    g = j // 4
                    v.wait_ge(T["rr"], g + 1)
                    hg = H[:, 4 * g:4 * g + 4, :]
                    nc.vector.tensor_tensor(hg, hg, PS[:, 7, 0:256].rearrange("p (j e) -> p j e", j=4), ALU.add
                                            ).then_inc(T["oh"], 1)

        block = ctx.enter_context(nc.Block())

        @block.sync
        def _(sp):
            tok_sp(sp)
            a0_sp(sp)
            for i in (1, 2, 3):
                moes[i - 1].wait(sp, "wprep", 1)
                cols = moes[i].nch * P
                sp.dma_start(W1S[:, 0:cols], a[f"w1_{i}"]).then_inc(s_w1[i], 16)
            dst = out.rearrange("(j b) t e -> b t j e", b=2)
            moes[3].wait(sp, "added", NG)
            for b in range(2):
                sp.dma_start(dst[b], H[64 * b:64 * b + 64, :, :]).then_inc(s_out, 16)
            sp.wait_ge(s_out, 32)

        @block.scalar
        def _(s):
            for name in maps:
                s.dma_start(w[name][:], a[name]).then_inc(s_maps, 16)
            for name in early:
                s.dma_start(w[name][:], a[name]).then_inc(s_early, 16)
            tok_act(s)
            s.wait_ge(s_early, 16 * n_early)
            ln_act(s, 0)
            a0_act(s)
            h1_load(s, 1)
            ln_act(s, 1, split_high(s, moes[0]))
            moe_act(s, moes[0])
            a1_act(s)
            s.wait_ge(s_late, 16 * n_late)
            ln_act(s, 2, split_high(s, moes[1]))
            moe_act(s, moes[1])
            a2_act(s)
            ln_act(s, 3)
            router_copies(s, moes[2])
            ln_act(s, 4, split_high(s, moes[2]))
            moe_act(s, moes[2])
            a3_act(s)
            ln_act(s, 5, split_high(s, moes[3]))
            moe_act(s, moes[3])

        @block.gpsimd
        def _(p):
            late = [k for k in w if k not in early + maps]
            for name in late:
                p.dma_start(w[name][:], a[name]).then_inc(s_late, 16)
            p.dma_start(W1S[:, 0:moes[0].nch * P], a["w1_0"]).then_inc(s_w1[0], 16)
            pool_chain.link(p, nc.gpsimd.memset(HALFPOW[:, :], -0.5))
            ln_pool(p, 0)
            a0_pool(p)
            ln_pool(p, 1)
            moe_main_pool(p, moes[0])
            moe_weights(p, moes[1])
            ln_pool(p, 2)
            moe_main_pool(p, moes[1])
            moe_weights(p, moes[2])
            ln_pool(p, 3)
            ln_pool(p, 4)
            moe_main_pool(p, moes[2])
            moe_weights(p, moes[3])
            ln_pool(p, 5)
            moe_main_pool(p, moes[3])

        @block.vector
        def _(v):
            tok_dve(v)
            ln_dve(v, 0, H, XA, lambda q: v.wait_ge(s_h0, q + 1))
            a0_dve(v)
            ln_dve(v, 1, H, XA, lambda q: v.wait_ge(s_h1ld[q // 2], 32), split_low(v, moes[0]))
            moe_dve(v, moes[0])
            a1_dve(v)
            ln_dve(v, 2, H, XA, lambda q: v.wait_ge(att[1]["oh"], q + 1), split_low(v, moes[1]))
            moe_dve(v, moes[1])
            a2_dve(v)
            ln_dve(v, 3, H, XA, lambda q: v.wait_ge(att[2]["oh"], q + 1))
            ln_dve(v, 4, XA, XC, lambda q: ln_wait(v, 3, "out", q + 1), split_low(v, moes[2]))
            moe_dve(v, moes[2])
            a3_dve(v)
            ln_dve(v, 5, H, XA, lambda q: v.wait_ge(att[3]["oh"], NG), split_low(v, moes[3]))
            moe_dve(v, moes[3])

        @block.tensor
        def _(pe):
            tok_pe(pe)
            a0_pe(pe)
            moe_pe(pe, moes[0])
            a1_pe(pe)
            moe_pe(pe, moes[1])
            a2_pe(pe)
            moe_pe(pe, moes[2])
            a3_pe(pe)
            moe_pe(pe, moes[3])


def resize_matrix(n, m=8):
    scale = n / m
    centre = (np.arange(m) + 0.5) * scale - 0.5
    t = np.maximum(0, 1 - np.abs(centre[:, None] - np.arange(n)[None]) / scale)
    return t / t.sum(1, keepdims=True)


def haar(n):
    lo, hi = np.zeros((n // 2, n)), np.zeros((n // 2, n))
    i = np.arange(n // 2)
    c = 0.7071067811865476
    lo[i, 2 * i] = lo[i, 2 * i + 1] = hi[i, 2 * i] = c
    hi[i, 2 * i + 1] = -c
    return lo, hi


def constants():
    lo1, hi1 = haar(224)
    lo2, hi2 = haar(112)
    r56, r112 = resize_matrix(56), resize_matrix(112)
    maps = np.concatenate([r56 @ lo2 @ lo1, r56 @ hi2 @ lo1, r112 @ lo1, r112 @ hi1])
    k = {}
    k["rowmap"] = maps.T.reshape(112, 2, 32)
    k["colmap"] = maps.T.reshape(2, 112, 32).transpose(1, 0, 2)
    eye, up = np.eye(128), np.triu(np.ones((64, 64)))
    k["I"] = eye
    k["IU"] = np.tile(np.concatenate([np.eye(64), up], 1), (2, 1))
    k["II"] = np.tile(np.eye(64), (2, 1))
    k["pool2"] = np.kron(np.eye(2), np.ones((64, 1))) / NT
    k["ones64"] = np.ones((64, 64))
    k["prio"] = np.tile(np.arange(16, 0, -1.0), (128, 1))
    k["cum"] = np.kron(np.eye(2), up)
    k["tri"] = np.tile(up, (2, 1))
    k["mixab"] = np.concatenate([np.tile([[1.0, 0.0]], (64, 1)), np.tile([[-1.0, 1.0]], (64, 1))])
    return {n: np.ascontiguousarray(v, np.float32) for n, v in k.items()}


def selectors(chunk_expert, ne):
    s = np.zeros((3 * ne, len(chunk_expert), 128), np.float32)
    for c, es in enumerate(chunk_expert):
        for half, e in enumerate(es):
            for part in range(3):
                s[part * ne + e, c, 64 * half:64 * half + 64] = 1
    return s.reshape(3 * ne, -1)


def bf16_bits(zeros_and_ones):
    return (zeros_and_ones != 0).astype(np.uint16) * np.uint16(0x3F80)


def laid_out(i):
    f = {k: np.asarray(v) for k, v in i.items()}
    a = {"x": f["x"]}
    a.update(constants())
    a["Ib"] = bf16_bits(np.eye(128))
    rep = lambda v, n=128: np.tile(v.reshape(1, -1), (n, 1))
    ops = [(0, 0), (1, 0), (0, 1), (1, 1), (3, 2), (2, 3), (3, 3)]
    tw = np.zeros((4, 8, 4, 8, 64), np.float32)
    for m, (ro, co) in enumerate(ops):
        for s in range(8):
            tw[co, s, ro, s, :] = f["L0_tok_W"][m]
    a["tokW"] = tw.reshape(32, 4, 512)
    a["tokb"] = rep(f["L0_tok_b"])
    bd = np.zeros((128, 3, 128), np.float32)
    for n, name in enumerate(("L0_attn_w1", "L0_attn_w2", "L0_attn_w3")):
        bd[:64, n, :64] = bd[64:, n, 64:] = f[name].T
    a["bd"] = bd
    a["b3"] = np.tile(f["L0_attn_b3"].reshape(-1, 1), (2, 1))
    w0 = np.zeros((128, 16, 32), np.float32)
    for k in range(16):
        w0[:64, k, 2 * k] = w0[64:, k, 2 * k + 1] = f["L0_attn_w0"]
    a["w0"] = w0
    dup = lambda v: np.concatenate([v, v], 0)

    def moe(n, w1, b1, w2, b2, rw, rb, chunk_expert):
        ne = w1.shape[0]
        nch = len(chunk_expert)
        a[f"w1_{n}"] = dup(w1.transpose(1, 0, 2).reshape(64, -1))
        a[f"b1_{n}"] = b1.reshape(nch, 128).T
        a[f"w2_{n}"] = w2.reshape(nch, 128, 64).transpose(1, 0, 2)
        a[f"b2_{n}"] = np.tile(b2, (3, 1))
        a[f"rw_{n}"] = dup(rw)
        a[f"rb_{n}"] = rep(rb)
        a[f"sel_{n}"] = bf16_bits(selectors(chunk_expert, ne))

    moe(0, f["L0_ffn_W1"], f["L0_ffn_b1"], f["L0_ffn_W2"], f["L0_ffn_b2"], f["L0_ffn_Wr"], f["L0_ffn_br"],
        [(e, e) for e in range(8)])
    moe(1, f["L1_ffn_w1"], f["L1_ffn_b1"], f["L1_ffn_w2"], f["L1_ffn_b2"], f["L1_ffn_router_w"].T, np.zeros(8, np.float32),
        [(2 * c, 2 * c + 1) for c in range(4)])
    moe(2, f["L2_ffn_W1"], f["L2_ffn_b1"], f["L2_ffn_W2"], f["L2_ffn_b2"], f["L2_ffn_Wr"], f["L2_ffn_br"],
        [(c // 2, c // 2) for c in range(16)])
    moe(3, f["L3_ffn_w1"], f["L3_ffn_b1"], f["L3_ffn_w2"], f["L3_ffn_b2"], f["L3_ffn_gate_w"], f["L3_ffn_gate_b"],
        [(c, c) for c in range(16)])
    a["lng"] = dup(f["L2_ffn_ln_g"].T)
    a["lnb"] = f["L2_ffn_ln_b"].T
    for n, l in ((0, "L0"), (3, "L3")):
        a[f"gamma_{n}"] = rep(f[l + "_ffn_gamma"])
        a[f"beta_{n}"] = rep(f[l + "_ffn_beta"])
    a["wqT"], a["wkT"], a["wv"] = f["L1_attn_Wq"].T, f["L1_attn_Wk"].T, f["L1_attn_Wv"]
    a["wkvr"] = dup(np.concatenate([f["L2_attn_Wk"], f["L2_attn_Wv"], f["L2_attn_Wr"]], 1))
    a["mix"] = dup(np.stack([f["L2_attn_time_mix_" + c].reshape(64) for c in "kvr"], 1))
    a["wo"] = f["L2_attn_Wo"]
    tw = f["L2_attn_time_w"]
    toep = np.zeros((128, 128), np.float32)
    for u in range(64):
        for t in range(u, 64):
            toep[u, t] = toep[64 + u, 64 + t] = tw[tw.shape[0] - 1 - (t - u)]
    a["toep"] = toep
    a["qh"] = f["L3_attn_Q"].transpose(1, 0, 2).reshape(64, 512)
    a["eh"] = f["L3_attn_E"].transpose(0, 2, 1).reshape(4, 128, 64).transpose(1, 0, 2)
    return {n: np.ascontiguousarray(v) for n, v in a.items()}


def kernel(**inputs):
    import concourse.bacc as _bacc
    from concourse.bass_utils import run_bass_kernel_spmd as _run

    nc = _bacc.Bacc("TRN2", target_bir_lowering=False, num_devices=1)
    arrays, aps = {}, {}
    for name, v in laid_out(inputs).items():
        arrays["in_" + name] = v
        aps[name] = nc.dram_tensor("in_" + name, v.shape, mybir.dt.from_np(v.dtype), kind="ExternalInput").ap()
    out = nc.dram_tensor("out_0", (NI, NT, D), F32, kind="ExternalOutput").ap()
    build(nc, aps, out)
    r = _run(nc, [arrays], core_ids=[0])
    return r.results[0]["out_0"]
```
